# Optimizing a Trainium2 kernel written in Bass

```python
import numpy as np
import jax
import jax.numpy as jnp

def _softmax(x, axis=-1):
    return jax.nn.softmax(x, axis=axis)

def _gelu(x):
    return jax.nn.gelu(x, approximate=True)

def _silu(x):
    return jax.nn.silu(x)

def _sigmoid(x):
    return jax.nn.sigmoid(x)

def _layernorm(x, axis=-1, eps=1e-05):
    m = jnp.mean(x, axis=axis, keepdims=True)
    v = jnp.var(x, axis=axis, keepdims=True)
    return (x - m) / jnp.sqrt(v + eps)

def _scatter_add(tgt, idx, src, axis=0):
    return tgt.at[idx].add(src)

def _segment_sum(src, seg, n):
    return jax.ops.segment_sum(src, seg, n)
kernel_name = 'mk_hybrid_d2_jaxref_r8_1127d9'

def setup_inputs(seed: int=0):
    np.random.seed(seed)
    _w = jnp.asarray

    def _L0_attn_a_setup():
        import math
        import jax, jax.numpy as jnp
        import numpy as np
        B, S, D, H, DH = (2, 256, 256, 16, 128)

        def _alibi_slopes(n):

            def pow2(m):
                start = 2 ** (-2 ** (-(math.log2(m) - 3)))
                return [start * start ** i for i in range(m)]
            if math.log2(n).is_integer():
                return pow2(n)
            c = 2 ** math.floor(math.log2(n))
            return pow2(c) + _alibi_slopes(2 * c)[0::2][:n - c]

        def _alibi_mask(n_heads, q_len, kv_len):
            slopes = jnp.asarray(np.array(_alibi_slopes(n_heads), dtype=np.float32))
            bias = slopes[:, None, None] * jnp.arange(kv_len, dtype=jnp.float32)[None, None, :]
            i = jnp.arange(q_len)[:, None]
            j = jnp.arange(kv_len)[None, :]
            causal = jnp.where(j > i, -jnp.inf, 0.0).astype(jnp.float32)
            return causal[None, :, :] + bias
        key = jax.random.key(seed)
        k1, k2, k3, k4, k5 = jax.random.split(key, 5)
        scale = 1.0 / math.sqrt(D)
        return {'resid_pre': jax.random.normal(k1, (B, S, D), dtype=jnp.float32), 'Wq': jax.random.normal(k2, (H * DH, D), dtype=jnp.float32) * scale, 'Wk': jax.random.normal(k3, (H * DH, D), dtype=jnp.float32) * scale, 'Wv': jax.random.normal(k4, (H * DH, D), dtype=jnp.float32) * scale, 'Wo': jax.random.normal(k5, (D, H * DH), dtype=jnp.float32) * scale}
    _L0_attn_a_in = _L0_attn_a_setup()

    def _L0_attn_b_setup():
        import jax, jax.numpy as jnp
        import numpy as np
        from jax import lax
        B, T, D = (2, 256, 256)
        H = 8
        DK = D // H
        DV = D // H
        CONV_K = 4
        CHUNK = 64
        EPS = 1e-05
        INTER = 352

        def rmsnorm(x, w, eps=EPS):
            return x * lax.rsqrt(jnp.mean(x * x, axis=-1, keepdims=True) + eps) * w

        def short_conv_silu(x, w):
            K = w.shape[-1]
            xp = jnp.pad(x, ((0, 0), (K - 1, 0), (0, 0)))
            y = sum((xp[:, i:i + x.shape[1], :] * w[None, None, :, i] for i in range(K)))
            return jax.nn.silu(y)

        def rope(x, cos, sin):
            x1, x2 = jnp.split(x, 2, axis=-1)
            c = cos[None, :, None, :]
            s = sin[None, :, None, :]
            return jnp.concatenate([x1 * c - x2 * s, x2 * c + x1 * s], axis=-1)

        def chunk_retention(q, k, v, gamma, C=CHUNK):
            b, t, h, dk = q.shape
            dv = v.shape[-1]
            q = q * dk ** (-0.5)
            n = t // C
            to_chunks = lambda x: x.reshape(b, n, C, h, -1).transpose(1, 0, 3, 2, 4)
            qc, kc, vc = map(to_chunks, (q, k, v))
            i = jnp.arange(C)
            diff = i[:, None] - i[None, :]
            pe = jnp.where(diff >= 0, diff, 0).astype(q.dtype)
            Dm = jnp.where(diff >= 0, gamma[:, None, None] ** pe, 0.0)
            di = gamma[:, None] ** (i + 1).astype(q.dtype)
            dkc = gamma[:, None] ** (C - 1 - i).astype(q.dtype)
            gC = gamma ** C

            def step(S, xs):
                qi, ki, vi = xs
                A = jnp.einsum('bhid,bhjd->bhij', qi, ki) * Dm
                o = A @ vi + jnp.einsum('bhid,bhde->bhie', qi, S) * di[None, :, :, None]
                S = S * gC[None, :, None, None] + jnp.einsum('bhjd,bhje->bhde', ki * dkc[None, :, :, None], vi)
                return (S, o)
            S0 = jnp.zeros((b, h, dk, dv), q.dtype)
            _, oc = lax.scan(step, S0, (qc, kc, vc))
            return oc.transpose(1, 0, 3, 2, 4).reshape(b, t, h, dv)
        key = jax.random.key(seed)
        ks = jax.random.split(key, 14)
        s = 0.02
        return {'hidden_states': jax.random.normal(ks[0], (B, T, D), jnp.float32), 'attn_norm_w': jnp.ones((D,), jnp.float32), 'Wq': jax.random.normal(ks[1], (D, D), jnp.float32) * s, 'Wk': jax.random.normal(ks[2], (D, D), jnp.float32) * s, 'Wv': jax.random.normal(ks[3], (D, D), jnp.float32) * s, 'Wg': jax.random.normal(ks[4], (D, D), jnp.float32) * s, 'Wo': jax.random.normal(ks[5], (D, D), jnp.float32) * s, 'conv_wq': jax.random.normal(ks[6], (D, CONV_K), jnp.float32) * 0.3, 'conv_wk': jax.random.normal(ks[7], (D, CONV_K), jnp.float32) * 0.3, 'conv_wv': jax.random.normal(ks[8], (D, CONV_K), jnp.float32) * 0.3, 'gnorm_w': jnp.ones((DV,), jnp.float32), 'mlp_norm_w': jnp.ones((D,), jnp.float32), 'W_gate': jax.random.normal(ks[9], (D, 2 * INTER), jnp.float32) * s, 'W_down': jax.random.normal(ks[10], (INTER, D), jnp.float32) * s}
    _L0_attn_b_in = _L0_attn_b_setup()

    def _L0_ffn_setup():
        import jax, jax.numpy as jnp
        import numpy as np
        B, S, H = (2, 256, 256)
        E, K = (16, 4)
        I_MOE, I_SH = (176, 704)
        key = jax.random.key(seed)
        ks = jax.random.split(key, 9)

        def w(k, shape, fan_in):
            return jax.random.normal(k, shape, jnp.float32) * fan_in ** (-0.5)
        return {'hidden_states': jax.random.normal(ks[0], (B, S, H), jnp.float32), 'router_w': w(ks[1], (E, H), H), 'w_gate': w(ks[2], (E, H, I_MOE), H), 'w_up': w(ks[3], (E, H, I_MOE), H), 'w_down': w(ks[4], (E, I_MOE, H), I_MOE), 'sh_gate': w(ks[5], (H, I_SH), H), 'sh_up': w(ks[6], (H, I_SH), H), 'sh_down': w(ks[7], (I_SH, H), I_SH), 'sh_gate_w': w(ks[8], (H, 1), H)}
    _L0_ffn_in = _L0_ffn_setup()

    def _L1_attn_a_setup():
        import jax, jax.numpy as jnp
        import numpy as np
        H = 16
        DK = 128
        DV = 128
        M = 64
        EPS = 1e-05
        CLAMP = 32.0
        ROPE_BASE = 10000.0

        def _rope(x, cos, sin):
            x1, x2 = jnp.split(x, 2, axis=-1)
            return jnp.concatenate([x1 * cos - x2 * sin, x2 * cos + x1 * sin], axis=-1)
        key = jax.random.key(seed)
        ks = jax.random.split(key, 9)
        B, T, D = (1, 256, 256)
        sc = 0.02
        return {'hidden_states': jax.random.normal(ks[0], (B, T, D), jnp.float32), 'Wq': jax.random.normal(ks[1], (H * DK, D), jnp.float32) * sc, 'Wk': jax.random.normal(ks[2], (H * DK, D), jnp.float32) * sc, 'Wv': jax.random.normal(ks[3], (H * DV, D), jnp.float32) * sc, 'Wg': jax.random.normal(ks[4], (H * DV, D), jnp.float32) * sc, 'Wo': jax.random.normal(ks[5], (D, H * DV), jnp.float32) * sc, 'Ws1': jax.random.normal(ks[6], (16, D), jnp.float32) * sc, 'Ws2': jax.random.normal(ks[7], (H * M, 16), jnp.float32) * sc, 'bs2': jnp.zeros((H * M,), jnp.float32), 'g_norm_weight': jnp.ones((DV,), jnp.float32)}
    _L1_attn_a_in = _L1_attn_a_setup()

    def _L1_attn_b_setup():
        import jax, jax.numpy as jnp
        import numpy as np
        B_SZ, L, D, N, R = (2, 256, 256, 128, 128)
        key = jax.random.key(seed)
        ks = jax.random.split(key, 8)
        s = lambda k, shape: jax.random.normal(k, shape, jnp.float32) * 0.02
        return {'x': jax.random.normal(ks[0], (B_SZ, L, D), jnp.float32), 'norm_w': jnp.ones((D,), jnp.float32), 'select_proj_w': s(ks[1], (D, D)), 'select_proj_b': jnp.zeros((D,), jnp.float32), 'select_gate': jnp.ones((D,), jnp.float32), 'x_proj_w': s(ks[2], (R + 2 * N, D)), 'dt_proj_w': s(ks[3], (D, R)), 'dt_proj_b': jnp.zeros((D,), jnp.float32), 'A_log': s(ks[4], (D, N)), 'D_param': jnp.ones((D,), jnp.float32), 'out_proj_w': s(ks[5], (D, D))}
    _L1_attn_b_in = _L1_attn_b_setup()

    def _L1_ffn_setup():
        import jax, jax.numpy as jnp
        import numpy as np
        DIM = 256
        E = 8
        TOPK = 2
        H = 176
        HS = H * 2
        TEMP = 1.0
        key = jax.random.key(seed)
        ks = jax.random.split(key, 8)
        s = 0.02
        return {'x': jax.random.normal(ks[0], (2, 128, DIM), dtype=jnp.float32), 'gate_w': jax.random.normal(ks[1], (E, DIM), dtype=jnp.float32) * (1.0 / np.sqrt(DIM)), 'w1': jax.random.normal(ks[2], (E, H, DIM), dtype=jnp.float32) * s, 'w2': jax.random.normal(ks[3], (E, DIM, H), dtype=jnp.float32) * s, 'w3': jax.random.normal(ks[4], (E, H, DIM), dtype=jnp.float32) * s, 'sw1': jax.random.normal(ks[5], (HS, DIM), dtype=jnp.float32) * s, 'sw2': jax.random.normal(ks[6], (DIM, HS), dtype=jnp.float32) * s, 'sw3': jax.random.normal(ks[7], (HS, DIM), dtype=jnp.float32) * s}
    _L1_ffn_in = _L1_ffn_setup()
    _d = {'L0_attn_a_resid_pre': _L0_attn_a_in['resid_pre'], 'L0_attn_a_Wq': _L0_attn_a_in['Wq'], 'L0_attn_a_Wk': _L0_attn_a_in['Wk'], 'L0_attn_a_Wv': _L0_attn_a_in['Wv'], 'L0_attn_a_Wo': _L0_attn_a_in['Wo'], 'L0_attn_b_attn_norm_w': _L0_attn_b_in['attn_norm_w'], 'L0_attn_b_Wq': _L0_attn_b_in['Wq'], 'L0_attn_b_Wk': _L0_attn_b_in['Wk'], 'L0_attn_b_Wv': _L0_attn_b_in['Wv'], 'L0_attn_b_Wg': _L0_attn_b_in['Wg'], 'L0_attn_b_Wo': _L0_attn_b_in['Wo'], 'L0_attn_b_conv_wq': _L0_attn_b_in['conv_wq'], 'L0_attn_b_conv_wk': _L0_attn_b_in['conv_wk'], 'L0_attn_b_conv_wv': _L0_attn_b_in['conv_wv'], 'L0_attn_b_gnorm_w': _L0_attn_b_in['gnorm_w'], 'L0_attn_b_mlp_norm_w': _L0_attn_b_in['mlp_norm_w'], 'L0_attn_b_W_gate': _L0_attn_b_in['W_gate'], 'L0_attn_b_W_down': _L0_attn_b_in['W_down'], 'L0_ffn_router_w': _L0_ffn_in['router_w'], 'L0_ffn_w_gate': _L0_ffn_in['w_gate'], 'L0_ffn_w_up': _L0_ffn_in['w_up'], 'L0_ffn_w_down': _L0_ffn_in['w_down'], 'L0_ffn_sh_gate': _L0_ffn_in['sh_gate'], 'L0_ffn_sh_up': _L0_ffn_in['sh_up'], 'L0_ffn_sh_down': _L0_ffn_in['sh_down'], 'L0_ffn_sh_gate_w': _L0_ffn_in['sh_gate_w'], 'L1_attn_a_Wq': _L1_attn_a_in['Wq'], 'L1_attn_a_Wk': _L1_attn_a_in['Wk'], 'L1_attn_a_Wv': _L1_attn_a_in['Wv'], 'L1_attn_a_Wg': _L1_attn_a_in['Wg'], 'L1_attn_a_Wo': _L1_attn_a_in['Wo'], 'L1_attn_a_Ws1': _L1_attn_a_in['Ws1'], 'L1_attn_a_Ws2': _L1_attn_a_in['Ws2'], 'L1_attn_a_bs2': _L1_attn_a_in['bs2'], 'L1_attn_a_g_norm_weight': _L1_attn_a_in['g_norm_weight'], 'L1_attn_b_norm_w': _L1_attn_b_in['norm_w'], 'L1_attn_b_select_proj_w': _L1_attn_b_in['select_proj_w'], 'L1_attn_b_select_proj_b': _L1_attn_b_in['select_proj_b'], 'L1_attn_b_select_gate': _L1_attn_b_in['select_gate'], 'L1_attn_b_x_proj_w': _L1_attn_b_in['x_proj_w'], 'L1_attn_b_dt_proj_w': _L1_attn_b_in['dt_proj_w'], 'L1_attn_b_dt_proj_b': _L1_attn_b_in['dt_proj_b'], 'L1_attn_b_A_log': _L1_attn_b_in['A_log'], 'L1_attn_b_D_param': _L1_attn_b_in['D_param'], 'L1_attn_b_out_proj_w': _L1_attn_b_in['out_proj_w'], 'L1_ffn_gate_w': _L1_ffn_in['gate_w'], 'L1_ffn_w1': _L1_ffn_in['w1'], 'L1_ffn_w2': _L1_ffn_in['w2'], 'L1_ffn_w3': _L1_ffn_in['w3'], 'L1_ffn_sw1': _L1_ffn_in['sw1'], 'L1_ffn_sw2': _L1_ffn_in['sw2'], 'L1_ffn_sw3': _L1_ffn_in['sw3']}
    _x0 = _d['L0_attn_a_resid_pre']
    _d['L0_attn_a_resid_pre'] = jax.random.normal(jax.random.fold_in(jax.random.key(seed), 1), (8, 256, 256), dtype=_x0.dtype)
    del _x0
    return _d

def reference(L0_attn_a_resid_pre, L0_attn_a_Wq, L0_attn_a_Wk, L0_attn_a_Wv, L0_attn_a_Wo, L0_attn_b_attn_norm_w, L0_attn_b_Wq, L0_attn_b_Wk, L0_attn_b_Wv, L0_attn_b_Wg, L0_attn_b_Wo, L0_attn_b_conv_wq, L0_attn_b_conv_wk, L0_attn_b_conv_wv, L0_attn_b_gnorm_w, L0_attn_b_mlp_norm_w, L0_attn_b_W_gate, L0_attn_b_W_down, L0_ffn_router_w, L0_ffn_w_gate, L0_ffn_w_up, L0_ffn_w_down, L0_ffn_sh_gate, L0_ffn_sh_up, L0_ffn_sh_down, L0_ffn_sh_gate_w, L1_attn_a_Wq, L1_attn_a_Wk, L1_attn_a_Wv, L1_attn_a_Wg, L1_attn_a_Wo, L1_attn_a_Ws1, L1_attn_a_Ws2, L1_attn_a_bs2, L1_attn_a_g_norm_weight, L1_attn_b_norm_w, L1_attn_b_select_proj_w, L1_attn_b_select_proj_b, L1_attn_b_select_gate, L1_attn_b_x_proj_w, L1_attn_b_dt_proj_w, L1_attn_b_dt_proj_b, L1_attn_b_A_log, L1_attn_b_D_param, L1_attn_b_out_proj_w, L1_ffn_gate_w, L1_ffn_w1, L1_ffn_w2, L1_ffn_w3, L1_ffn_sw1, L1_ffn_sw2, L1_ffn_sw3):

    def _L0_attn_a_ref(resid_pre, Wq, Wk, Wv, Wo):
        import math
        import jax, jax.numpy as jnp
        import numpy as np
        B, S, D, H, DH = (2, 256, 256, 16, 128)

        def _alibi_slopes(n):

            def pow2(m):
                start = 2 ** (-2 ** (-(math.log2(m) - 3)))
                return [start * start ** i for i in range(m)]
            if math.log2(n).is_integer():
                return pow2(n)
            c = 2 ** math.floor(math.log2(n))
            return pow2(c) + _alibi_slopes(2 * c)[0::2][:n - c]

        def _alibi_mask(n_heads, q_len, kv_len):
            slopes = jnp.asarray(np.array(_alibi_slopes(n_heads), dtype=np.float32))
            bias = slopes[:, None, None] * jnp.arange(kv_len, dtype=jnp.float32)[None, None, :]
            i = jnp.arange(q_len)[:, None]
            j = jnp.arange(kv_len)[None, :]
            causal = jnp.where(j > i, -jnp.inf, 0.0).astype(jnp.float32)
            return causal[None, :, :] + bias
        b, s, d = resid_pre.shape
        q = (resid_pre @ Wq.T).reshape(b, s, H, DH)
        k = (resid_pre @ Wk.T).reshape(b, s, H, DH)
        v = (resid_pre @ Wv.T).reshape(b, s, H, DH)
        scores = jnp.einsum('bqhd,bkhd->bhqk', q, k) / math.sqrt(DH)
        scores = jnp.clip(scores, -1024.0, 1024.0)
        scores = scores + _alibi_mask(H, s, s)[None]
        attn = jax.nn.softmax(scores.astype(jnp.float32), axis=-1).astype(q.dtype)
        z = jnp.einsum('bhqk,bkhd->bqhd', attn, v)
        out = jnp.einsum('bqhd,ohd->bqo', z, Wo.reshape(d, H, DH))
        return out

    def _L0_attn_b_ref(hidden_states, attn_norm_w, Wq, Wk, Wv, Wg, Wo, conv_wq, conv_wk, conv_wv, gnorm_w, mlp_norm_w, W_gate, W_down):
        import jax, jax.numpy as jnp
        import numpy as np
        from jax import lax
        B, T, D = (2, 256, 256)
        H = 8
        DK = D // H
        DV = D // H
        CONV_K = 4
        CHUNK = 64
        EPS = 1e-05
        INTER = 352

        def rmsnorm(x, w, eps=EPS):
            return x * lax.rsqrt(jnp.mean(x * x, axis=-1, keepdims=True) + eps) * w

        def short_conv_silu(x, w):
            K = w.shape[-1]
            xp = jnp.pad(x, ((0, 0), (K - 1, 0), (0, 0)))
            y = sum((xp[:, i:i + x.shape[1], :] * w[None, None, :, i] for i in range(K)))
            return jax.nn.silu(y)

        def rope(x, cos, sin):
            x1, x2 = jnp.split(x, 2, axis=-1)
            c = cos[None, :, None, :]
            s = sin[None, :, None, :]
            return jnp.concatenate([x1 * c - x2 * s, x2 * c + x1 * s], axis=-1)

        def chunk_retention(q, k, v, gamma, C=CHUNK):
            b, t, h, dk = q.shape
            dv = v.shape[-1]
            q = q * dk ** (-0.5)
            n = t // C
            to_chunks = lambda x: x.reshape(b, n, C, h, -1).transpose(1, 0, 3, 2, 4)
            qc, kc, vc = map(to_chunks, (q, k, v))
            i = jnp.arange(C)
            diff = i[:, None] - i[None, :]
            pe = jnp.where(diff >= 0, diff, 0).astype(q.dtype)
            Dm = jnp.where(diff >= 0, gamma[:, None, None] ** pe, 0.0)
            di = gamma[:, None] ** (i + 1).astype(q.dtype)
            dkc = gamma[:, None] ** (C - 1 - i).astype(q.dtype)
            gC = gamma ** C

            def step(S, xs):
                qi, ki, vi = xs
                A = jnp.einsum('bhid,bhjd->bhij', qi, ki) * Dm
                o = A @ vi + jnp.einsum('bhid,bhde->bhie', qi, S) * di[None, :, :, None]
                S = S * gC[None, :, None, None] + jnp.einsum('bhjd,bhje->bhde', ki * dkc[None, :, :, None], vi)
                return (S, o)
            S0 = jnp.zeros((b, h, dk, dv), q.dtype)
            _, oc = lax.scan(step, S0, (qc, kc, vc))
            return oc.transpose(1, 0, 3, 2, 4).reshape(b, t, h, dv)
        b, t, d = hidden_states.shape
        x = rmsnorm(hidden_states, attn_norm_w)
        q = short_conv_silu(x @ Wq, conv_wq)
        k = short_conv_silu(x @ Wk, conv_wk)
        v = short_conv_silu(x @ Wv, conv_wv)
        q = q.reshape(b, t, H, DK)
        k = k.reshape(b, t, H, DK)
        v = v.reshape(b, t, H, DV)
        inv_freq = 1.0 / 10000.0 ** (jnp.arange(0, DK, 2, dtype=jnp.float32) / DK)
        freqs = jnp.arange(t, dtype=jnp.float32)[:, None] * inv_freq[None, :]
        cos, sin = (jnp.cos(freqs), jnp.sin(freqs))
        q, k = (rope(q, cos, sin), rope(k, cos, sin))
        gamma = 1.0 - jnp.exp2(-5.0 - jnp.arange(H, dtype=jnp.float32))
        o = chunk_retention(q, k, v, gamma)
        g = (x @ Wg).reshape(b, t, H, DV)
        o = rmsnorm(o, gnorm_w) * (g * jax.nn.sigmoid(g))
        o = o.reshape(b, t, d) @ Wo
        h = hidden_states + o
        y = rmsnorm(h, mlp_norm_w)
        gy = y @ W_gate
        gate, yv = jnp.split(gy, 2, axis=-1)
        y = gate * jax.nn.sigmoid(gate) * yv @ W_down
        return h + y

    def _L0_ffn_ref(hidden_states, router_w, w_gate, w_up, w_down, sh_gate, sh_up, sh_down, sh_gate_w):
        import jax, jax.numpy as jnp
        import numpy as np
        B, S, H = (2, 256, 256)
        E, K = (16, 4)
        I_MOE, I_SH = (176, 704)
        orig = hidden_states.shape
        h = hidden_states.reshape(-1, orig[-1])
        N = h.shape[0]
        logits = h @ router_w.T
        probs = jax.nn.softmax(logits.astype(jnp.float32), axis=-1)
        top_vals, top_idx = jax.lax.top_k(probs, K)
        top_vals = top_vals / jnp.maximum(top_vals.sum(-1, keepdims=True), 1e-09)
        top_vals = top_vals.astype(h.dtype)
        comb = jnp.zeros((N, E), h.dtype).at[jnp.arange(N)[:, None], top_idx].add(top_vals)
        g = jnp.einsum('nh,ehi->eni', h, w_gate)
        u = jnp.einsum('nh,ehi->eni', h, w_up)
        y = jnp.einsum('eni,eih->enh', jax.nn.silu(g) * u, w_down)
        routed = jnp.einsum('enh,ne->nh', y, comb)
        shared = jax.nn.silu(h @ sh_gate) * (h @ sh_up) @ sh_down
        sg = jax.nn.sigmoid(h @ sh_gate_w)
        return (routed + sg * shared).reshape(orig)

    def _L1_attn_a_ref(hidden_states, Wq, Wk, Wv, Wg, Wo, Ws1, Ws2, bs2, g_norm_weight):
        import jax, jax.numpy as jnp
        import numpy as np
        H = 16
        DK = 128
        DV = 128
        M = 64
        EPS = 1e-05
        CLAMP = 32.0
        ROPE_BASE = 10000.0

        def _rope(x, cos, sin):
            x1, x2 = jnp.split(x, 2, axis=-1)
            return jnp.concatenate([x1 * cos - x2 * sin, x2 * cos + x1 * sin], axis=-1)
        B, T, D = hidden_states.shape
        hs = hidden_states
        q = (hs @ Wq.T).reshape(B, T, H, DK)
        k = (hs @ Wk.T).reshape(B, T, H, DK)
        pos = jnp.arange(T, dtype=jnp.float32)
        inv_freq = 1.0 / ROPE_BASE ** (jnp.arange(0, DK, 2, dtype=jnp.float32) / DK)
        ang = pos[:, None] * inv_freq[None, :]
        cos = jnp.cos(ang)[None, :, None, :]
        sin = jnp.sin(ang)[None, :, None, :]
        q = _rope(q, cos, sin).transpose(0, 2, 1, 3)
        k = _rope(k, cos, sin).transpose(0, 2, 1, 3)
        v = (hs @ Wv.T).reshape(B, T, H, DV).transpose(0, 2, 1, 3)
        s = hs @ Ws1.T @ Ws2.T + bs2
        s = jnp.clip(s, -CLAMP, CLAMP).reshape(B, T, H, M).transpose(0, 2, 1, 3)
        z = jax.lax.cumlogsumexp(s, axis=2)
        es = jnp.exp(s)
        enz = jnp.exp(-z)
        scale = DK ** (-0.5)
        mask = jnp.tril(jnp.ones((T, T), dtype=bool))
        A = jnp.einsum('bhtd,bhjd->bhtj', q, k) * scale
        A = jnp.where(mask, A, 0.0)
        ok = enz * jnp.einsum('bhtj,bhjm->bhtm', A, es)
        qv = jax.nn.softmax(ok, axis=-1)
        W2 = jnp.einsum('bhtm,bhjm->bhtj', qv * enz, es)
        W2 = jnp.where(mask, W2, 0.0)
        o = jnp.einsum('bhtj,bhjd->bhtd', W2, v)
        o = o.transpose(0, 2, 1, 3)
        g = (hs @ Wg.T).reshape(B, T, H, DV)
        o_n = o * jax.lax.rsqrt(jnp.mean(o * o, axis=-1, keepdims=True) + EPS) * g_norm_weight
        o_g = o_n * (g * jax.nn.sigmoid(g))
        return o_g.reshape(B, T, H * DV) @ Wo.T

    def _L1_attn_b_ref(x, norm_w, select_proj_w, select_proj_b, select_gate, x_proj_w, dt_proj_w, dt_proj_b, A_log, D_param, out_proj_w):
        import jax, jax.numpy as jnp
        import numpy as np
        B_SZ, L, D, N, R = (2, 256, 256, 128, 128)
        xn = x * jax.lax.rsqrt(jnp.mean(x * x, axis=-1, keepdims=True) + 1e-06) * norm_w
        mask = jax.nn.sigmoid((xn @ select_proj_w.T + select_proj_b) * select_gate)
        xn = xn * mask
        xp = xn @ x_proj_w.T
        delta = xp[..., :R]
        B_ssm = xp[..., R:R + N]
        C_ssm = xp[..., R + N:]
        delta = jax.nn.softplus(delta @ dt_proj_w.T + dt_proj_b)
        A = -jnp.exp(A_log)

        def step(h, inp):
            dt, bt, ct, xt = inp
            h = jnp.exp(dt[:, :, None] * A) * h + (dt * xt)[:, :, None] * bt[:, None, :]
            y = jnp.einsum('bdn,bn->bd', h, ct)
            return (h, y)
        h0 = jnp.zeros((x.shape[0], D, N), x.dtype)
        xs = (jnp.moveaxis(delta, 1, 0), jnp.moveaxis(B_ssm, 1, 0), jnp.moveaxis(C_ssm, 1, 0), jnp.moveaxis(xn, 1, 0))
        _, ys = jax.lax.scan(step, h0, xs)
        y = jnp.moveaxis(ys, 0, 1)
        return (y + x * D_param) @ out_proj_w.T

    def _L1_ffn_ref(x, gate_w, w1, w2, w3, sw1, sw2, sw3):
        import jax, jax.numpy as jnp
        import numpy as np
        DIM = 256
        E = 8
        TOPK = 2
        H = 176
        HS = H * 2
        TEMP = 1.0
        orig_shape = x.shape
        xf = x.reshape(-1, orig_shape[-1])
        N = xf.shape[0]
        scores = xf @ gate_w.T / TEMP
        probs = jax.nn.softmax(scores, axis=-1)
        topk_vals, topk_idx = jax.lax.top_k(probs, TOPK)
        expert_mask = jnp.zeros((N, E), dtype=xf.dtype)
        expert_mask = expert_mask.at[jnp.arange(N)[:, None], topk_idx].set(topk_vals)
        h = jax.nn.silu(jnp.einsum('nd,ehd->neh', xf, w1)) * jnp.einsum('nd,ehd->neh', xf, w3)
        expert_out = jnp.einsum('neh,edh->ned', h, w2)
        y = jnp.einsum('ned,ne->nd', expert_out, expert_mask)
        hs = jax.nn.silu(xf @ sw1.T) * (xf @ sw3.T)
        y = y + hs @ sw2.T
        return y.reshape(orig_shape)
    x = L0_attn_a_resid_pre
    x = x + _L0_attn_a_ref(_layernorm(x, axis=-1), L0_attn_a_Wq, L0_attn_a_Wk, L0_attn_a_Wv, L0_attn_a_Wo)
    x = x + _L0_ffn_ref(_layernorm(x, axis=-1), L0_ffn_router_w, L0_ffn_w_gate, L0_ffn_w_up, L0_ffn_w_down, L0_ffn_sh_gate, L0_ffn_sh_up, L0_ffn_sh_down, L0_ffn_sh_gate_w)
    x = x + _L0_attn_b_ref(_layernorm(x, axis=-1), L0_attn_b_attn_norm_w, L0_attn_b_Wq, L0_attn_b_Wk, L0_attn_b_Wv, L0_attn_b_Wg, L0_attn_b_Wo, L0_attn_b_conv_wq, L0_attn_b_conv_wk, L0_attn_b_conv_wv, L0_attn_b_gnorm_w, L0_attn_b_mlp_norm_w, L0_attn_b_W_gate, L0_attn_b_W_down)
    x = x + _L0_ffn_ref(_layernorm(x, axis=-1), L0_ffn_router_w, L0_ffn_w_gate, L0_ffn_w_up, L0_ffn_w_down, L0_ffn_sh_gate, L0_ffn_sh_up, L0_ffn_sh_down, L0_ffn_sh_gate_w)
    x = x + _L1_attn_a_ref(_layernorm(x, axis=-1), L1_attn_a_Wq, L1_attn_a_Wk, L1_attn_a_Wv, L1_attn_a_Wg, L1_attn_a_Wo, L1_attn_a_Ws1, L1_attn_a_Ws2, L1_attn_a_bs2, L1_attn_a_g_norm_weight)
    x = x + _L1_ffn_ref(_layernorm(x, axis=-1), L1_ffn_gate_w, L1_ffn_w1, L1_ffn_w2, L1_ffn_w3, L1_ffn_sw1, L1_ffn_sw2, L1_ffn_sw3)
    x = x + _L1_attn_b_ref(_layernorm(x, axis=-1), L1_attn_b_norm_w, L1_attn_b_select_proj_w, L1_attn_b_select_proj_b, L1_attn_b_select_gate, L1_attn_b_x_proj_w, L1_attn_b_dt_proj_w, L1_attn_b_dt_proj_b, L1_attn_b_A_log, L1_attn_b_D_param, L1_attn_b_out_proj_w)
    x = x + _L1_ffn_ref(_layernorm(x, axis=-1), L1_ffn_gate_w, L1_ffn_w1, L1_ffn_w2, L1_ffn_w3, L1_ffn_sw1, L1_ffn_sw2, L1_ffn_sw3)
    return x

_drawn_inputs = setup_inputs


def setup_inputs(seed=0):
    import zlib

    import numpy as np

    out = dict(_drawn_inputs(seed))
    spreads = {'L0_attn_b_attn_norm_w': (1.0, 0.6),
     'L0_attn_b_gnorm_w': (1.0, 0.6),
     'L0_attn_b_mlp_norm_w': (1.0, 0.6),
     'L1_attn_a_bs2': (0.0, 0.8),
     'L1_attn_a_g_norm_weight': (1.0, 0.6),
     'L1_attn_b_norm_w': (1.0, 0.6),
     'L1_attn_b_select_proj_b': (0.0, 0.8),
     'L1_attn_b_select_gate': (1.0, 0.6),
     'L1_attn_b_dt_proj_b': (0.0, 0.8),
     'L1_attn_b_D_param': (1.0, 0.6)}
    factors = {'L0_attn_b_W_gate': 5.687,
     'L0_attn_b_W_down': 5.473,
     'L1_attn_a_Wq': 8.0,
     'L1_attn_a_Wk': 8.0,
     'L1_attn_a_Ws1': 8.0,
     'L1_attn_a_Ws2': 8.0,
     'L1_attn_b_select_proj_w': 8.0,
     'L1_attn_b_x_proj_w': 3.134,
     'L1_attn_b_dt_proj_w': 8.0,
     'L1_attn_b_A_log': 8.0,
     'L1_ffn_gate_w': 8.0,
     'L1_ffn_w1': 8.0,
     'L1_ffn_w2': 8.0,
     'L1_ffn_w3': 8.0,
     'L1_ffn_sw1': 3.857,
     'L1_ffn_sw2': 3.833,
     'L1_ffn_sw3': 3.844}
    for name, (base, spread) in spreads.items():
        noise = np.random.default_rng([zlib.crc32(name.encode()), seed]).standard_normal(out[name].shape)
        drawn = base * np.exp(spread * noise) if base else spread * noise
        out[name] = jnp.asarray(drawn.astype(out[name].dtype))
    for name, factor in factors.items():
        out[name] = (out[name] * factor).astype(out[name].dtype)
    return out
```

```python
from contextlib import ExitStack

import numpy as np

import concourse.bass as bass
from concourse import mybir

F32 = mybir.dt.float32
BF16 = mybir.dt.bfloat16
ALU = mybir.AluOpType
ACT = mybir.ActivationFunctionType
AX = mybir.AxisListType.X

P = 128
B, S, D = 8, 256, 256
KC = D // P
TILES = B * S // P
CHUNKS = 4
CT = TILES // CHUNKS
N = CT * P
SEQS = N // S
LN_EPS = 1e-5
CAUSAL = S + P


class Chain:

    def __init__(self, eng, sem, base, per):
        self.eng, self.sem, self.base, self.per, self.k = eng, sem, base, per, 0

    def mark(self, ins):
        ins.then_inc(self.sem, 1)
        self.k += 1

    def wait(self, carrier=None):
        self.eng.wait_ge(self.sem, self.base + self.k)
        if carrier is not None:
            self.eng.memset(carrier, 0.0)

    def link(self, ins, carrier=None):
        self.mark(ins)
        self.wait(carrier)

    def done(self):
        assert self.k == self.per, (self.k, self.per)


class Shared:

    def __init__(self, nc, ctx, dram):
        self.nc, self.ctx, self.dram = nc, ctx, dram
        sb = lambda name, shape, dt=F32: ctx.enter_context(nc.sbuf_tensor(name, shape, dt))
        self.x = sb("x", [P, TILES + CT, D])
        self.fresh = sb("fresh", [P, CT, D])
        self.moments = sb("moments", [P, CT, 2])
        self.mean = sb("mean", [P, TILES + CT])
        self.rstd = sb("rstd", [P, TILES + CT])
        self.bn = sb("bn", [P, CT, 6])
        self.var_eps = sb("var_eps", [P, CT])
        self.minus_half = sb("minus_half", [P, 64])
        self.ident = sb("ident", [P, P])
        self.identb = sb("identb", [P, P], BF16)
        self.xn = sb("xn", [P, CT, D])
        self.xT = sb("xT", [P, KC, N])
        self.scratch = sb("scratch", [P, 1])
        self.pool_scratch = sb("pool_scratch", [P, 2])

        self.sems = []

    def sem(self, name):
        self.sems.append(self.nc.alloc_semaphore(name=name))
        return self.sems[-1]

    def end_block(self):
        self.nc.clear_and_free_semaphores(self.sems)
        self.sems = []
        self.nc.all_engine_barrier()


def tiles(c):
    return bass.ds(c * CT, CT)


def dve_stats(nc, sh, dve, c, new, chain, var_ready, rstd_ready):
    for j in range(CT):
        chain.mark(nc.vector.bn_stats(sh.bn[:, j, :], new[:, j, :]))
    chain.wait(carrier=sh.scratch[:, :])
    for j in range(CT):
        chain.mark(nc.vector.bn_aggr(sh.moments[:, j, :], sh.bn[:, j, :]))
    chain.wait(carrier=sh.scratch[:, :])
    chain.mark(nc.vector.tensor_copy(sh.mean[:, bass.ds(c * CT, CT)], sh.moments[:, :, 0]))
    nc.vector.tensor_scalar(sh.var_eps[:, :], sh.moments[:, :, 1], LN_EPS, None, ALU.add).then_inc(var_ready, 1)
    dve.wait_ge(rstd_ready, c + 1)


STATS_LINKS = 2 * CT + 1


def pool_rstd(nc, sh, pool, c, var_ready, rstd_ready):
    pool.wait_ge(var_ready, c + 1)
    nc.gpsimd.tensor_tensor(sh.rstd[:, bass.ds(c * CT, CT)], sh.var_eps[:, :],
                            sh.minus_half[:, 0:CT], ALU.pow).then_inc(rstd_ready, 1)


def dve_normalise(nc, sh, c, xn_ready):
    for j in range(CT):
        last = nc.vector.tensor_scalar(sh.xn[:, j, :], sh.x[:, bass.ds(c * CT + j, 1), :],
                                       sh.mean[:, bass.ds(c * CT + j, 1)],
                                       sh.rstd[:, bass.ds(c * CT + j, 1)],
                                       ALU.subtract, ALU.mult)
    last.then_inc(xn_ready, 1)


def dve_first_normalised(nc, sh, dve, xn_ready, kept=None, written=None):
    if written:
        dve.wait_ge(xn_ready, written)
    if kept:
        dve.wait_ge(kept, 1)
    dve_normalise(nc, sh, 0, xn_ready)


def pe_features(nc, src, ident, banks, done):
    for kc in range(KC):
        for j in range(CT):
            last = nc.tensor.transpose(banks[kc][:, j * P:(j + 1) * P],
                                       src[:, j, kc * P:(kc + 1) * P], ident[:, :])
        last.then_inc(done, 1)


def dve_add_residual(nc, sh, dve, c, out, out_used, kept):
    dve.wait_ge(kept, c)
    nc.vector.tensor_tensor(sh.fresh[:, :, :], sh.x[:, tiles(c), :], out[:, :, :], ALU.add).then_inc(out_used, 1)
    dve.wait_ge(out_used, c + 1)


def pool_keep(nc, sh, pool, c, out_used, kept):
    pool.wait_ge(out_used, c + 1)
    nc.gpsimd.tensor_copy(sh.x[:, tiles(c), :], sh.fresh[:, :, :]).then_inc(kept, 1)


def pool_carry(nc, sh, i):
    nc.gpsimd.tensor_tensor(sh.pool_scratch[:, i:i + 1], sh.minus_half[:, 0:1], sh.minus_half[:, 0:1], ALU.add)


def stream(sp, units, loads):
    def again(c, t, i, target):
        for used, load in loads:
            sp.wait_ge(used, c * units + t + 1)
            load(target, i)

    def chunk(c, last):
        with sp.Fori(0, units // 2 - 1) as pair:
            for i in range(2):
                again(c, 2 * pair + i, i, 2 * pair + i + 2)
        if not last:
            for i in range(2):
                again(c, units - 2 + i, i, i)

    for i in range(2):
        for _, load in loads:
            load(i, i)
    with sp.Fori(0, CHUNKS - 1) as c:
        chunk(c, False)
    chunk(CHUNKS - 1, True)


def load_block(nc, sh):
    d = sh.dram
    x_in, xn_ready = sh.sem("x_in"), sh.sem("ld_xn_ready")
    cleared, const_ready = sh.sem("ld_cleared"), sh.sem("ld_const")
    own, var_ready, rstd_ready = sh.sem("ld_own"), sh.sem("ld_var"), sh.sem("ld_rstd")
    xs = d["x"].rearrange("b (h p) d -> p (b h) d", p=P)
    with nc.Block() as block:
        @block.sync
        def _(sp):
            for c in range(CHUNKS):
                sp.dma_start(sh.x[:, c * CT:(c + 1) * CT, :], xs[:, c * CT:(c + 1) * CT, :]).then_inc(x_in, 16)
                sp.wait_ge(x_in, 16 * (c + 1))

        @block.gpsimd
        def _(pool):
            nc.gpsimd.memset(sh.minus_half[:, :], -0.5).then_inc(cleared, 1)
            nc.gpsimd.memset(sh.ident[:, :], 0.0).then_inc(cleared, 1)
            nc.gpsimd.memset(sh.identb[:, :], 0.0).then_inc(cleared, 1)
            nc.gpsimd.memset(sh.x[:, TILES:TILES + CT, :], 0.0).then_inc(cleared, 1)
            for t in (sh.mean, sh.rstd):
                nc.gpsimd.memset(t[:, TILES:TILES + CT], 0.0).then_inc(cleared, 1)
            pool.wait_ge(cleared, 3)
            for m in (sh.ident, sh.identb):
                nc.gpsimd.affine_select(out=m[:, :], in_=m[:, :], compare_op=ALU.not_equal, fill=1.0, base=0,
                                        pattern=[[-1, P]], channel_multiplier=1).then_inc(const_ready, 1)
            with pool.Fori(0, CHUNKS) as c:
                pool_rstd(nc, sh, pool, c, var_ready, rstd_ready)

        @block.vector
        def _(dve):
            for c in range(CHUNKS):
                dve.wait_ge(x_in, 16 * (c + 1))
                chain = Chain(dve, own, c * STATS_LINKS, STATS_LINKS)
                dve_stats(nc, sh, dve, c, sh.x[:, c * CT:(c + 1) * CT, :], chain, var_ready, rstd_ready)
                chain.done()
                if c == 0:
                    dve_first_normalised(nc, sh, dve, xn_ready)


def store_block(nc, sh):
    out_done = sh.sem("out_done")
    with nc.Block() as block:
        @block.sync
        def _(sp):
            sp.dma_start(sh.dram["out"].rearrange("b (h p) d -> p (b h) d", p=P), sh.x[:, 0:TILES, :]).then_inc(out_done, 16)
            sp.wait_ge(out_done, 16)


def l0_attention_block(nc, sh):
    d = sh.dram
    H, DH = 16, 128
    SCALE = float(DH) ** -0.5
    CLIP = 1024.0
    QCOLS = [(0, P), (P, CAUSAL)]
    s = lambda name: sh.sem(f"a0_{name}")
    bias_in = s("bias_in")
    w_in = [s(f"w_in{i}") for i in range(2)]
    wo_in = [s(f"wo_in{i}") for i in range(2)]
    xn_ready, xT_banked, xT_ready = s("xn_ready"), s("xT_banked"), s("xT_ready")
    q_done, k_done, v_done = s("q_done"), s("k_done"), s("v_done")
    q_ready, k_ready, v_ready = s("q_ready"), s("k_ready"), s("v_ready")
    scores_done, top_ready, exps_done = s("scores_done"), s("top_ready"), s("exps_done")
    inv_ready, probs_ready, turned = s("inv_ready"), s("probs_ready"), s("turned")
    probsT_ready = [s(f"probsT_ready{i}") for i in range(SEQS)]
    z_done, z_ready, wo_done = s("z_done"), s("z_ready"), s("wo_done")
    out_used, kept, own, var_ready, rstd_ready = s("out_used"), s("kept"), s("own"), s("var"), s("rstd")

    with ExitStack() as ctx:
        sb = lambda name, shape, dt=F32: ctx.enter_context(nc.sbuf_tensor(f"a0_{name}", shape, dt))
        ps = lambda name, shape: ctx.enter_context(nc.psum_tensor(f"a0_{name}", shape, F32))
        bias = sb("bias", [P, H, CAUSAL])
        w = sb("w", [P, 2, 3, KC, DH])
        wo = sb("wo", [P, 2, D])
        q, k = sb("q", [P, N]), sb("k", [P, N])
        v = sb("v", [P, 2, CT, DH])
        clipped = sb("clipped", [P, SEQS, CAUSAL])
        biased = sb("biased", [P, SEQS, CAUSAL])
        top, neg_top = sb("top", [P, SEQS, 2]), sb("neg_top", [P, SEQS, 2])
        sums, inv = sb("sums", [P, SEQS, 2]), sb("inv", [P, SEQS, 2])
        exps = sb("exps", [P, SEQS, CAUSAL])
        probs = sb("probs", [P, SEQS, CAUSAL])
        probsT = sb("probsT", [P, SEQS, CAUSAL])
        z = sb("z", [P, 2, N])
        qb, kb, vb, zb = (ps(f"{n}_bank", [P, N]) for n in "qkvz")
        score = ps("score", [P, SEQS, N])
        out = ps("out", [P, CT, D])
        block = ctx.enter_context(nc.Block())

        @block.sync
        def _(sp):
            def load_w(h, i):
                sp.dma_start(w[:, i, :, :, :].rearrange("p a k m -> p (a k m)"),
                             d["a0_w"][bass.ds(h, 1), :, 0:3 * D].rearrange("a p m -> (a p) m")).then_inc(w_in[i], 16)

            def load_wo(h, i):
                sp.dma_start(wo[:, i, :],
                             d["a0_w"][bass.ds(h, 1), :, 3 * D:4 * D].rearrange("a p m -> (a p) m")).then_inc(wo_in[i], 16)

            def again(used, count, load, unit, slot):
                sp.wait_ge(used, count)
                load(unit, slot)

            def chunk(c, first=False, last=False):
                n = c * H
                for i in range(2):
                    again(v_done, n + i + 1, load_w, i + 2, i)
                    if i or not first:
                        again(wo_done, n + i, load_wo, i + 1, 1 - i)
                with sp.Fori(1, H // 2 - 1) as k2:
                    for i in range(2):
                        again(v_done, n + 2 * k2 + i + 1, load_w, 2 * k2 + i + 2, i)
                        again(wo_done, n + 2 * k2 + i, load_wo, 2 * k2 + i + 1, 1 - i)
                if not last:
                    again(v_done, n + H - 1, load_w, 0, 0)
                again(wo_done, n + H - 2, load_wo, H - 1, 1)
                if not last:
                    again(v_done, n + H, load_w, 1, 1)
                    again(wo_done, n + H - 1, load_wo, 0, 0)

            for i in range(2):
                load_w(i, i)
                load_wo(i, i)
            chunk(0, first=True)
            with sp.Fori(1, CHUNKS - 1) as c:
                chunk(c)
            chunk(CHUNKS - 1, last=True)

        @block.tensor
        def _(pe):
            def project_qk(c, k2, i):
                n = c * H + 2 * k2 + i
                pe.wait_ge(w_in[i], 16 * (c * (H // 2) + k2 + 1))
                pe.wait_ge(q_ready, n)
                for a, bank, done in ((0, qb, q_done), (1, kb, k_done)):
                    if a == 1:
                        pe.wait_ge(k_ready, n)
                    for kc in range(KC):
                        last = nc.tensor.matmul(bank[:, :], w[:, i, a, kc, :], sh.xT[:, kc, :],
                                                start=kc == 0, stop=kc == KC - 1)
                    last.then_inc(done, 1)

            def project_v(c, k2, i):
                pe.wait_ge(v_ready, c * H + 2 * k2 + i)
                for j in range(CT):
                    for kc in range(KC):
                        last = nc.tensor.matmul(vb[:, j * DH:(j + 1) * DH], sh.xT[:, kc, j * P:(j + 1) * P],
                                                w[:, i, 2, kc, :], start=kc == 0, stop=kc == KC - 1)
                last.then_inc(v_done, 1)

            def scores(c, k2, i):
                n = c * H + 2 * k2 + i
                pe.wait_ge(q_ready, n + 1)
                pe.wait_ge(k_ready, n + 1)
                for b in range(SEQS):
                    pe.wait_ge(probsT_ready[b], n)
                    for half in range(2):
                        t0, (c0, c1) = b * S, QCOLS[half]
                        last = nc.tensor.matmul(score[:, b, c0:c1], q[:, t0 + half * P:t0 + (half + 1) * P],
                                                k[:, t0:t0 + (half + 1) * P], start=True, stop=True)
                    last.then_inc(scores_done, 1)

            def turn(c, k2, i):
                n = c * H + 2 * k2 + i
                for b in range(SEQS):
                    pe.wait_ge(probs_ready, 2 * n + b + 1)
                    for blk in range(3):
                        last = nc.tensor.transpose(score[:, b, blk * P:(blk + 1) * P],
                                                   probs[:, b, blk * P:(blk + 1) * P], sh.ident[:, :])
                    last.then_inc(turned, 1)

            def values(c, k2, i):
                n = c * H + 2 * k2 + i
                pe.wait_ge(v_ready, n + 1)
                pe.wait_ge(z_ready, n)
                for b in range(SEQS):
                    pe.wait_ge(probsT_ready[b], n + 1)
                    nc.tensor.matmul(zb[:, b * S:(b + 1) * S], v[:, i, 2 * b, :], probsT[:, b, 0:S],
                                     start=True, stop=False, skip_group_check=True)
                    last = nc.tensor.matmul(zb[:, b * S + P:(b + 1) * S], v[:, i, 2 * b + 1, :],
                                            probsT[:, b, S:CAUSAL], start=False, stop=True, skip_group_check=True)
                last.then_inc(z_done, 1)

            def output(c, k2, i, first=False, last_head=False):
                n = c * H + 2 * k2 + i
                pe.wait_ge(wo_in[i], 16 * (c * (H // 2) + k2 + 1))
                pe.wait_ge(z_ready, n + 1)
                if first:
                    pe.wait_ge(out_used, c)
                for j in range(CT):
                    last = nc.tensor.matmul(out[:, j, :], z[:, i, j * P:(j + 1) * P], wo[:, i, :],
                                            start=first and j % 2 == 0, stop=last_head, skip_group_check=True)
                last.then_inc(wo_done, 1)

            with pe.Fori(0, CHUNKS) as c:
                pe.wait_ge(xn_ready, c)
                pe_features(nc, sh.xn, sh.ident, (qb, kb), xT_banked)
                pe.wait_ge(xT_ready, 2 * (c + 1))
                project_qk(c, 0, 0)
                project_v(c, 0, 0)
                scores(c, 0, 0)
                project_qk(c, 0, 1)
                project_v(c, 0, 1)
                turn(c, 0, 0)
                values(c, 0, 0)
                scores(c, 0, 1)
                project_qk(c, 1, 0)
                project_v(c, 1, 0)
                turn(c, 0, 1)
                output(c, 0, 0, first=True)
                values(c, 0, 1)
                scores(c, 1, 0)
                with pe.Fori(1, H // 2 - 1) as k2:
                    project_qk(c, k2, 1)
                    project_v(c, k2, 1)
                    turn(c, k2, 0)
                    output(c, k2 - 1, 1)
                    values(c, k2, 0)
                    scores(c, k2, 1)
                    project_qk(c, k2 + 1, 0)
                    project_v(c, k2 + 1, 0)
                    turn(c, k2, 1)
                    output(c, k2, 0)
                    values(c, k2, 1)
                    scores(c, k2 + 1, 0)
                project_qk(c, H // 2 - 1, 1)
                project_v(c, H // 2 - 1, 1)
                turn(c, H // 2 - 1, 0)
                output(c, H // 2 - 2, 1)
                values(c, H // 2 - 1, 0)
                scores(c, H // 2 - 1, 1)
                output(c, H // 2 - 1, 0)
                turn(c, H // 2 - 1, 1)
                values(c, H // 2 - 1, 1)
                output(c, H // 2 - 1, 1, last_head=True)

        @block.scalar
        def _(act):
            act.dma_start(bias[:, :, :], d["a0_bias"]).then_inc(bias_in, 16)

            def take_q(c, k2, i):
                n = c * H + 2 * k2 + i
                act.wait_ge(q_done, n + 1)
                act.wait_ge(scores_done, 2 * n)
                nc.scalar.activation(q[:, :], qb[:, :], ACT.Copy, scale=SCALE).then_inc(q_ready, 1)

            def take_k(c, k2, i):
                act.wait_ge(k_done, c * H + 2 * k2 + i + 1)
                nc.scalar.activation(k[:, :], kb[:, :], ACT.Copy).then_inc(k_ready, 1)

            def take_v(c, k2, i):
                n = c * H + 2 * k2 + i
                act.wait_ge(v_done, n + 1)
                nc.scalar.activation(v[:, i, :, :].rearrange("p j e -> p (j e)"), vb[:, :], ACT.Copy).then_inc(v_ready, 1)

            def softmax(c, k2, i, b):
                n = c * H + 2 * k2 + i
                act.wait_ge(top_ready, 2 * n + b + 1)
                act.wait_ge(probs_ready, 2 * n)
                for half in range(2):
                    c0, c1 = QCOLS[half]
                    last = nc.scalar.activation(exps[:, b, c0:c1], biased[:, b, c0:c1], ACT.Exp,
                                                bias=neg_top[:, b, half:half + 1],
                                                accum_out=sums[:, b, half:half + 1])
                last.then_inc(exps_done, 1)

            def take_probsT(c, k2, i):
                act.wait_ge(turned, 2 * (c * H + 2 * k2 + i) + 2)
                nc.scalar.activation(probsT[:, 1, :], score[:, 1, 0:CAUSAL], ACT.Copy).then_inc(probsT_ready[1], 1)

            def step(c, head, following):
                softmax(c, *head, 0)
                take_q(c, *following)
                softmax(c, *head, 1)
                take_k(c, *following)
                take_v(c, *following)
                take_probsT(c, *head)

            with act.Fori(0, CHUNKS) as c:
                for kc, bank in enumerate((qb, kb)):
                    act.wait_ge(xT_banked, 2 * c + kc + 1)
                    nc.scalar.activation(sh.xT[:, kc, :], bank[:, :], ACT.Copy).then_inc(xT_ready, 1)
                take_q(c, 0, 0)
                take_k(c, 0, 0)
                take_v(c, 0, 0)
                step(c, (0, 0), (0, 1))
                with act.Fori(1, H // 2) as k2:
                    for (pk, pi), (nk, ni) in (((k2 - 1, 1), (k2, 0)), ((k2, 0), (k2, 1))):
                        step(c, (pk, pi), (nk, ni))
                softmax(c, H // 2 - 1, 1, 0)
                softmax(c, H // 2 - 1, 1, 1)
                take_probsT(c, H // 2 - 1, 1)

        @block.gpsimd
        def _(pool):
            with pool.Fori(0, CHUNKS) as c:
                with pool.Fori(0, H) as h:
                    n = c * H + h
                    for b in range(SEQS):
                        pool.wait_ge(inv_ready, 2 * n + b + 1)
                        pool.wait_ge(turned, 2 * n)
                        pool_carry(nc, sh, b)
                        for half in range(2):
                            c0, c1 = QCOLS[half]
                            last = nc.gpsimd.tensor_scalar(probs[:, b, c0:c1], exps[:, b, c0:c1],
                                                           inv[:, b, half:half + 1], 1.0, ALU.mult, ALU.mult)
                        last.then_inc(probs_ready, 1)
                pool_keep(nc, sh, pool, c, out_used, kept)
                pool_rstd(nc, sh, pool, c, var_ready, rstd_ready)

        @block.vector
        def _(dve):
            PER_HEAD = SEQS * 4
            LINKS = H * PER_HEAD + STATS_LINKS
            dve.wait_ge(bias_in, 16)
            with dve.Fori(0, CHUNKS) as c:
                with dve.Fori(0, H // 2) as k2:
                    for i in range(2):
                        h = 2 * k2 + i
                        n = c * H + h
                        chain = Chain(dve, own, c * LINKS + h * PER_HEAD, PER_HEAD)
                        for b in range(SEQS):
                            dve.wait_ge(scores_done, 2 * n + b + 1)
                            chain.link(nc.vector.tensor_scalar(clipped[:, b, :], score[:, b, 0:CAUSAL], CLIP, -CLIP,
                                                               ALU.min, ALU.max))
                            dve.wait_ge(exps_done, 2 * n)
                            chain.link(nc.vector.tensor_tensor(biased[:, b, :], clipped[:, b, :],
                                                               bias[:, bass.ds(h, 1), :], ALU.add))
                            for half in range(2):
                                c0, c1 = QCOLS[half]
                                chain.mark(nc.vector.tensor_reduce(top[:, b, half:half + 1], biased[:, b, c0:c1],
                                                                   AX, ALU.max))
                            chain.wait()
                            nc.vector.tensor_scalar(neg_top[:, b, :], top[:, b, :], -1.0, None,
                                                    ALU.mult).then_inc(top_ready, 1)
                        for b in range(SEQS):
                            dve.wait_ge(exps_done, 2 * n + b + 1)
                            nc.vector.reciprocal(inv[:, b, :], sums[:, b, :]).then_inc(inv_ready, 1)
                        chain.done()
                        dve.wait_ge(turned, 2 * n + 1)
                        nc.vector.tensor_copy(probsT[:, 0, :], score[:, 0, 0:CAUSAL]).then_inc(probsT_ready[0], 1)
                        dve.wait_ge(z_done, n + 1)
                        nc.vector.tensor_copy(z[:, i, :], zb[:, :]).then_inc(z_ready, 1)
                chain = Chain(dve, own, c * LINKS + H * PER_HEAD, STATS_LINKS)
                dve_normalise(nc, sh, c + 1, xn_ready)
                dve.wait_ge(wo_done, (c + 1) * H)
                dve_add_residual(nc, sh, dve, c, out, out_used, kept)
                dve_stats(nc, sh, dve, c, sh.fresh, chain, var_ready, rstd_ready)
                chain.done()
            dve_first_normalised(nc, sh, dve, xn_ready, kept, CHUNKS)


def ffn_block(nc, sh, tag, weights, router, sel, experts, top, n_tiles, gated):
    R = experts + 1
    T = n_tiles
    PAIRS = T // 2
    pad = max(8 - top, 4)
    assert T % 2 == 0 and 3 * R <= P
    s = lambda name: sh.sem(f"{tag}_{name}")
    rt_in, hot_in = s("rt_in"), s("hot_in")
    w_gu_in = [s(f"w_gu_in{i}") for i in range(2)]
    w_down_in = [s(f"w_down_in{i}") for i in range(2)]
    xn_ready, xT_banked, xT_ready = s("xn_ready"), s("xT_banked"), s("xT_ready")
    logits_done, shifted, exps_done, parts_ready = s("logits"), s("shifted"), s("exps"), s("parts")
    shares_banked, shares_ready = s("shares_banked"), s("shares")
    gate_done, up_done, bcast_done = s("gate_done"), s("up_done"), s("bcast_done")
    silu_done, act_done, hidden_done = s("silu_done"), s("act_done"), s("hidden_done")
    down_done, out_used = s("down_done"), s("out_used")
    own, init, var_ready, rstd_ready = s("own"), s("init"), s("var"), s("rstd")
    kept = s("kept")

    with ExitStack() as ctx:
        sb = lambda name, shape, dt=F32: ctx.enter_context(nc.sbuf_tensor(f"{tag}_{name}", shape, dt))
        ps = lambda name, shape, dt=F32: ctx.enter_context(nc.psum_tensor(f"{tag}_{name}", shape, dt))
        gu = sb("gu", [P, 2, 2, KC, P])
        down = sb("down", [P, 2, D])
        rt = sb("rt", [P, KC, R])
        onehot = sb("onehot", [P, T * P], BF16)
        logit = sb("logit", [P, CT, R])
        top1 = sb("top1", [P, CT])
        exps = sb("exps", [P, CT, R])
        total = sb("total", [P, CT])
        inv = sb("inv", [P, CT])
        probs = sb("probs", [P, CT, experts + pad])
        best = sb("best", [P, CT, 8])
        rest = sb("rest", [P, CT, experts + pad])
        share = sb("share", [P, CT, R])
        left = sb("left", [P, 2, CT, R])
        parts = sb("parts", [P, CT, P], BF16)
        shares = sb("shares", [P, N], BF16)
        act_g = sb("act_g", [P, 2, N])
        hidden = sb("hidden", [P, 2, N])
        gate = [ps(f"gate{i}", [P, N]) for i in range(2)]
        up = [ps(f"up{i}", [P, N]) for i in range(2)]
        bcast = [ps(f"bcast{i}", [P, N]) for i in range(2)]
        out = ps("out", [P, CT, D])
        logits = bcast[0][:, 0:CT * R].rearrange("p (j r) -> p j r", j=CT)
        turned = bcast[1][:, 0:N // 2].bitcast(BF16)

        block = ctx.enter_context(nc.Block())

        @block.sync
        def _(sp):
            sp.dma_start(rt[:, :, :], router).then_inc(rt_in, 16)

            def load_gate_up(t, i):
                sp.dma_start(gu[:, i, :, :, :].rearrange("p g k m -> p (g k m)"),
                             weights[bass.ds(t, 1), :, 0:2 * KC * P].rearrange("a p m -> (a p) m")).then_inc(w_gu_in[i], 16)

            def load_down(t, i):
                sp.dma_start(down[:, i, :],
                             weights[bass.ds(t, 1), :, 2 * KC * P:2 * KC * P + D]
                             .rearrange("a p m -> (a p) m")).then_inc(w_down_in[i], 16)

            stream(sp, T, [(up_done, load_gate_up), (down_done, load_down)])

        @block.tensor
        def _(pe):
            def gate_up(c, k, i, first):
                n = c * T + 2 * k + i
                pe.wait_ge(w_gu_in[i], 16 * (c * PAIRS + k + 1))
                if not first:
                    pe.wait_ge(silu_done, n - 1)
                for kc in range(KC):
                    last = nc.tensor.matmul(gate[i][:, :], gu[:, i, 0, kc, :], sh.xT[:, kc, :],
                                            start=kc == 0, stop=kc == KC - 1)
                last.then_inc(gate_done, 1)
                if not first:
                    pe.wait_ge(act_done, n - 1)
                for kc in range(KC):
                    last = nc.tensor.matmul(up[i][:, :], gu[:, i, 1, kc, :], sh.xT[:, kc, :],
                                            start=kc == 0, stop=kc == KC - 1)
                last.then_inc(up_done, 1)

            def broadcast(c, k, i, first):
                t = 2 * k + i
                if not first:
                    pe.wait_ge(hidden_done, c * T + t - 1)
                nc.tensor.matmul(bcast[i][:, :], onehot[:, bass.ds(t * P, P)], shares[:, :],
                                 start=True, stop=True).then_inc(bcast_done, 1)

            def project(c, k, i, first, last_tile):
                n = c * T + 2 * k + i
                pe.wait_ge(w_down_in[i], 16 * (c * PAIRS + k + 1))
                pe.wait_ge(hidden_done, n + 1)
                if first:
                    pe.wait_ge(out_used, c)
                for j in range(CT):
                    last = nc.tensor.matmul(out[:, j, :], hidden[:, i, j * P:(j + 1) * P], down[:, i, :],
                                            start=first and j % 2 == 0, stop=last_tile,
                                            skip_group_check=True)
                last.then_inc(down_done, 1)

            with pe.Fori(0, CHUNKS) as c:
                pe.wait_ge(xn_ready, c)
                pe.wait_ge(silu_done, c * T)
                pe_features(nc, sh.xn, sh.ident, gate, xT_banked)
                pe.wait_ge(xT_ready, 2 * (c + 1))
                pe.wait_ge(hidden_done, c * T)
                pe.wait_ge(rt_in, 16)
                for j in range(CT):
                    for kc in range(KC):
                        last = nc.tensor.matmul(logits[:, j, :], sh.xT[:, kc, j * P:(j + 1) * P], rt[:, kc, :],
                                                start=kc == 0, stop=kc == KC - 1)
                last.then_inc(logits_done, 1)
                gate_up(c, 0, 0, True)
                gate_up(c, 0, 1, True)
                pe.wait_ge(parts_ready, c + 1)
                for j in range(CT):
                    last = nc.tensor.transpose(turned[:, j * P:(j + 1) * P], parts[:, j, :], sh.identb[:, :])
                last.then_inc(shares_banked, 1)
                pe.wait_ge(shares_ready, c + 1)
                pe.wait_ge(hot_in, 16)
                broadcast(c, 0, 0, True)
                broadcast(c, 0, 1, True)
                project(c, 0, 0, True, False)
                with pe.Fori(0, PAIRS - 1) as pair:
                    for i in range(2):
                        gate_up(c, pair + 1, i, False)
                        broadcast(c, pair + 1, i, False)
                        project(c, pair + i, 1 - i, False, False)
                project(c, PAIRS - 1, 1, False, True)

        @block.scalar
        def _(act):
            act.dma_start(onehot[:, :], sel).then_inc(hot_in, 16)

            def silu(c, t, i, first):
                n = c * T + t
                act.wait_ge(gate_done, n + 1)
                if first:
                    act.wait_ge(hidden_done, c * T)
                else:
                    act.wait_ge(hidden_done, n - 1)
                nc.scalar.activation(act_g[:, i, :], gate[i][:, :], ACT.Silu).then_inc(silu_done, 1)

            with act.Fori(0, CHUNKS) as c:
                act.wait_ge(up_done, c * T)
                for kc in range(KC):
                    act.wait_ge(xT_banked, 2 * c + kc + 1)
                    nc.scalar.activation(sh.xT[:, kc, :], gate[kc][:, :], ACT.Copy).then_inc(xT_ready, 1)
                act.wait_ge(shifted, c + 1)
                nc.scalar.activation(exps[:, :, :], logit[:, :, :], ACT.Exp).then_inc(exps_done, 1)
                silu(c, 0, 0, True)
                silu(c, 1, 1, True)
                with act.Fori(0, PAIRS - 1) as pair:
                    for i in range(2):
                        silu(c, 2 * pair + i + 2, i, False)

        @block.gpsimd
        def _(pool):
            nc.gpsimd.memset(parts[:, :, :], 0.0).then_inc(init, 1)
            nc.gpsimd.memset(probs[:, :, :], -1.0).then_inc(init, 1)
            if not gated:
                nc.gpsimd.memset(share[:, :, :], 1.0).then_inc(init, 1)
                nc.gpsimd.memset(logit[:, :, :], 0.0).then_inc(init, 1)
            with pool.Fori(0, CHUNKS) as c:
                pool_keep(nc, sh, pool, c, out_used, kept)
                pool_rstd(nc, sh, pool, c, var_ready, rstd_ready)

        @block.vector
        def _(dve):
            LINKS = (24 if gated else 17) + STATS_LINKS
            E = experts
            dve.wait_ge(init, 2 if gated else 4)

            def wide(v, n):
                return v.rearrange("p (j a) -> p j a", a=1).broadcast_to([P, CT, n])

            def hidden_tile(c, t, i, first):
                n = c * T + t
                dve.wait_ge(silu_done, n + 1)
                dve.wait_ge(up_done, n + 1)
                nc.vector.tensor_tensor(act_g[:, i, :], act_g[:, i, :], up[i][:, :], ALU.mult).then_inc(act_done, 1)
                dve.wait_ge(bcast_done, n + 1)
                dve.wait_ge(act_done, n + 1)
                if not first:
                    dve.wait_ge(down_done, n - 1)
                nc.vector.tensor_tensor(hidden[:, i, :], act_g[:, i, :], bcast[i][:, :],
                                        ALU.mult).then_inc(hidden_done, 1)

            with dve.Fori(0, CHUNKS) as c:
                chain = Chain(dve, own, c * LINKS, LINKS)
                link = chain.link
                dve.wait_ge(logits_done, c + 1)
                link(nc.vector.tensor_reduce(top1[:, :], logits[:, :, 0:E], AX, ALU.max))
                if gated:
                    link(nc.vector.tensor_scalar(logit[:, :, E], logits[:, :, E], -1.0, None, ALU.mult))
                nc.vector.tensor_tensor(logit[:, :, 0:E], logits[:, :, 0:E], wide(top1[:, :], E),
                                        ALU.subtract).then_inc(shifted, 1)
                dve.wait_ge(exps_done, c + 1)
                link(nc.vector.tensor_reduce(total[:, :], exps[:, :, 0:E], AX, ALU.add))
                link(nc.vector.reciprocal(inv[:, :], total[:, :]))
                link(nc.vector.tensor_tensor(probs[:, :, 0:E], exps[:, :, 0:E], wide(inv[:, :], E), ALU.mult), carrier=sh.scratch[:, :])
                for j in range(CT):
                    chain.mark(nc.vector.max(best[:, j, :], probs[:, j, :]))
                chain.wait()
                if gated:
                    link(nc.vector.tensor_reduce(total[:, :], best[:, :, 0:top], AX, ALU.add))
                    link(nc.vector.tensor_scalar(total[:, :], total[:, :], 1e-9, None, ALU.max))
                    link(nc.vector.reciprocal(inv[:, :], total[:, :]))
                link(nc.vector.memset(best[:, :, top:8], -1.0), carrier=sh.scratch[:, :])
                for j in range(CT):
                    chain.mark(nc.vector.match_replace(rest[:, j, :], best[:, j, :], probs[:, j, :], 0.0))
                chain.wait()
                link(nc.vector.tensor_tensor(share[:, :, 0:E], probs[:, :, 0:E], rest[:, :, 0:E], ALU.subtract))
                if gated:
                    link(nc.vector.tensor_tensor(share[:, :, 0:E], share[:, :, 0:E], wide(inv[:, :], E), ALU.mult))
                    link(nc.vector.tensor_scalar(left[:, 0, :, E], exps[:, :, E], 1.0, None, ALU.add))
                    link(nc.vector.reciprocal(share[:, :, E], left[:, 0, :, E]))
                link(nc.vector.tensor_copy(parts[:, :, 0:R], share[:, :, :]))
                link(nc.vector.tensor_tensor(left[:, 0, :, :], share[:, :, :], parts[:, :, 0:R], ALU.subtract))
                link(nc.vector.tensor_copy(parts[:, :, R:2 * R], left[:, 0, :, :]))
                nc.vector.tensor_tensor(parts[:, :, 2 * R:3 * R], left[:, 0, :, :], parts[:, :, R:2 * R],
                                        ALU.subtract).then_inc(parts_ready, 1)
                dve.wait_ge(shares_banked, c + 1)
                nc.vector.tensor_copy(shares[:, :], turned).then_inc(shares_ready, 1)
                hidden_tile(c, 0, 0, True)
                hidden_tile(c, 1, 1, True)
                with dve.Fori(0, PAIRS - 1) as pair:
                    for i in range(2):
                        hidden_tile(c, 2 * pair + i + 2, i, False)
                dve_normalise(nc, sh, c + 1, xn_ready)
                dve.wait_ge(down_done, (c + 1) * T)
                dve_add_residual(nc, sh, dve, c, out, out_used, kept)
                dve_stats(nc, sh, dve, c, sh.fresh, chain, var_ready, rstd_ready)
                chain.done()
            dve_first_normalised(nc, sh, dve, xn_ready, kept, CHUNKS)


def retention_block(nc, sh):
    d = sh.dram
    H, DK, TAPS, EPS, MT = 8, 32, 4, 1e-5, 3
    HT = H // KC
    s = lambda name: sh.sem(f"rt_{name}")
    w_in = [s(f"w_in{i}") for i in range(9)]
    init, xn_ready = s("init"), s("xn_ready")
    sq_done, ms_ready, r_ready, normed = s("sq_done"), s("ms_ready"), s("r_ready"), s("normed")
    xT_banked, xT_ready = s("xT_banked"), s("xT_ready")
    proj_done, raw_ready, conv_ready, silu_ready = s("proj_done"), s("raw_ready"), s("conv_ready"), s("silu_ready")
    g_done, g_ready = s("g_done"), s("g_ready")
    swap_done, cosed, rot_ready = s("swap_done"), s("cosed"), s("rot_ready")
    v_turned, v_ready = s("v_turned"), s("v_ready")
    a_done, a_ready, o_done = s("a_done"), s("a_ready"), s("o_done")
    og_ready, turned_done, turned_ready = s("og_ready"), s("turned_done"), s("turned_ready")
    wo_done, h_ready = s("wo_done"), s("h_ready")
    gate_done, act_ready, hidden_ready, down_done = s("gate_done"), s("act_ready"), s("hidden_ready"), s("down_done")
    out_used, kept, own, var_ready, rstd_ready = s("out_used"), s("kept"), s("own"), s("var"), s("rstd")

    with ExitStack() as ctx:
        sb = lambda name, shape, dt=F32: ctx.enter_context(nc.sbuf_tensor(f"rt_{name}", shape, dt))
        ps = lambda name: ctx.enter_context(nc.psum_tensor(f"rt_{name}", [P, 2, N], F32))
        wqkvg = sb("wqkvg", [P, 4, KC, D])
        wo = sb("wo", [P, KC, D])
        w_gate = sb("w_gate", [P, 2, KC, MT * P])
        w_down = sb("w_down", [P, MT, D])
        swap = sb("swap", [P, P])
        rope = sb("rope", [P, 2, S])
        decay = sb("decay", [P, H, S])
        cols = sb("cols", [P, KC, 3 * TAPS + 2])
        gnw = sb("gnw", [P, D])
        square = sb("square", [P, CT, D])
        squares, ms, rr = sb("squares", [P, CT]), sb("ms", [P, CT * H]), sb("rr", [P, CT * H])
        normal = sb("normal", [P, CT, D])
        raw = sb("raw", [P, 3, KC, SEQS, TAPS - 1 + S])
        conv = sb("conv", [P, 3, KC, SEQS, S])
        qkv = sb("qkv", [P, 3, KC, N])
        turned = sb("turned", [P, 2, KC, N])
        sines = sb("sines", [P, KC, N])
        v = sb("v", [P, CT, D])
        gate = sb("gate", [P, CT, D])
        ad = sb("ad", [P, 2, SEQS, CAUSAL])
        og = sb("og", [P, CT, D])
        featT = sb("featT", [P, KC, N])
        hh = sb("hh", [P, CT, D])
        act_g = sb("act_g", [P, MT, N])
        A, Bk, C, E = ps("A"), ps("B"), ps("C"), ps("D")
        block = ctx.enter_context(nc.Block())
        flat = lambda t: t.rearrange("p j e -> p (j e)")
        token = lambda bank: bank[:, :, :].rearrange("p a t -> p (a t)").rearrange("p (j e) -> p j e", j=CT)

        @block.sync
        def _(sp):
            for t, name, in_ in ((cols, "rt_cols", 0), (wqkvg, "rt_wqkvg", 1), (swap, "rt_swap", 2),
                                 (rope, "rt_rope", 3), (decay, "rt_decay", 4)):
                sp.dma_start(t[:], d[name]).then_inc(w_in[in_], 16)

        @block.tensor
        def _(pe):
            def turn(src, bank, done):
                pe_features(nc, src, sh.ident, (bank[:, 0, :], bank[:, 1, :]), done)

            for in_ in w_in:
                pe.wait_ge(in_, 16)
            with pe.Fori(0, CHUNKS) as c:
                pe.wait_ge(normed, 2 * c + 1)
                pe.wait_ge(hidden_ready, c * MT)
                turn(normal, A, xT_banked)
                pe.wait_ge(xT_ready, 2 * c + 1)
                pe.wait_ge(kept, c)
                for a, bank in enumerate((Bk, C, E)):
                    for m in range(KC):
                        for kc in range(KC):
                            last = nc.tensor.matmul(bank[:, m, :], wqkvg[:, a, kc, m * P:(m + 1) * P], sh.xT[:, kc, :],
                                                    start=kc == 0, stop=kc == KC - 1)
                    last.then_inc(proj_done, 1)
                for j in range(CT):
                    for kc in range(KC):
                        last = nc.tensor.matmul(token(A)[:, j, :], sh.xT[:, kc, j * P:(j + 1) * P], wqkvg[:, 3, kc, :],
                                                start=kc == 0, stop=kc == KC - 1, skip_group_check=True)
                last.then_inc(g_done, 1)
                for a, bank in enumerate((Bk, C)):
                    pe.wait_ge(silu_ready, 3 * c + a + 1)
                    for m in range(KC):
                        last = nc.tensor.matmul(bank[:, m, :], swap[:, :], qkv[:, a, m, :], start=True, stop=True)
                    last.then_inc(swap_done, 1)
                pe.wait_ge(silu_ready, 3 * c + 3)
                for m in range(KC):
                    for j in range(CT):
                        last = nc.tensor.transpose(token(E)[:, j, m * P:(m + 1) * P],
                                                   qkv[:, 2, m, j * P:(j + 1) * P], sh.ident[:, :])
                last.then_inc(v_turned, 1)
                pe.wait_ge(rot_ready, 2 * c + 2)

                def scores(h):
                    bank, p0, m = (Bk, C)[h % 2], DK * (h % HT), h // HT
                    if h >= 2:
                        pe.wait_ge(a_ready, c * H + h - 1)
                    for b in range(SEQS):
                        for kb in range(2):
                            t0 = b * S
                            last = nc.tensor.matmul(bank[:, b, kb * S:kb * S + S - kb * P],
                                                    turned[p0:p0 + DK, 1, m, t0 + kb * P:t0 + (kb + 1) * P],
                                                    turned[p0:p0 + DK, 0, m, t0 + kb * P:t0 + S],
                                                    start=True, stop=True, skip_group_check=True)
                    last.then_inc(a_done, 1)

                def values(h):
                    pe.wait_ge(a_ready, c * H + h + 1)
                    for b in range(SEQS):
                        for half in range(2):
                            for kb in range(half + 1):
                                c0 = half * P if kb == 0 else S
                                last = nc.tensor.matmul(token(E)[:, 2 * b + half, h * DK:(h + 1) * DK],
                                                        ad[:, h % 2, b, c0:c0 + P], v[:, 2 * b + kb, h * DK:(h + 1) * DK],
                                                        start=kb == 0, stop=kb == half, skip_group_check=True)
                    if h == H - 1:
                        last.then_inc(o_done, 1)

                scores(0)
                pe.wait_ge(v_ready, c + 1)
                for h in range(1, H):
                    scores(h)
                    values(h - 1)
                values(H - 1)
                pe.wait_ge(og_ready, c + 1)
                turn(og, Bk, turned_done)
                pe.wait_ge(turned_ready, 2 * c + 1)
                for j in range(CT):
                    for kc in range(KC):
                        last = nc.tensor.matmul(token(C)[:, j, :], featT[:, kc, j * P:(j + 1) * P], wo[:, kc, :],
                                                start=kc == 0, stop=kc == KC - 1, skip_group_check=True)
                last.then_inc(wo_done, 1)
                pe.wait_ge(normed, 2 * c + 2)
                turn(normal, Bk, turned_done)
                pe.wait_ge(turned_ready, 2 * c + 2)
                pe.wait_ge(g_ready, c + 1)
                for t, bank in enumerate((A, Bk, C)):
                    for a in range(2):
                        for kc in range(KC):
                            last = nc.tensor.matmul(bank[:, a, :], w_gate[:, a, kc, t * P:(t + 1) * P], featT[:, kc, :],
                                                    start=kc == 0, stop=kc == KC - 1)
                    last.then_inc(gate_done, 1)
                for t in range(MT):
                    pe.wait_ge(hidden_ready, c * MT + t + 1)
                    for j in range(CT):
                        last = nc.tensor.matmul(token(E)[:, j, :], act_g[:, t, j * P:(j + 1) * P], w_down[:, t, :],
                                                start=t == 0 and j % 2 == 0, stop=t == MT - 1, skip_group_check=True)
                last.then_inc(down_done, 1)

        @block.scalar
        def _(act):
            for t, name, in_ in ((gnw, "rt_gnw", 5), (wo, "rt_wo", 6), (w_gate, "rt_w_gate", 7), (w_down, "rt_w_down", 8)):
                act.dma_start(t[:], d[name]).then_inc(w_in[in_], 16)

            def squares_of(src, k, n):
                act.wait_ge(ms_ready, n)
                for j in range(CT):
                    last = nc.scalar.activation(square[:, j, :], src[:, j, :], ACT.Square, accum_out=squares[:, j:j + 1])
                last.then_inc(sq_done, 1)

            act.wait_ge(w_in[0], 16)
            act.wait_ge(init, 1)
            with act.Fori(0, CHUNKS) as c:
                act.wait_ge(xn_ready, c + 1)
                squares_of(sh.xn, 0, 3 * c)
                act.wait_ge(xT_banked, 2 * c + 2)
                for kc in range(KC):
                    last = nc.scalar.activation(sh.xT[:, kc, :], A[:, kc, :], ACT.Copy, scale=cols[:, kc, 12:13])
                    if kc == KC - 1:
                        last.then_inc(xT_ready, 2)
                for a, bank in enumerate((Bk, C, E)):
                    act.wait_ge(proj_done, 3 * c + a + 1)
                    act.wait_ge(conv_ready, 3 * c + a)
                    for m in range(KC):
                        last = nc.scalar.activation(raw[:, a, m, :, TAPS - 1:TAPS - 1 + S],
                                                    bank[:, m, :].rearrange("p (b t) -> p b t", b=SEQS), ACT.Copy)
                    last.then_inc(raw_ready, 1)
                act.wait_ge(g_done, c + 1)
                nc.scalar.activation(flat(gate[:, :, :]), A[:, :, :].rearrange("p a t -> p (a t)"), ACT.Silu).then_inc(g_ready, 1)
                for a in range(3):
                    act.wait_ge(conv_ready, 3 * c + a + 1)
                    nc.scalar.activation(qkv[:, a, :, :].rearrange("p m t -> p (m t)"),
                                         conv[:, a, :, :, :].rearrange("p m b t -> p (m b t)"), ACT.Silu).then_inc(silu_ready, 1)
                act.wait_ge(v_turned, c + 1)
                nc.scalar.activation(flat(v[:, :, :]), E[:, :, :].rearrange("p a t -> p (a t)"), ACT.Copy).then_inc(v_ready, 1)
                act.wait_ge(o_done, c + 1)
                act.wait_ge(ms_ready, 3 * c + 1)
                nc.scalar.activation(flat(square[:, :, :]), E[:, :, :].rearrange("p a t -> p (a t)"), ACT.Square).then_inc(sq_done, 1)
                act.wait_ge(turned_done, 4 * c + 2)
                nc.scalar.activation(featT[:, :, :].rearrange("p k t -> p (k t)"),
                                     Bk[:, :, :].rearrange("p a t -> p (a t)"), ACT.Copy).then_inc(turned_ready, 1)
                act.wait_ge(h_ready, c + 1)
                squares_of(hh, 2, 3 * c + 2)
                act.wait_ge(turned_done, 4 * c + 4)
                for kc in range(KC):
                    last = nc.scalar.activation(featT[:, kc, :], Bk[:, kc, :], ACT.Copy, scale=cols[:, kc, 13:14])
                last.then_inc(turned_ready, 1)
                for t, bank in enumerate((A, Bk, C)):
                    act.wait_ge(gate_done, c * MT + t + 1)
                    nc.scalar.activation(act_g[:, t, :], bank[:, 0, :], ACT.Silu).then_inc(act_ready, 1)

        @block.gpsimd
        def _(pool):
            nc.gpsimd.memset(raw[:, :, :, :, :].rearrange("p a m b t -> p (a m b t)"), 0.0).then_inc(init, 1)
            pool.wait_ge(w_in[3], 16)

            def root(n, width):
                pool.wait_ge(ms_ready, n)
                nc.gpsimd.tensor_tensor(rr[:, 0:width], ms[:, 0:width], sh.minus_half[:, 0:width], ALU.pow).then_inc(r_ready, 1)

            with pool.Fori(0, CHUNKS) as c:
                root(3 * c + 1, CT)
                for a in range(2):
                    pool.wait_ge(silu_ready, 3 * c + a + 1)
                    for m in range(KC):
                        for b in range(SEQS):
                            last = nc.gpsimd.tensor_tensor(turned[:, a, m, b * S:(b + 1) * S], qkv[:, a, m, b * S:(b + 1) * S],
                                                           rope[:, 0, :], ALU.mult)
                    last.then_inc(cosed, 1)
                root(3 * c + 2, CT * H)
                root(3 * c + 3, CT)
                pool_keep(nc, sh, pool, c, out_used, kept)
                pool_rstd(nc, sh, pool, c, var_ready, rstd_ready)

        @block.vector
        def _(dve):
            LINKS = 3 * KC * (TAPS - 1) + 8 + STATS_LINKS
            for in_ in w_in:
                dve.wait_ge(in_, 16)

            def mean_square(chain, n, width, count):
                nc.vector.tensor_scalar(ms[:, 0:width], ms[:, 0:width] if width > CT else squares[:, :], 1.0 / count, EPS,
                                        ALU.mult, ALU.add).then_inc(ms_ready, 1)
                dve.wait_ge(r_ready, n)

            def scale_rows(src):
                for j in range(CT):
                    last = nc.vector.tensor_scalar(normal[:, j, :], src[:, j, :], rr[:, j:j + 1], None, ALU.mult)
                last.then_inc(normed, 1)

            with dve.Fori(0, CHUNKS) as c:
                chain = Chain(dve, own, c * LINKS, LINKS)
                dve_normalise(nc, sh, c, xn_ready)
                dve.wait_ge(sq_done, 3 * c + 1)
                mean_square(chain, 3 * c + 1, CT, D)
                scale_rows(sh.xn)
                for a in range(3):
                    dve.wait_ge(raw_ready, 3 * c + a + 1)
                    for i in range(TAPS):
                        for m in range(KC):
                            tap = cols[:, m, a * TAPS + i:a * TAPS + i + 1]
                            shifted = raw[:, a, m, :, i:i + S]
                            if i == 0:
                                ins = nc.vector.tensor_scalar(conv[:, a, m, :, :], shifted, tap, None, ALU.mult)
                            else:
                                ins = nc.vector.scalar_tensor_tensor(out=conv[:, a, m, :, :], in0=shifted, scalar=tap,
                                                                     in1=conv[:, a, m, :, :], op0=ALU.mult, op1=ALU.add)
                            if i < TAPS - 1:
                                chain.mark(ins)
                        if i < TAPS - 1:
                            chain.wait()
                    ins.then_inc(conv_ready, 1)
                for a, bank in enumerate((Bk, C)):
                    dve.wait_ge(swap_done, 2 * c + a + 1)
                    for m in range(KC):
                        ins = nc.vector.tensor_tensor(
                            sines[:, m, :].rearrange("p (b t) -> p b t", b=SEQS),
                            bank[:, m, :].rearrange("p (b t) -> p b t", b=SEQS),
                            rope[:, 1, :].rearrange("p (a t) -> p a t", a=1).broadcast_to([P, SEQS, S]), ALU.mult)
                        chain.mark(ins)
                    chain.wait()
                    dve.wait_ge(cosed, 2 * c + a + 1)
                    nc.vector.tensor_tensor(turned[:, a, :, :].rearrange("p m t -> p (m t)"),
                                            turned[:, a, :, :].rearrange("p m t -> p (m t)"),
                                            sines[:, :, :].rearrange("p m t -> p (m t)"), ALU.add).then_inc(rot_ready, 1)
                    dve.wait_ge(rot_ready, 2 * c + a + 1)
                for h in range(H):
                    dve.wait_ge(a_done, c * H + h + 1)
                    bank = (Bk, C)[h % 2]
                    for b in range(SEQS):
                        nc.vector.tensor_tensor(ad[:, h % 2, b, 0:S], bank[:, b, 0:S], decay[:, h, :], ALU.mult)
                        last = nc.vector.tensor_tensor(ad[:, h % 2, b, S:CAUSAL], bank[:, b, S:CAUSAL],
                                                       decay[:, h, 0:P], ALU.mult)
                    last.then_inc(a_ready, 1)
                dve.wait_ge(g_ready, c + 1)
                chain.mark(nc.vector.tensor_tensor(gate[:, :, :], gate[:, :, :],
                                                   gnw[:, :].rearrange("p (a e) -> p a e", a=1).broadcast_to([P, CT, D]),
                                                   ALU.mult))
                dve.wait_ge(sq_done, 3 * c + 2)
                chain.link(nc.vector.tensor_reduce(ms[:, :], flat(square[:, :, :]).rearrange("p (g e) -> p g e", e=DK),
                                                   AX, ALU.add))
                mean_square(chain, 3 * c + 2, CT * H, DK)
                chain.link(nc.vector.tensor_tensor(
                    flat(og[:, :, :]).rearrange("p (g e) -> p g e", e=DK),
                    E[:, :, :].rearrange("p a t -> p (a t)").rearrange("p (g e) -> p g e", e=DK),
                    rr[:, :].rearrange("p (g a) -> p g a", a=1).broadcast_to([P, CT * H, DK]), ALU.mult))
                nc.vector.tensor_tensor(flat(og[:, :, :]), flat(og[:, :, :]), flat(gate[:, :, :]), ALU.mult).then_inc(og_ready, 1)
                dve.wait_ge(wo_done, c + 1)
                nc.vector.tensor_tensor(hh[:, :, :], sh.xn[:, :, :], token(C), ALU.add).then_inc(h_ready, 1)
                dve.wait_ge(sq_done, 3 * c + 3)
                dve.wait_ge(h_ready, c + 1)
                mean_square(chain, 3 * c + 3, CT, D)
                scale_rows(hh)
                for t, bank in enumerate((A, Bk, C)):
                    dve.wait_ge(act_ready, c * MT + t + 1)
                    nc.vector.tensor_tensor(act_g[:, t, :], act_g[:, t, :], bank[:, 1, :], ALU.mult).then_inc(hidden_ready, 1)
                dve.wait_ge(down_done, c + 1)
                chain.link(nc.vector.tensor_tensor(hh[:, :, :], hh[:, :, :], token(E), ALU.add))
                dve_add_residual(nc, sh, dve, c, hh, out_used, kept)
                dve_stats(nc, sh, dve, c, sh.fresh, chain, var_ready, rstd_ready)
                chain.done()
            dve_first_normalised(nc, sh, dve, xn_ready, kept, CHUNKS)


def l1_attention_block(nc, sh):
    d = sh.dram
    H, DH, M, R = 16, 128, 64, 16
    CLAMP, EPS = 32.0, 1e-5
    RA = R + 1
    s = lambda name: sh.sem(f"a1_{name}")
    const_in = [s(f"const_in{i}") for i in range(3)]
    gn_in = s("gn_in")
    w_in = [s(f"w_in{i}") for i in range(2)]
    wo_in = [s(f"wo_in{i}") for i in range(2)]
    xn_ready, xT_banked, xT_ready = s("xn_ready"), s("xT_banked"), s("xT_ready")
    low_done, low_ready, init = s("low_done"), s("low_ready"), s("init")
    q_done, k_done, v_done, g_done = s("q_done"), s("k_done"), s("v_done"), s("g_done")
    qk_cosed, qk_swapped, qk_sined, qk_ready = s("qk_cosed"), s("qk_swapped"), s("qk_sined"), s("qk_ready")
    v_ready, tanh_ready, g_ready = s("v_ready"), s("tanh_ready"), s("g_ready")
    slot_done, slot_clipped, es_ready = s("slot_done"), s("slot_clipped"), s("es_ready")
    slotT_done, slotT_clipped, esT_ready = s("slotT_done"), s("slotT_clipped"), s("esT_ready")
    sum_done, enz_ready = s("sum_done"), s("enz_ready")
    a_done, a_ready, ok_done, ok_read = s("a_done"), s("a_ready"), s("ok_done"), s("ok_read")
    shifted, exps_done, w_ready = s("shifted"), s("exps_done"), s("w_ready")
    wT_done, wT_ready, w2_done, w2_ready = s("wT_done"), s("wT_ready"), s("w2_done"), s("w2_ready")
    o_done, squares_done, ms_ready, rms_ready, og_ready = (
        s("o_done"), s("squares_done"), s("ms_ready"), s("rms_ready"), s("og_ready"))
    oT_done, oT_ready, wo_done = s("oT_done"), s("oT_ready"), s("wo_done")
    out_used, kept, own, var_ready, rstd_ready = s("out_used"), s("kept"), s("own"), s("var"), s("rstd")

    with ExitStack() as ctx:
        sb = lambda name, shape, dt=F32: ctx.enter_context(nc.sbuf_tensor(f"a1_{name}", shape, dt))
        ps = lambda name, shape: ctx.enter_context(nc.psum_tensor(f"a1_{name}", shape, F32))
        w = sb("w", [P, 2, 4 * D + M])
        wo = sb("wo", [P, 2, D])
        ws1 = sb("ws1", [P, KC, R])
        rope = sb("rope", [P, 2, S])
        masks = sb("masks", [P, 2, CAUSAL])
        ones = sb("ones", [P, P])
        gn = sb("gn", [P, 1])
        gn_half = sb("gn_half", [P, 1])
        low = sb("low", [RA, N])
        qk = sb("qk", [P, 2, N])
        cosed = sb("cosed", [P, 2, N])
        swapped = sb("swapped", [P, 2, N])
        v = sb("v", [P, 2, CT, DH])
        tanh = sb("tanh", [P, N])
        gate = sb("gate", [P, 2, CT, DH])
        slot_in = sb("slot_in", [P, CT, M])
        es = sb("es", [P, CT, M])
        slotT_in = sb("slotT_in", [M, N])
        esT = sb("esT", [M, 2, N])
        enz = sb("enz", [P, CT, M])
        a = sb("a", [P, SEQS, CAUSAL])
        ok = sb("ok", [P, CT, M])
        top = sb("top", [P, CT])
        exps = sb("exps", [P, CT, M])
        total, inv = sb("total", [P, CT]), sb("inv", [P, CT])
        slot_w = sb("slot_w", [P, CT, M])
        wT = sb("wT", [M, N])
        w2 = sb("w2", [P, SEQS, CAUSAL])
        square = sb("square", [P, CT, DH])
        squares, ms, rms = sb("squares", [P, CT]), sb("ms", [P, CT]), sb("rms", [P, CT])
        og = sb("og", [P, CT, DH])
        oT = sb("oT", [P, 2, N])
        pair = ps("pair", [P, 2, N])
        vb, gb = ps("v_bank", [P, N]), ps("g_bank", [P, N])
        ab = ps("a_bank", [P, 2, N])
        out = ps("out", [P, CT, D])
        okb = ab[:, 0, 0:CT * M].rearrange("p (j m) -> p j m", j=CT)
        slotb = ab[:, 0, CT * M:2 * CT * M].rearrange("p (j m) -> p j m", j=CT)
        slotTb = ab[0:M, 1, :]
        sumb = gb[:, 0:CT * M].rearrange("p (j m) -> p j m", j=CT)
        wTb = ab[0:M, 1, :]
        ob = vb
        oTb = gb
        block = ctx.enter_context(nc.Block())
        HH = H // 2

        @block.sync
        def _(sp):
            def load_w(h, i):
                sp.dma_start(w[:, i, :], d["a1_w"][bass.ds(h, 1), :, 0:4 * D + M]
                             .rearrange("a p m -> (a p) m")).then_inc(w_in[i], 16)

            def load_wo(h, i):
                sp.dma_start(wo[:, i, :], d["a1_w"][bass.ds(h, 1), :, 4 * D + M:5 * D + M]
                             .rearrange("a p m -> (a p) m")).then_inc(wo_in[i], 16)

            sp.dma_start(ws1[:, :, :], d["a1_ws1"]).then_inc(const_in[0], 16)
            stream(sp, H, [(slotT_done, load_w), (wo_done, load_wo)])

        @block.tensor
        def _(pe):
            lhs = lambda i, a_, kc: w[:, i, a_ * D + kc * P:a_ * D + (kc + 1) * P]

            def project_qk(c, k2, i):
                n = c * H + 2 * k2 + i
                pe.wait_ge(w_in[i], 16 * (c * HH + k2 + 1))
                for a_, done in ((0, q_done), (1, k_done)):
                    for kc in range(KC):
                        last = nc.tensor.matmul(pair[:, a_, :], lhs(i, a_, kc), sh.xT[:, kc, :],
                                                start=kc == 0, stop=kc == KC - 1)
                    last.then_inc(done, 1)

            def project_tokens(c, k2, i, a_, bank, done, then=None):
                for j in range(CT):
                    if then and j == CT - 1:
                        pe.wait_ge(*then)
                    for kc in range(KC):
                        last = nc.tensor.matmul(bank[:, j * DH:(j + 1) * DH], sh.xT[:, kc, j * P:(j + 1) * P],
                                                lhs(i, a_, kc), start=kc == 0, stop=kc == KC - 1)
                last.then_inc(done, 1)

            def slots(c, k2, i, token_major):
                n = c * H + 2 * k2 + i
                ws2 = w[0:RA, i, 4 * D:4 * D + M]
                if token_major:
                    pe.wait_ge(ok_read, n)
                    for j in range(CT):
                        last = nc.tensor.matmul(slotb[:, j, :], low[:, j * P:(j + 1) * P], ws2, start=True, stop=True,
                                                skip_group_check=True)
                    last.then_inc(slot_done, 1)
                else:
                    nc.tensor.matmul(slotTb, ws2, low[:, :], start=True, stop=True).then_inc(slotT_done, 1)

            def slot_sums(c, k2, i):
                n = c * H + 2 * k2 + i
                pe.wait_ge(es_ready, n + 1)
                pe.wait_ge(g_ready, n + 1)
                nc.tensor.matmul(sumb, masks[:, 1, 0:P], es[:, :, :], start=True, stop=False, skip_group_check=True)
                nc.tensor.matmul(sumb[:, 1:CT:2, :], ones[:, :], es[:, 0:CT:2, :], start=False, stop=True,
                                 skip_group_check=True).then_inc(sum_done, 1)

            def scores(c, k2, i):
                n = c * H + 2 * k2 + i
                pe.wait_ge(qk_ready, 2 * (n + 1))
                pe.wait_ge(slot_clipped, n + 1)
                pe.wait_ge(slotT_clipped, n + 1)
                for b in range(SEQS):
                    for kb in range(2):
                        t0 = b * S
                        last = nc.tensor.matmul(ab[:, b, kb * S:kb * S + S - kb * P],
                                                qk[:, 1, t0 + kb * P:t0 + (kb + 1) * P], qk[:, 0, t0 + kb * P:t0 + S],
                                                start=True, stop=True, skip_group_check=True)
                last.then_inc(a_done, 1)

            def key_block(t, b, half, kb):
                c0 = half * P if kb == 0 else S
                return t[:, b, c0:c0 + P]

            def ok_products(c, k2, i, then):
                pe.wait_ge(a_ready, c * H + 2 * k2 + i + 1)
                for b in range(SEQS):
                    for half in range(2):
                        for kb in range(half + 1):
                            if b == SEQS - 1 and kb:
                                for wait in then:
                                    pe.wait_ge(*wait)
                            last = nc.tensor.matmul(okb[:, 2 * b + half, :], key_block(a, b, half, kb), es[:, 2 * b + kb, :],
                                                    start=kb == 0, stop=kb == half, skip_group_check=True)
                last.then_inc(ok_done, 1)

            def turn_w(c, k2, i):
                n = c * H + 2 * k2 + i
                for j in range(CT):
                    last = nc.tensor.transpose(wTb[:, j * P:(j + 1) * P], slot_w[:, j, :], sh.ident[:, :])
                last.then_inc(wT_done, 1)

            def w2_products(c, k2, i, swapped_by):
                n = c * H + 2 * k2 + i
                pe.wait_ge(wT_ready, n + 1)
                pe.wait_ge(esT_ready, n + 1)
                pe.wait_ge(qk_swapped, swapped_by)
                for b in range(SEQS):
                    for kb in range(2):
                        t0 = b * S
                        last = nc.tensor.matmul(pair[:, b, kb * S:kb * S + S - kb * P],
                                                esT[:, i, t0 + kb * P:t0 + (kb + 1) * P], wT[:, t0 + kb * P:t0 + S],
                                                start=True, stop=True, skip_group_check=True)
                last.then_inc(w2_done, 1)

            def o_products(c, k2, i, v_taken):
                n = c * H + 2 * k2 + i
                pe.wait_ge(w2_ready, n + 1)
                pe.wait_ge(v_ready, v_taken)
                for b in range(SEQS):
                    for half in range(2):
                        j = 2 * b + half
                        for kb in range(half + 1):
                            last = nc.tensor.matmul(ob[:, j * DH:(j + 1) * DH], key_block(w2, b, half, kb),
                                                    v[:, i, 2 * b + kb, :], start=kb == 0, stop=kb == half,
                                                    skip_group_check=True)
                last.then_inc(o_done, 1)

            def turn_o(c, k2, i):
                for j in range(CT):
                    last = nc.tensor.transpose(oTb[:, j * P:(j + 1) * P], og[:, j, :], sh.ident[:, :])
                last.then_inc(oT_done, 1)

            def output(c, k2, i, js, first=False, last_head=False):
                n = c * H + 2 * k2 + i
                if 0 in js:
                    pe.wait_ge(wo_in[i], 16 * (c * HH + k2 + 1))
                    pe.wait_ge(oT_ready, n + 1)
                    if first:
                        pe.wait_ge(out_used, c)
                for j in js:
                    last = nc.tensor.matmul(out[:, j, :], oT[:, i, j * P:(j + 1) * P], wo[:, i, :],
                                            start=first and j % 2 == 0, stop=last_head, skip_group_check=True)
                if CT - 1 in js:
                    last.then_inc(wo_done, 1)

            def head(c, k2, i, following=None, before=None, first=False):
                n = c * H + 2 * k2 + i
                scores(c, k2, i)
                if following:
                    project_qk(c, *following)
                ok_products(c, k2, i, [(og_ready, n), (enz_ready, n + 1)] if before else [(enz_ready, n + 1)])
                if before:
                    turn_o(c, *before)
                if following:
                    project_tokens(c, *following, 2, vb, v_done)
                if before:
                    output(c, *before, (0, 1), first=first)
                if following:
                    project_tokens(c, *following, 3, gb, g_done, then=(w_ready, n + 1))
                    turn_w(c, k2, i)
                    slots(c, *following, True)
                    if before:
                        output(c, *before, (2, 3), first=first)
                else:
                    pe.wait_ge(w_ready, n + 1)
                    output(c, *before, (2, 3), first=first)
                    turn_w(c, k2, i)
                w2_products(c, k2, i, 2 * (n + 2 if following else n + 1))
                if following:
                    slots(c, *following, False)
                    slot_sums(c, *following)
                o_products(c, k2, i, n + 2 if following else n + 1)

            pe.wait_ge(init, 2)
            with pe.Fori(0, CHUNKS) as c:
                pe.wait_ge(xn_ready, c)
                pe.wait_ge(w2_ready, c * H)
                pe_features(nc, sh.xn, sh.ident, (pair[:, 0, :], pair[:, 1, :]), xT_banked)
                pe.wait_ge(xT_ready, 2 * (c + 1))
                for in_ in const_in:
                    pe.wait_ge(in_, 16)
                for kc in range(KC):
                    last = nc.tensor.matmul(vb[0:R, :], ws1[:, kc, :], sh.xT[:, kc, :], start=kc == 0, stop=kc == KC - 1)
                last.then_inc(low_done, 1)
                project_qk(c, 0, 0)
                project_tokens(c, 0, 0, 3, gb, g_done)
                pe.wait_ge(low_ready, c + 1)
                project_tokens(c, 0, 0, 2, vb, v_done)
                slots(c, 0, 0, True)
                slots(c, 0, 0, False)
                slot_sums(c, 0, 0)
                head(c, 0, 0, following=(0, 1))
                head(c, 0, 1, following=(1, 0), before=(0, 0), first=True)
                with pe.Fori(1, HH - 1) as k2:
                    head(c, k2, 0, following=(k2, 1), before=(k2 - 1, 1))
                    head(c, k2, 1, following=(k2 + 1, 0), before=(k2, 0))
                head(c, HH - 1, 0, following=(HH - 1, 1), before=(HH - 2, 1))
                head(c, HH - 1, 1, before=(HH - 1, 0))
                pe.wait_ge(og_ready, (c + 1) * H)
                nc.tensor.matmul(pair[:, 0, 0:P], sh.ident[:, :], sh.ident[:, :], start=True, stop=True)
                turn_o(c, HH - 1, 1)
                output(c, HH - 1, 1, range(CT), last_head=True)

        @block.scalar
        def _(act):
            act.dma_start(rope[:, :, :], d["a1_rope"]).then_inc(const_in[1], 16)
            act.dma_start(masks[:, :, :], d["a1_masks"]).then_inc(const_in[2], 16)

            def take_qk(c, k2, i):
                n = c * H + 2 * k2 + i
                act.wait_ge(qk_ready, 2 * n)
                for a_ in range(2):
                    act.wait_ge(qk_cosed, 2 * n + a_ + 1)
                    nc.scalar.activation(swapped[0:64, a_, :], pair[64:P, a_, :], ACT.Copy)
                    nc.scalar.activation(swapped[64:P, a_, :], pair[0:64, a_, :], ACT.Copy).then_inc(qk_swapped, 1)

            def take_v(c, k2, i):
                n = c * H + 2 * k2 + i
                act.wait_ge(v_done, n + 1)
                nc.scalar.activation(v[:, i, :, :].rearrange("p j e -> p (j e)"), vb[:, :], ACT.Copy).then_inc(v_ready, 1)

            def tanh_g(c, k2, i):
                n = c * H + 2 * k2 + i
                act.wait_ge(g_done, n + 1)
                act.wait_ge(g_ready, n)
                nc.scalar.activation(tanh[:, :], gb[:, :], ACT.Tanh, scale=0.5).then_inc(tanh_ready, 1)

            def exp_slots(c, k2, i):
                n = c * H + 2 * k2 + i
                act.wait_ge(slot_clipped, n + 1)
                act.wait_ge(ok_done, n)
                nc.scalar.activation(es[:, :, :], slot_in[:, :, :], ACT.Exp).then_inc(es_ready, 1)
                act.wait_ge(slotT_clipped, n + 1)
                nc.scalar.activation(esT[:, i, :], slotT_in[:, :], ACT.Exp).then_inc(esT_ready, 1)

            def softmax(c, k2, i):
                n = c * H + 2 * k2 + i
                act.wait_ge(shifted, n + 1)
                nc.scalar.activation(exps[:, :, :], ok[:, :, :], ACT.Exp).then_inc(exps_done, 1)

            def take_wT(c, k2, i):
                n = c * H + 2 * k2 + i
                act.wait_ge(wT_done, n + 1)
                nc.scalar.activation(wT[:, :], wTb, ACT.Copy).then_inc(wT_ready, 1)

            def square_o(c, k2, i):
                n = c * H + 2 * k2 + i
                act.wait_ge(o_done, n + 1)
                act.wait_ge(ms_ready, n)
                for j in range(CT):
                    last = nc.scalar.activation(square[:, j, :], ob[:, j * DH:(j + 1) * DH], ACT.Square,
                                                accum_out=squares[:, j:j + 1])
                last.then_inc(squares_done, 1)

            def take_oT(c, k2, i):
                act.wait_ge(oT_done, c * H + 2 * k2 + i + 1)
                nc.scalar.activation(oT[:, i, :], oTb[:, :], ACT.Copy, scale=gn_half[:, 0:1]).then_inc(oT_ready, 1)

            def head(c, k2, i, following=None, before=None):
                if before:
                    square_o(c, *before)
                if following:
                    take_qk(c, *following)
                if before:
                    take_oT(c, *before)
                softmax(c, k2, i)
                if following:
                    take_v(c, *following)
                    tanh_g(c, *following)
                take_wT(c, k2, i)
                if following:
                    exp_slots(c, *following)

            act.wait_ge(init, 3)
            with act.Fori(0, CHUNKS) as c:
                for kc in range(KC):
                    act.wait_ge(xT_banked, 2 * c + kc + 1)
                    nc.scalar.activation(sh.xT[:, kc, :], pair[:, kc, :], ACT.Copy).then_inc(xT_ready, 1)
                act.wait_ge(low_done, c + 1)
                nc.scalar.activation(low[0:R, :], vb[0:R, :], ACT.Copy).then_inc(low_ready, 1)
                take_qk(c, 0, 0)
                tanh_g(c, 0, 0)
                take_v(c, 0, 0)
                exp_slots(c, 0, 0)
                head(c, 0, 0, following=(0, 1))
                head(c, 0, 1, following=(1, 0), before=(0, 0))
                with act.Fori(1, HH - 1) as k2:
                    head(c, k2, 0, following=(k2, 1), before=(k2 - 1, 1))
                    head(c, k2, 1, following=(k2 + 1, 0), before=(k2, 0))
                head(c, HH - 1, 0, following=(HH - 1, 1), before=(HH - 2, 1))
                head(c, HH - 1, 1, before=(HH - 1, 0))
                square_o(c, HH - 1, 1)
                take_oT(c, HH - 1, 1)

        @block.gpsimd
        def _(pool):
            pool.dma_start(gn[:, :], d["a1_gn"]).then_inc(gn_in, 16)
            nc.gpsimd.memset(low[:, :], 1.0).then_inc(init, 1)
            nc.gpsimd.memset(ones[:, :], 1.0).then_inc(init, 1)
            pool.wait_ge(gn_in, 16)
            nc.gpsimd.tensor_scalar(gn_half[:, :], gn[:, :], 0.5, 1.0, ALU.mult, ALU.mult).then_inc(init, 1)
            pool.wait_ge(const_in[1], 16)

            def rotate(c, n):
                for a_ in range(2):
                    pool.wait_ge(qk_swapped, 2 * n + a_ + 1)
                    for b in range(SEQS):
                        last = nc.gpsimd.tensor_tensor(swapped[:, a_, b * S:(b + 1) * S], swapped[:, a_, b * S:(b + 1) * S],
                                                       rope[:, 1, :], ALU.mult)
                    last.then_inc(qk_sined, 1)

            def rms_step(c, n):
                pool.wait_ge(ms_ready, n + 1)
                nc.gpsimd.tensor_tensor(rms[:, :], ms[:, :], sh.minus_half[:, 0:CT], ALU.pow).then_inc(rms_ready, 1)

            with pool.Fori(0, CHUNKS) as c:
                rotate(c, c * H)
                rotate(c, c * H + 1)
                with pool.Fori(0, H - 2) as h:
                    rms_step(c, c * H + h)
                    rotate(c, c * H + h + 2)
                rms_step(c, c * H + H - 2)
                rms_step(c, c * H + H - 1)
                pool_keep(nc, sh, pool, c, out_used, kept)
                pool_rstd(nc, sh, pool, c, var_ready, rstd_ready)

        @block.vector
        def _(dve):
            def both(v_):
                return v_.rearrange("p (a t) -> p a t", a=1).broadcast_to([P, SEQS, v_.shape[-1]])

            def wide(v_, n_):
                return v_.rearrange("p (j a) -> p j a", a=1).broadcast_to([P, CT, n_])

            def cos_qk(c, n):
                for a_, done in ((0, q_done), (1, k_done)):
                    dve.wait_ge(done, n + 1)
                    nc.vector.tensor_tensor(cosed[:, a_, :].rearrange("p (b t) -> p b t", b=SEQS),
                                            pair[:, a_, :].rearrange("p (b t) -> p b t", b=SEQS),
                                            both(rope[:, 0, :]), ALU.mult).then_inc(qk_cosed, 1)

            def sum_qk(c, n):
                for a_ in range(2):
                    dve.wait_ge(qk_cosed, 2 * n + a_ + 1)
                    dve.wait_ge(qk_sined, 2 * n + a_ + 1)
                    nc.vector.tensor_tensor(qk[:, a_, :], cosed[:, a_, :], swapped[:, a_, :], ALU.add).then_inc(qk_ready, 1)

            def take_g(c, n, i):
                dve.wait_ge(tanh_ready, n + 1)
                nc.vector.scalar_tensor_tensor(out=gate[:, i, :, :].rearrange("p j e -> p (j e)"), in0=tanh[:, :], scalar=1.0,
                                               in1=gb[:, :], op0=ALU.add, op1=ALU.mult).then_inc(g_ready, 1)

            def take_slots(c, n):
                dve.wait_ge(slot_done, n + 1)
                dve.wait_ge(es_ready, n)
                nc.vector.tensor_scalar(slot_in[:, :, :], slotb, CLAMP, -CLAMP, ALU.min, ALU.max).then_inc(slot_clipped, 1)

            def take_slotsT(c, n):
                dve.wait_ge(slotT_done, n + 1)
                dve.wait_ge(esT_ready, n)
                nc.vector.tensor_scalar(slotT_in[:, :], slotTb, CLAMP, -CLAMP, ALU.min, ALU.max).then_inc(slotT_clipped, 1)

            def take_sums(c, n):
                dve.wait_ge(sum_done, n + 1)
                nc.vector.reciprocal(enz[:, :, :], sumb).then_inc(enz_ready, 1)

            def masked(c, n, bank, dst, mask, done, ready):
                dve.wait_ge(done, n + 1)
                nc.vector.tensor_tensor(dst[:, :, :], bank[:, :, 0:CAUSAL], both(masks[:, mask, :]), ALU.mult).then_inc(ready, 1)

            HEAD_LINKS = 4

            def slot_softmax(c, n, chain):
                dve.wait_ge(ok_done, n + 1)
                dve.wait_ge(enz_ready, n + 1)
                nc.vector.tensor_tensor(ok[:, :, :], okb, enz[:, :, :], ALU.mult).then_inc(ok_read, 1)
                dve.wait_ge(ok_read, n + 1)
                chain.link(nc.vector.tensor_reduce(top[:, :], ok[:, :, :], AX, ALU.max))
                nc.vector.tensor_tensor(ok[:, :, :], ok[:, :, :], wide(top[:, :], M), ALU.subtract).then_inc(shifted, 1)
                dve.wait_ge(exps_done, n + 1)
                chain.link(nc.vector.tensor_reduce(total[:, :], exps[:, :, :], AX, ALU.add))
                chain.link(nc.vector.reciprocal(inv[:, :], total[:, :]))
                chain.link(nc.vector.tensor_tensor(exps[:, :, :], exps[:, :, :], enz[:, :, :], ALU.mult))
                nc.vector.tensor_tensor(slot_w[:, :, :], exps[:, :, :], wide(inv[:, :], M), ALU.mult).then_inc(w_ready, 1)

            def mean_square(c, n):
                dve.wait_ge(squares_done, n + 1)
                nc.vector.tensor_scalar(ms[:, :], squares[:, :], 1.0 / DH, EPS, ALU.mult, ALU.add).then_inc(ms_ready, 1)

            def gate_o(c, n, i):
                dve.wait_ge(rms_ready, n + 1)
                dve.wait_ge(oT_done, n)
                for j in range(CT):
                    last = nc.vector.scalar_tensor_tensor(out=og[:, j, :], in0=ob[:, j * DH:(j + 1) * DH],
                                                          scalar=rms[:, j:j + 1], in1=gate[:, i, j, :],
                                                          op0=ALU.mult, op1=ALU.mult)
                last.then_inc(og_ready, 1)

            def head(c, h, i, following=True, before=True):
                n = c * H + h
                chain = Chain(dve, own, c * LINKS + h * HEAD_LINKS, HEAD_LINKS)
                masked(c, n, ab, a, 0, a_done, a_ready)
                if before:
                    mean_square(c, n - 1)
                    gate_o(c, n - 1, 1 - i)
                if following:
                    cos_qk(c, n + 1)
                slot_softmax(c, n, chain)
                if following:
                    sum_qk(c, n + 1)
                    if before:
                        dve.wait_ge(og_ready, n)
                    take_g(c, n + 1, 1 - i)
                    take_slots(c, n + 1)
                masked(c, n, pair, w2, 1, w2_done, w2_ready)
                if following:
                    take_slotsT(c, n + 1)
                    take_sums(c, n + 1)
                chain.done()

            LINKS = H * HEAD_LINKS + STATS_LINKS
            for in_ in const_in:
                dve.wait_ge(in_, 16)
            with dve.Fori(0, CHUNKS) as c:
                cos_qk(c, c * H)
                sum_qk(c, c * H)
                take_g(c, c * H, 0)
                take_slots(c, c * H)
                take_slotsT(c, c * H)
                take_sums(c, c * H)
                head(c, 0, 0, before=False)
                head(c, 1, 1)
                with dve.Fori(1, HH - 1) as k2:
                    head(c, 2 * k2, 0)
                    head(c, 2 * k2 + 1, 1)
                head(c, H - 2, 0)
                head(c, H - 1, 1, following=False)
                mean_square(c, c * H + H - 1)
                gate_o(c, c * H + H - 1, 1)
                chain = Chain(dve, own, c * LINKS + H * HEAD_LINKS, STATS_LINKS)
                dve_normalise(nc, sh, c + 1, xn_ready)
                dve.wait_ge(wo_done, (c + 1) * H)
                dve_add_residual(nc, sh, dve, c, out, out_used, kept)
                dve_stats(nc, sh, dve, c, sh.fresh, chain, var_ready, rstd_ready)
                chain.done()
            dve_first_normalised(nc, sh, dve, xn_ready, kept, CHUNKS)


def ssm_block(nc, sh):
    d = sh.dram
    NS, G, RN = 128, 4, 32
    SLOTS = 4
    EPS, FAR, LEAST = 1e-6, 1e25, 1e-22
    s = lambda name: sh.sem(f"ss_{name}")
    w_in = [s(f"w_in{i}") for i in range(7)]
    a_ready, bias_ready = s("a_ready"), s("bias_ready")
    xn_ready, sq_done, ms_ready, r_ready, normed = s("xn_ready"), s("sq_done"), s("ms_ready"), s("r_ready"), s("normed")
    turned, xT_ready, hsT_ready = s("turned"), s("xT_ready"), s("hsT_ready")
    select_done, mask_ready, xg_ready = s("select_done"), s("mask_ready"), s("xg_ready")
    proj_done, delta_ready, dt_done = s("proj_done"), s("delta_ready"), s("dt_done")
    dt_neg, dt_exp, dt_ln, dt_ready, u_ready = s("dt_neg"), s("dt_exp"), s("dt_ln"), s("dt_ready"), s("u_ready")
    split_ready = s("split_ready")
    packed_in = [s(f"packed_in{i}") for i in range(6)]
    rows_done, c_ready, decay_ready = s("rows_done"), s("c_ready"), s("decay_ready")
    dbu_ready, state_ready, hc_ready, added = s("dbu_ready"), s("state_ready"), s("hc_ready"), s("added")
    y_ready, proj_out, out_used, kept = s("y_ready"), s("proj_out"), s("out_used"), s("kept")
    own, var_ready, rstd_ready = s("own"), s("var"), s("rstd")

    with ExitStack() as ctx:
        sb = lambda name, shape, dt=F32: ctx.enter_context(nc.sbuf_tensor(f"ss_{name}", shape, dt))
        ps = lambda name, banks: ctx.enter_context(nc.psum_tensor(f"ss_{name}", [P, banks, N], F32))
        w_sel = sb("w_sel", [P, KC, D])
        w_xp = sb("w_xp", [P, KC, 3 * P])
        w_dt = sb("w_dt", [P, D])
        w_out = sb("w_out", [P, KC, D])
        onehot = sb("onehot", [3 * RN, RN, P], BF16)
        cols = sb("cols", [P, KC, 5])
        a_log = sb("a_log", [P, KC, NS])
        a_neg = sb("a_neg", [P, KC, NS])
        gated_bias = sb("gated_bias", [P, KC])
        square = sb("square", [P, CT, D])
        squares, ms, rr = sb("squares", [P, CT]), sb("ms", [P, CT]), sb("rr", [P, CT])
        normal = sb("normal", [P, CT, D])
        hsT = sb("hsT", [P, KC, N])
        mask = sb("mask", [P, KC, N])
        xg = sb("xg", [P, KC, N])
        delta = sb("delta", [P, N])
        z, e, w1, low = sb("z", [P, KC, N]), sb("e", [P, KC, N]), sb("w1", [P, KC, N]), sb("low", [P, KC, N])
        dt = sb("dt", [P, KC, N])
        u = sb("u", [P, KC, N])
        part = sb("part", [P, 2, 3, N], BF16)
        rest = sb("rest", [P, 2, N])
        packed = sb("packed", [3 * RN, 2, G, N], BF16)
        dbu = sb("dbu", [P, SLOTS, KC, N])
        decay = sb("decay", [P, 2, KC, N])
        crow = sb("crow", [P, 2, N])
        state = sb("state", [P, 2, KC, N])
        hc = sb("hc", [P, 2, KC, N])
        yT = sb("yT", [P, KC, N])
        rows = ps("rows", 4)
        spare = ps("spare", 2)
        y = ps("y", 2)
        out = spare[:, :, :].rearrange("p a t -> p (a t)").rearrange("p (j e) -> p j e", j=CT)
        flat = lambda t: t.rearrange("p k t -> p (k t)")
        block = ctx.enter_context(nc.Block())

        @block.sync
        def _(sp):
            for n_, (t, name) in enumerate(((cols, "ss_cols"), (a_log, "ss_a_log"), (w_sel, "ss_w_sel"), (w_xp, "ss_w_xp"))):
                sp.dma_start(t[:], d[name]).then_inc(w_in[n_], 16)
            with sp.Fori(0, CHUNKS) as c:
                for bc in range(2):
                    sp.wait_ge(split_ready, 2 * c + bc + 1)
                    for p in range(3):
                        for g in range(G):
                            sp.dma_start(packed[RN * p:RN * (p + 1), bc, g, :],
                                         part[RN * g:RN * (g + 1), bc, p, :]).then_inc(packed_in[3 * bc + p], 16)

        @block.tensor
        def _(pe):
            pe.sem_inc(added, 2)
            for in_ in w_in:
                pe.wait_ge(in_, 16)
            with pe.Fori(0, CHUNKS) as c:
                pe.wait_ge(normed, c + 1)
                pe_features(nc, normal, sh.ident, (rows[:, 0, :], rows[:, 1, :]), turned)
                pe.wait_ge(kept, c)
                pe_features(nc, sh.xn, sh.ident, (spare[:, 0, :], spare[:, 1, :]), turned)
                pe.wait_ge(xT_ready, c + 1)
                for m in range(KC):
                    for kc in range(KC):
                        last = nc.tensor.matmul(rows[:, 2 + m, :], w_sel[:, kc, m * P:(m + 1) * P], sh.xT[:, kc, :],
                                                start=kc == 0, stop=kc == KC - 1)
                last.then_inc(select_done, 1)
                pe.wait_ge(xg_ready, c + 1)
                pe.wait_ge(hsT_ready, c + 1)
                for m, bank in enumerate((spare[:, 0, :], rows[:, 0, :], rows[:, 1, :])):
                    for kc in range(KC):
                        last = nc.tensor.matmul(bank, w_xp[:, kc, m * P:(m + 1) * P], xg[:, kc, :],
                                                start=kc == 0, stop=kc == KC - 1)
                    last.then_inc(proj_done, 1)
                pe.wait_ge(delta_ready, c + 1)
                for m in range(KC):
                    last = nc.tensor.matmul(rows[:, 2 + m, :], w_dt[:, m * P:(m + 1) * P], delta[:, :], start=True, stop=True)
                last.then_inc(dt_done, 1)
                pe.wait_ge(u_ready, c + 1)
                for in_ in packed_in:
                    pe.wait_ge(in_, 16 * G * (c + 1))

                def spread(g, k, i, first=False):
                    if not first:
                        pe.wait_ge(c_ready, c * NS + RN * g + 2 * k + i - 1)
                        pe.wait_ge(dbu_ready, c * NS + RN * g + 2 * k + i - 1)
                    for bc in range(2):
                        last = nc.tensor.matmul(rows[:, 2 * bc + i, :], onehot[:, bass.ds(2 * k + i, 1), :],
                                                packed[:, bc, bass.ds(g, 1), :], start=True, stop=True)
                    last.then_inc(rows_done, 1)

                def add(n, i, first=False, final=False):
                    pe.wait_ge(hc_ready, c * NS + n + 3)
                    if first:
                        pe.wait_ge(y_ready, c)
                    for m in range(KC):
                        last = nc.tensor.matmul(y[:, m, :], sh.ident[:, :], hc[:, i, m, :], start=first, stop=final)
                    last.then_inc(added, 1)

                spread(0, 0, 0, first=True)
                spread(0, 0, 1, first=True)
                spread(0, 1, 0)
                spread(0, 1, 1)
                add(0, 0, first=True)
                with pe.Fori(2, RN // 2) as k:
                    for i in range(2):
                        spread(0, k, i)
                        add(2 * k + i - 3, 1 - i)
                with pe.Fori(1, G) as g:
                    with pe.Fori(0, RN // 2) as k:
                        for i in range(2):
                            spread(g, k, i)
                            add(RN * g + 2 * k + i - 3, 1 - i)
                add(NS - 3, 1)
                add(NS - 2, 0)
                add(NS - 1, 1, final=True)
                pe.wait_ge(y_ready, c + 1)
                for j in range(CT):
                    for kc in range(KC):
                        last = nc.tensor.matmul(out[:, j, :], yT[:, kc, j * P:(j + 1) * P], w_out[:, kc, :],
                                                start=kc == 0, stop=kc == KC - 1, skip_group_check=True)
                last.then_inc(proj_out, 1)

        @block.scalar
        def _(act):
            for n_, (t, name) in enumerate(((onehot, "ss_onehot"), (w_dt, "ss_w_dt"), (w_out, "ss_w_out"))):
                act.dma_start(t[:], d[name]).then_inc(w_in[4 + n_], 16)
            act.wait_ge(w_in[1], 16)
            nc.scalar.activation(flat(a_neg[:, :, :]), flat(a_log[:, :, :]), ACT.Exp).then_inc(a_ready, 1)
            act.wait_ge(a_ready, 2)
            act.wait_ge(bias_ready, 1)
            with act.Fori(0, CHUNKS) as c:
                act.wait_ge(xn_ready, c + 1)
                act.wait_ge(ms_ready, c)
                for j in range(CT):
                    last = nc.scalar.activation(square[:, j, :], sh.xn[:, j, :], ACT.Square, accum_out=squares[:, j:j + 1])
                last.then_inc(sq_done, 1)
                act.wait_ge(turned, 4 * c + 2)
                for kc in range(KC):
                    last = nc.scalar.activation(sh.xT[:, kc, :], rows[:, kc, :], ACT.Copy, scale=cols[:, kc, 0:1])
                last.then_inc(xT_ready, 1)
                act.wait_ge(select_done, c + 1)
                for m in range(KC):
                    last = nc.scalar.activation(mask[:, m, :], rows[:, 2 + m, :], ACT.Sigmoid, scale=cols[:, m, 2:3],
                                                bias=gated_bias[:, m:m + 1])
                last.then_inc(mask_ready, 1)
                act.wait_ge(proj_done, 3 * c + 1)
                nc.scalar.activation(delta[:, :], spare[:, 0, :], ACT.Copy).then_inc(delta_ready, 1)
                act.wait_ge(dt_neg, c + 1)
                nc.scalar.activation(flat(e[:, :, :]), flat(e[:, :, :]), ACT.Exp).then_inc(dt_exp, 1)
                act.wait_ge(dt_ln, 3 * c + 1)
                nc.scalar.activation(flat(low[:, :, :]), flat(w1[:, :, :]), ACT.Ln).then_inc(dt_ln, 1)
                act.wait_ge(dt_ln, 3 * c + 2)
                nc.scalar.activation(flat(mask[:, :, :]), flat(low[:, :, :]), ACT.Exp, scale=-1.0).then_inc(dt_ln, 1)
                act.wait_ge(dt_ready, c + 1)

                def row(k, i, first=False):
                    n = c * NS + 2 * k + i
                    if not first:
                        act.wait_ge(state_ready, n - 1)
                    for m in range(KC):
                        last = nc.scalar.activation(decay[:, i, m, :], dt[:, m, :], ACT.Exp,
                                                    scale=a_neg[:, m, bass.ds(2 * k + i, 1)])
                    last.then_inc(decay_ready, 1)
                    act.wait_ge(hc_ready, n + 1)
                    act.wait_ge(rows_done, n + 1)
                    nc.scalar.activation(crow[:, i, :], rows[:, 2 + i, :], ACT.Copy).then_inc(c_ready, 1)

                row(0, 0, first=True)
                row(0, 1, first=True)
                with act.Fori(1, NS // 2) as k:
                    for i in range(2):
                        row(k, i)

        @block.gpsimd
        def _(pool):
            pool.sem_inc(hc_ready, 2)
            with pool.Fori(0, CHUNKS) as c:
                pool.wait_ge(ms_ready, c + 1)
                nc.gpsimd.tensor_tensor(rr[:, :], ms[:, :], sh.minus_half[:, 0:CT], ALU.pow).then_inc(r_ready, 1)
                with pool.Fori(0, NS // 2) as k:
                    for i in range(2):
                        n = c * NS + 2 * k + i
                        pool.wait_ge(state_ready, n + 1)
                        pool.wait_ge(c_ready, n + 1)
                        pool.wait_ge(added, n + 1)
                        nc.gpsimd.tensor_tensor(hc[:, i, :, :], state[:, i, :, :],
                                                crow[:, i, :].rearrange("p (a t) -> p a t", a=1).broadcast_to([P, KC, N]),
                                                ALU.mult).then_inc(hc_ready, 1)
                pool_keep(nc, sh, pool, c, out_used, kept)
                pool_rstd(nc, sh, pool, c, var_ready, rstd_ready)

        @block.vector
        def _(dve):
            LINKS = 6 + 2 * 3 + STATS_LINKS
            dve.wait_ge(a_ready, 1)
            nc.vector.tensor_scalar(flat(a_neg[:, :, :]), flat(a_neg[:, :, :]), LEAST, -1.0, ALU.max,
                                    ALU.mult).then_inc(a_ready, 1)
            dve.wait_ge(w_in[0], 16)
            nc.vector.tensor_tensor(gated_bias[:, :], cols[:, :, 1], cols[:, :, 2], ALU.mult).then_inc(bias_ready, 1)
            with dve.Fori(0, CHUNKS) as c:
                chain = Chain(dve, own, c * LINKS, LINKS)
                link = chain.link
                dve_normalise(nc, sh, c, xn_ready)
                dve.wait_ge(sq_done, c + 1)
                nc.vector.tensor_scalar(ms[:, :], squares[:, :], 1.0 / D, EPS, ALU.mult, ALU.add).then_inc(ms_ready, 1)
                dve.wait_ge(r_ready, c + 1)
                for j in range(CT):
                    last = nc.vector.tensor_scalar(normal[:, j, :], sh.xn[:, j, :], rr[:, j:j + 1], None, ALU.mult)
                last.then_inc(normed, 1)
                dve.wait_ge(turned, 4 * c + 4)
                nc.vector.tensor_copy(flat(hsT[:, :, :]), flat(spare[:, :, :])).then_inc(hsT_ready, 1)
                dve.wait_ge(mask_ready, c + 1)
                nc.vector.tensor_tensor(flat(xg[:, :, :]), flat(mask[:, :, :]), flat(sh.xT[:, :, :]), ALU.mult).then_inc(xg_ready, 1)
                for bc in range(2):
                    dve.wait_ge(proj_done, 3 * c + 2 + bc)
                    link(nc.vector.tensor_copy(part[:, bc, 0, :], rows[:, bc, :]))
                    link(nc.vector.tensor_tensor(rest[:, bc, :], rows[:, bc, :], part[:, bc, 0, :], ALU.subtract))
                    link(nc.vector.tensor_copy(part[:, bc, 1, :], rest[:, bc, :]))
                    nc.vector.tensor_tensor(part[:, bc, 2, :], rest[:, bc, :], part[:, bc, 1, :],
                                            ALU.subtract).then_inc(split_ready, 1)
                dve.wait_ge(dt_done, c + 1)
                for m in range(KC):
                    chain.mark(nc.vector.tensor_scalar(z[:, m, :], rows[:, 2 + m, :], cols[:, m, 3:4], None, ALU.add))
                chain.wait()
                nc.vector.scalar_tensor_tensor(out=flat(e[:, :, :]), in0=flat(z[:, :, :]), scalar=-1.0,
                                               in1=flat(z[:, :, :]), op0=ALU.mult, op1=ALU.min).then_inc(dt_neg, 1)
                dve.wait_ge(dt_exp, c + 1)
                nc.vector.tensor_scalar(flat(w1[:, :, :]), flat(e[:, :, :]), 1.0, None, ALU.add).then_inc(dt_ln, 1)
                dve.wait_ge(dt_ln, 3 * c + 1)
                link(nc.vector.scalar_tensor_tensor(out=flat(e[:, :, :]), in0=flat(w1[:, :, :]), scalar=-1.0,
                                                    in1=flat(e[:, :, :]), op0=ALU.add, op1=ALU.subtract))
                dve.wait_ge(dt_ln, 3 * c + 3)
                link(nc.vector.tensor_tensor(flat(e[:, :, :]), flat(e[:, :, :]), flat(mask[:, :, :]), ALU.mult))
                link(nc.vector.tensor_tensor(flat(low[:, :, :]), flat(low[:, :, :]), flat(e[:, :, :]), ALU.subtract))
                link(nc.vector.scalar_tensor_tensor(out=flat(dt[:, :, :]), in0=flat(z[:, :, :]), scalar=0.0,
                                                    in1=flat(low[:, :, :]), op0=ALU.max, op1=ALU.add))
                nc.vector.tensor_tensor(flat(u[:, :, :]), flat(dt[:, :, :]), flat(xg[:, :, :]), ALU.mult).then_inc(u_ready, 1)
                dve.wait_ge(u_ready, c + 1)
                nc.vector.memset(flat(dt[:, :, :]).rearrange("p (a t) -> p a t", t=S)[:, :, 0:1], FAR).then_inc(dt_ready, 1)

                def product(m_, j, free=False):
                    if not free:
                        dve.wait_ge(state_ready, c * NS + m_ - SLOTS + 1)
                    dve.wait_ge(rows_done, c * NS + m_ + 1)
                    nc.vector.tensor_tensor(dbu[:, j, :, :], u[:, :, :],
                                            rows[:, j % 2, :].rearrange("p (a t) -> p a t", a=1).broadcast_to([P, KC, N]),
                                            ALU.mult).then_inc(dbu_ready, 1)

                def scan(m_, j):
                    n, i = c * NS + m_, j % 2
                    dve.wait_ge(decay_ready, n + 1)
                    dve.wait_ge(hc_ready, n + 1)
                    dve.wait_ge(dbu_ready, n + 1)
                    nc.vector.tensor_tensor_scan(flat(state[:, i, :, :]), flat(decay[:, i, :, :]), flat(dbu[:, j, :, :]),
                                                 0.0, ALU.mult, ALU.add).then_inc(state_ready, 1)

                product(0, 0, free=True)
                for j in range(SLOTS):
                    product(j + 1, (j + 1) % SLOTS, free=j + 1 < SLOTS)
                    scan(j, j)
                with dve.Fori(1, NS // SLOTS - 1) as k:
                    for j in range(SLOTS):
                        product(SLOTS * k + j + 1, (j + 1) % SLOTS)
                        scan(SLOTS * k + j, j)
                for j in range(SLOTS):
                    if j < SLOTS - 1:
                        product(NS - SLOTS + j + 1, j + 1)
                    scan(NS - SLOTS + j, j)
                dve.wait_ge(added, (c + 1) * NS + 2)
                for m in range(KC):
                    last = nc.vector.scalar_tensor_tensor(out=yT[:, m, :], in0=hsT[:, m, :], scalar=cols[:, m, 4:5],
                                                          in1=y[:, m, :], op0=ALU.mult, op1=ALU.add)
                last.then_inc(y_ready, 1)
                dve.wait_ge(proj_out, c + 1)
                dve_add_residual(nc, sh, dve, c, out, out_used, kept)
                dve_stats(nc, sh, dve, c, sh.fresh, chain, var_ready, rstd_ready)
                chain.done()
            dve_first_normalised(nc, sh, dve, xn_ready, kept, CHUNKS)


def alibi_columns(heads):
    slopes = np.array([2.0 ** (-8.0 * (h + 1) / heads) for h in range(heads)], np.float32)
    key = np.concatenate([np.arange(P), np.arange(S)])
    query = np.arange(P)[:, None] + np.concatenate([np.zeros(P), np.full(S, P)])[None, :]
    bias = slopes[None, :, None] * key.astype(np.float32)[None, None, :]
    return np.where((key[None, :] > query)[:, None, :], np.float32(-1e30), bias).astype(np.float32)


def head_rows(w, heads):
    return w.reshape(heads, P, KC, P).transpose(0, 3, 2, 1).reshape(heads, P, KC * P)


def head_out(w, heads):
    return w.reshape(D, heads, P).transpose(1, 2, 0)


def pack_rest(i):
    out = {}
    a = {k[10:]: v for k, v in i.items() if k.startswith("L0_attn_a_W")}
    out["a0_w"] = np.concatenate([head_rows(a["Wq"], 16), head_rows(a["Wk"], 16), head_rows(a["Wv"], 16),
                                  head_out(a["Wo"], 16)], 2)
    out["a0_bias"] = alibi_columns(16)
    g = {k[10:]: v for k, v in i.items() if k.startswith("L1_attn_a_")}
    slot = np.zeros((16, P, 64), np.float32)
    slot[:, 0:16] = g["Ws2"].reshape(16, 64, 16).transpose(0, 2, 1)
    slot[:, 16] = g["bs2"].reshape(16, 64)
    out["a1_w"] = np.concatenate([head_rows(g["Wq"], 16), head_rows(g["Wk"], 16), head_rows(g["Wv"], 16),
                                  head_rows(g["Wg"], 16), slot, head_out(g["Wo"], 16)], 2)
    out["a1_ws1"] = rows_in(g["Ws1"].T)
    out["a1_rope"] = rope_table(P)
    out["a1_masks"] = np.stack([causal_columns() * np.float32(P ** -0.5), causal_columns()], 1)
    r = {k[10:]: v for k, v in i.items() if k.startswith("L0_attn_b_")}
    out["rt_wqkvg"] = np.stack([rows_in(r[k]) for k in ("Wq", "Wk", "Wv", "Wg")], 1)
    out["rt_wo"] = rows_in(r["Wo"])
    halves = [np.pad(w, ((0, 0), (0, 32))) for w in (r["W_gate"][:, :352], r["W_gate"][:, 352:])]
    out["rt_w_gate"] = np.stack([rows_in(w) for w in halves], 1)
    out["rt_w_down"] = np.pad(r["W_down"], ((0, 32), (0, 0))).reshape(3, P, D).transpose(1, 0, 2)
    columns = np.concatenate([r["conv_wq"], r["conv_wk"], r["conv_wv"], r["attn_norm_w"][:, None],
                              r["mlp_norm_w"][:, None]], 1)
    out["rt_cols"] = rows_in(columns)
    out["rt_gnw"] = np.tile(r["gnorm_w"], (P, 8))
    out["rt_swap"] = np.kron(np.eye(4), np.roll(np.eye(32), 16, 1)).astype(np.float32)
    out["rt_rope"] = rope_table(32)
    out["rt_decay"] = decay_columns(8, 32)
    m = {k[10:]: v for k, v in i.items() if k.startswith("L1_attn_b_")}
    out["ss_cols"] = rows_in(np.stack([m["norm_w"], m["select_proj_b"], m["select_gate"], m["dt_proj_b"], m["D_param"]], 1))
    out["ss_a_log"] = rows_in(m["A_log"])
    out["ss_w_sel"] = rows_in(m["select_proj_w"].T)
    out["ss_w_xp"] = rows_in(m["x_proj_w"].T)
    out["ss_w_dt"] = m["dt_proj_w"].T
    out["ss_w_out"] = rows_in(m["out_proj_w"].T)
    hot = np.tile(np.eye(32, dtype=np.float32), (3, 1))
    out["ss_onehot"] = np.broadcast_to(hot[:, :, None], (96, 32, P)).astype(mybir.dt.np(BF16))
    out["a1_gn"] = g["g_norm_weight"].reshape(P, 1)
    return out


def rope_table(width):
    half = width // 2
    freq = 1.0 / 10000.0 ** (np.arange(0, width, 2) / width)
    angle = (np.arange(S)[None, :].astype(np.float32) * freq.astype(np.float32)[:, None]).astype(np.float64)
    cos, sin = np.cos(angle), np.sin(angle)
    one = np.stack([np.concatenate([cos, cos]), np.concatenate([-sin, sin])], 1)
    return np.tile(one, (P // width, 1, 1)).astype(np.float32)


def causal_columns():
    key, query = np.arange(P)[:, None], np.arange(P)[None, :]
    tri = (query >= key).astype(np.float32)
    return np.concatenate([tri, np.ones((P, P), np.float32), tri], 1)


def decay_columns(heads, width):
    gamma = 1.0 - 2.0 ** (-5.0 - np.arange(heads))
    ahead = np.arange(S)[None, :] - np.arange(P)[:, None]
    table = gamma[None, :, None] ** np.maximum(ahead, 0)[:, None, :] * width ** -0.5
    return np.where((ahead >= 0)[:, None, :], table, 0).astype(np.float32)


def pack_ffn(gates, ups, downs):
    def cat(parts, axis):
        a = np.concatenate(parts, axis)
        short = -a.shape[axis] % P
        return np.pad(a, [(0, short if ax == axis else 0) for ax in range(2)])
    g, u, d = cat(gates, 1), cat(ups, 1), cat(downs, 0)
    lay = lambda w: w.reshape(KC, P, -1, P).transpose(2, 1, 0, 3).reshape(-1, P, KC * P)
    return np.concatenate([lay(g), lay(u), d.reshape(-1, P, D)], 2)


def rows_in(w):
    return w.reshape(KC, P, -1).transpose(1, 0, 2)


def one_hot_parts(experts, width, shared):
    owner = np.concatenate([np.repeat(np.arange(experts), width), np.full(shared, experts)])
    hot = np.zeros((P, -(-owner.size // P) * P), np.float32)
    for part in range(3):
        hot[part * (experts + 1) + owner, np.arange(owner.size)] = 1
    return hot.astype(mybir.dt.np(BF16))


def pack(i):
    i = {k: np.asarray(v) for k, v in i.items()}
    f0 = {k[7:]: v for k, v in i.items() if k.startswith("L0_ffn_")}
    f1 = {k[7:]: v for k, v in i.items() if k.startswith("L1_ffn_")}
    out = {"x": i["L0_attn_a_resid_pre"]}
    out["f0_w"] = pack_ffn([*f0["w_gate"], f0["sh_gate"]], [*f0["w_up"], f0["sh_up"]],
                           [*f0["w_down"], f0["sh_down"]])
    out["f0_router"] = rows_in(np.concatenate([f0["router_w"].T, f0["sh_gate_w"]], 1))
    out["f0_hot"] = one_hot_parts(16, 176, 704)
    t = lambda ws: [w.T for w in ws]
    out["f1_w"] = pack_ffn(t([*f1["w1"], f1["sw1"]]), t([*f1["w3"], f1["sw3"]]), t([*f1["w2"], f1["sw2"]]))
    out["f1_router"] = rows_in(np.concatenate([f1["gate_w"].T, np.zeros((D, 1), np.float32)], 1))
    out["f1_hot"] = one_hot_parts(8, 176, 352)
    out.update(pack_rest(i))
    return {k: np.ascontiguousarray(v) for k, v in out.items()}


def program(nc, d, blocks):
    with ExitStack() as ctx:
        sh = Shared(nc, ctx, d)
        load_block(nc, sh)
        sh.end_block()
        for n in blocks:
            if n == 0:
                l0_attention_block(nc, sh)
            if n in (1, 3):
                ffn_block(nc, sh, f"f0{n}", d["f0_w"], d["f0_router"], d["f0_hot"], 16, 4, 28, True)
            if n == 2:
                retention_block(nc, sh)
            if n == 4:
                l1_attention_block(nc, sh)
            if n in (5, 7):
                ffn_block(nc, sh, f"f1{n}", d["f1_w"], d["f1_router"], d["f1_hot"], 8, 2, 14, False)
            if n == 6:
                ssm_block(nc, sh)
            sh.end_block()
        store_block(nc, sh)


def kernel(**inputs):
    import concourse.bacc as bacc
    from concourse.bass_utils import run_bass_kernel_spmd

    arrays = pack(inputs)
    nc = bacc.Bacc("TRN2", target_bir_lowering=False, num_devices=1)
    d = {k: nc.dram_tensor(f"in_{k}", a.shape, mybir.dt.from_np(a.dtype), kind="ExternalInput").ap() for k, a in arrays.items()}
    d["out"] = nc.dram_tensor("out", (B, S, D), F32, kind="ExternalOutput").ap()
    program(nc, d, range(8))
    r = run_bass_kernel_spmd(nc, [{f"in_{k}": a for k, a in arrays.items()}], core_ids=[0])
    return r.results[0]["out"]
```

```python
from contextlib import ExitStack

import numpy as np

import concourse.bass as bass
from concourse import mybir

F32 = mybir.dt.float32
BF16 = mybir.dt.bfloat16
F32R = mybir.dt.float32r
ALU = mybir.AluOpType
ACT = mybir.ActivationFunctionType
AX = mybir.AxisListType.X

P = 128
B, S, D = 8, 256, 256
KC = D // P
TILES = B * S // P
CHUNKS = 4
CT = TILES // CHUNKS
N = CT * P
SEQS = N // S
LN_EPS = 1e-5
CAUSAL = S + P


class Chain:

    def __init__(self, eng, sem, base, per):
        self.eng, self.sem, self.base, self.per, self.k = eng, sem, base, per, 0

    def mark(self, ins):
        ins.then_inc(self.sem, 1)
        self.k += 1

    def wait(self, carrier=None):
        self.eng.wait_ge(self.sem, self.base + self.k)
        if carrier is not None:
            self.eng.memset(carrier, 0.0)

    def link(self, ins, carrier=None):
        self.mark(ins)
        self.wait(carrier)

    def done(self):
        assert self.k == self.per, (self.k, self.per)


class Shared:

    def __init__(self, nc, ctx, dram):
        self.nc, self.ctx, self.dram = nc, ctx, dram
        sb = lambda name, shape, dt=F32: ctx.enter_context(nc.sbuf_tensor(name, shape, dt))
        self.x = sb("x", [P, TILES + CT, D])
        self.fresh = sb("fresh", [P, CT, D])
        self.moments = sb("moments", [P, CT, 2])
        self.mean = sb("mean", [P, TILES + CT])
        self.rstd = sb("rstd", [P, TILES + CT])
        self.bn = sb("bn", [P, CT, 6])
        self.var_eps = sb("var_eps", [P, CT])
        self.minus_half = sb("minus_half", [P, 64])
        self.ident = sb("ident", [P, P])
        self.identb = sb("identb", [P, P], BF16)
        self.xn = sb("xn", [P, CT, D])
        self.xT = sb("xT", [P, KC, N])
        self.scratch = sb("scratch", [P, 1])
        self.pool_scratch = sb("pool_scratch", [P, 2])

        self.sems = []

    def sem(self, name):
        self.sems.append(self.nc.alloc_semaphore(name=name))
        return self.sems[-1]

    def end_block(self):
        self.nc.clear_and_free_semaphores(self.sems)
        self.sems = []
        self.nc.all_engine_barrier()


def tiles(c):
    return bass.ds(c * CT, CT)


def dve_stats(nc, sh, dve, c, new, chain, var_ready, rstd_ready, kept=None):
    for j in range(CT):
        chain.mark(nc.vector.bn_stats(sh.bn[:, j, :], new[:, j, :]))
    chain.wait(carrier=sh.scratch[:, :])
    for j in range(CT):
        chain.mark(nc.vector.bn_aggr(sh.moments[:, j, :], sh.bn[:, j, :]))
    chain.wait(carrier=sh.scratch[:, :])
    chain.mark(nc.vector.tensor_copy(sh.mean[:, bass.ds(c * CT, CT)], sh.moments[:, :, 0]))
    dve.wait_ge(rstd_ready, c)
    nc.vector.tensor_scalar(sh.var_eps[:, :], sh.moments[:, :, 1], LN_EPS, None, ALU.add).then_inc(var_ready, 1)
    if kept:
        nc.vector.tensor_copy(sh.x[:, tiles(c), :], sh.fresh[:, :, :]).then_inc(kept, 1)


STATS_LINKS = 2 * CT + 1


def pool_rstd(nc, sh, pool, c, var_ready, rstd_ready):
    pool.wait_ge(var_ready, c + 1)
    nc.gpsimd.tensor_tensor(sh.rstd[:, bass.ds(c * CT, CT)], sh.var_eps[:, :],
                            sh.minus_half[:, 0:CT], ALU.pow).then_inc(rstd_ready, 1)


def dve_normalise(nc, sh, c, xn_ready):
    for j in range(CT):
        last = nc.vector.tensor_scalar(sh.xn[:, j, :], sh.x[:, bass.ds(c * CT + j, 1), :],
                                       sh.mean[:, bass.ds(c * CT + j, 1)],
                                       sh.rstd[:, bass.ds(c * CT + j, 1)],
                                       ALU.subtract, ALU.mult)
    last.then_inc(xn_ready, 1)


def dve_first_normalised(nc, sh, dve, xn_ready, kept=None, written=None):
    if written:
        dve.wait_ge(xn_ready, written)
    if kept:
        dve.wait_ge(kept, 1)
    dve_normalise(nc, sh, 0, xn_ready)


def pe_three(nc, bank, highs, lows, start, stop, **kw):
    nc.tensor.matmul(bank, highs[0], highs[1], start=start, stop=False, **kw)
    nc.tensor.matmul(bank, highs[0], lows[1], start=False, stop=False, **kw)
    return nc.tensor.matmul(bank, lows[0], highs[1], start=False, stop=stop, **kw)


def pool_low(nc, value, high, low):
    return nc.gpsimd.tensor_tensor(low, value, high.bitcast(F32), ALU.subtract)


def pe_features(nc, src, ident, banks, done):
    for kc in range(KC):
        for j in range(CT):
            last = nc.tensor.transpose(banks[kc][:, j * P:(j + 1) * P],
                                       src[:, j, kc * P:(kc + 1) * P], ident[:, :])
        last.then_inc(done, 1)


def dve_add_residual(nc, sh, dve, c, out, out_used, kept):
    dve.wait_ge(kept, c)
    nc.vector.tensor_tensor(sh.fresh[:, :, :], sh.x[:, tiles(c), :], out[:, :, :], ALU.add).then_inc(out_used, 1)
    dve.wait_ge(out_used, c + 1)


def pool_carry(nc, sh, i):
    nc.gpsimd.tensor_tensor(sh.pool_scratch[:, i:i + 1], sh.minus_half[:, 0:1], sh.minus_half[:, 0:1], ALU.add)


def stream_late(sp, units, used, load, late_used, late_load):
    def again(c, t, i, target, first=False):
        if target is not None:
            for semaphore in used:
                sp.wait_ge(semaphore, c * units + t + 1)
            load(target, i)
        if not first:
            sp.wait_ge(late_used, c * units + t - 1)
        late_load(t, i)

    def chunk(c, first=False, last=False):
        for i in range(2):
            again(c, i, i, i + 2, first)
        with sp.Fori(1, units // 2 - 1) as pair:
            for i in range(2):
                again(c, 2 * pair + i, i, 2 * pair + i + 2)
        for i in range(2):
            again(c, units - 2 + i, i, None if last else i)

    for i in range(2):
        load(i, i)
    chunk(0, first=True)
    with sp.Fori(1, CHUNKS - 1) as c:
        chunk(c)
    chunk(CHUNKS - 1, last=True)


def load_block(nc, sh):
    d = sh.dram
    x_in, xn_ready = sh.sem("x_in"), sh.sem("ld_xn_ready")
    cleared, const_ready = sh.sem("ld_cleared"), sh.sem("ld_const")
    own, var_ready, rstd_ready = sh.sem("ld_own"), sh.sem("ld_var"), sh.sem("ld_rstd")
    xs = d["x"].rearrange("b (h p) d -> p (b h) d", p=P)
    with nc.Block() as block:
        @block.sync
        def _(sp):
            for c in range(CHUNKS):
                sp.dma_start(sh.x[:, c * CT:(c + 1) * CT, :], xs[:, c * CT:(c + 1) * CT, :]).then_inc(x_in, 16)
                sp.wait_ge(x_in, 16 * (c + 1))

        @block.gpsimd
        def _(pool):
            nc.gpsimd.memset(sh.minus_half[:, :], -0.5).then_inc(cleared, 1)
            nc.gpsimd.memset(sh.ident[:, :], 0.0).then_inc(cleared, 1)
            nc.gpsimd.memset(sh.identb[:, :], 0.0).then_inc(cleared, 1)
            nc.gpsimd.memset(sh.x[:, TILES:TILES + CT, :], 0.0).then_inc(cleared, 1)
            for t in (sh.mean, sh.rstd):
                nc.gpsimd.memset(t[:, TILES:TILES + CT], 0.0).then_inc(cleared, 1)
            pool.wait_ge(cleared, 3)
            for m in (sh.ident, sh.identb):
                nc.gpsimd.affine_select(out=m[:, :], in_=m[:, :], compare_op=ALU.not_equal, fill=1.0, base=0,
                                        pattern=[[-1, P]], channel_multiplier=1).then_inc(const_ready, 1)
            with pool.Fori(0, CHUNKS) as c:
                pool_rstd(nc, sh, pool, c, var_ready, rstd_ready)

        @block.vector
        def _(dve):
            for c in range(CHUNKS):
                dve.wait_ge(x_in, 16 * (c + 1))
                chain = Chain(dve, own, c * STATS_LINKS, STATS_LINKS)
                dve_stats(nc, sh, dve, c, sh.x[:, c * CT:(c + 1) * CT, :], chain, var_ready, rstd_ready)
                chain.done()
                if c == 0:
                    dve.wait_ge(rstd_ready, 1)
                    dve_first_normalised(nc, sh, dve, xn_ready)


def store_block(nc, sh):
    out_done = sh.sem("out_done")
    with nc.Block() as block:
        @block.sync
        def _(sp):
            sp.dma_start(sh.dram["out"].rearrange("b (h p) d -> p (b h) d", p=P), sh.x[:, 0:TILES, :]).then_inc(out_done, 16)
            sp.wait_ge(out_done, 16)


def l0_attention_block(nc, sh):
    d = sh.dram
    H, DH = 16, 128
    SCALE = float(DH) ** -0.5
    CLIP = 1024.0
    QCOLS = [(0, P), (P, CAUSAL)]
    s = lambda name: sh.sem(f"a0_{name}")
    bias_in = s("bias_in")
    w_in = [s(f"w_in{i}") for i in range(2)]
    wo_in = [s(f"wo_in{i}") for i in range(2)]
    xn_ready, xT_banked, xT_ready = s("xn_ready"), s("xT_banked"), s("xT_ready")
    x_low, w_high, w_low = s("x_low"), s("w_high"), s("w_low")
    q_done, k_done, v_done = s("q_done"), s("k_done"), s("v_done")
    q_ready, k_ready, v_ready = s("q_ready"), s("k_ready"), s("v_ready")
    scores_done, top_ready, exps_done = s("scores_done"), s("top_ready"), s("exps_done")
    inv_ready, probs_ready, turned = s("inv_ready"), s("probs_ready"), s("turned")
    probsT_ready = [s(f"probsT_ready{i}") for i in range(SEQS)]
    z_done, z_ready, wo_done = s("z_done"), s("z_ready"), s("wo_done")
    out_used, kept, own, var_ready, rstd_ready = s("out_used"), s("kept"), s("own"), s("var"), s("rstd")

    with ExitStack() as ctx:
        sb = lambda name, shape, dt=F32: ctx.enter_context(nc.sbuf_tensor(f"a0_{name}", shape, dt))
        ps = lambda name, shape: ctx.enter_context(nc.psum_tensor(f"a0_{name}", shape, F32))
        bias = sb("bias", [P, H, CAUSAL])
        w = sb("w", [P, 2, 3, KC, DH])
        w_h, w_l = (sb(f"w_{n}", [P, 2, 2, KC, DH], F32R) for n in "hl")
        x_h, x_l = (sb(f"x_{n}", [P, KC, N], F32R) for n in "hl")
        wo = sb("wo", [P, 2, D])
        q, k = sb("q", [P, N]), sb("k", [P, N])
        v = sb("v", [P, 2, CT, DH])
        clipped = sb("clipped", [P, SEQS, CAUSAL])
        biased = sb("biased", [P, SEQS, CAUSAL])
        top, neg_top = sb("top", [P, SEQS, 2]), sb("neg_top", [P, SEQS, 2])
        sums, inv = sb("sums", [P, SEQS, 2]), sb("inv", [P, SEQS, 2])
        exps = sb("exps", [P, SEQS, CAUSAL])
        probs = sb("probs", [P, SEQS, CAUSAL])
        probsT = sb("probsT", [P, SEQS, CAUSAL])
        z = sb("z", [P, 2, N])
        qb, kb, vb, zb = (ps(f"{n}_bank", [P, N]) for n in "qkvz")
        score = ps("score", [P, SEQS, N])
        out = ps("out", [P, CT, D])
        block = ctx.enter_context(nc.Block())

        @block.sync
        def _(sp):
            def load_w(h, i):
                sp.dma_start(w[:, i, :, :, :].rearrange("p a k m -> p (a k m)"),
                             d["a0_w"][bass.ds(h, 1), :, 0:3 * D].rearrange("a p m -> (a p) m")).then_inc(w_in[i], 16)

            def load_wo(h, i):
                sp.dma_start(wo[:, i, :],
                             d["a0_w"][bass.ds(h, 1), :, 3 * D:4 * D].rearrange("a p m -> (a p) m")).then_inc(wo_in[i], 16)

            stream_late(sp, H, (k_done, v_done), load_w, wo_done, load_wo)

        @block.tensor
        def _(pe):
            def project_qk(c, k2, i):
                n = c * H + 2 * k2 + i
                pe.wait_ge(w_low, n + 1)
                pe.wait_ge(q_ready, n)
                for a, bank, done in ((0, qb, q_done), (1, kb, k_done)):
                    if a == 1:
                        pe.wait_ge(k_ready, n)
                    for kc in range(KC):
                        last = pe_three(nc, bank[:, :], (w_h[:, i, a, kc, :], x_h[:, kc, :]),
                                        (w_l[:, i, a, kc, :], x_l[:, kc, :]), kc == 0, kc == KC - 1)
                    last.then_inc(done, 1)

            def project_v(c, k2, i):
                pe.wait_ge(v_ready, c * H + 2 * k2 + i)
                for j in range(CT):
                    for kc in range(KC):
                        last = nc.tensor.matmul(vb[:, j * DH:(j + 1) * DH], sh.xT[:, kc, j * P:(j + 1) * P],
                                                w[:, i, 2, kc, :], start=kc == 0, stop=kc == KC - 1)
                last.then_inc(v_done, 1)

            def scores(c, k2, i):
                n = c * H + 2 * k2 + i
                pe.wait_ge(q_ready, n + 1)
                pe.wait_ge(k_ready, n + 1)
                for b in range(SEQS):
                    pe.wait_ge(probsT_ready[b], n)
                    for half in range(2):
                        t0, (c0, c1) = b * S, QCOLS[half]
                        last = nc.tensor.matmul(score[:, b, c0:c1], q[:, t0 + half * P:t0 + (half + 1) * P],
                                                k[:, t0:t0 + (half + 1) * P], start=True, stop=True)
                    last.then_inc(scores_done, 1)

            def turn(c, k2, i):
                n = c * H + 2 * k2 + i
                for b in range(SEQS):
                    pe.wait_ge(probs_ready, 2 * n + b + 1)
                    for blk in range(3):
                        last = nc.tensor.transpose(score[:, b, blk * P:(blk + 1) * P],
                                                   probs[:, b, blk * P:(blk + 1) * P], sh.ident[:, :])
                    last.then_inc(turned, 1)

            def values(c, k2, i):
                n = c * H + 2 * k2 + i
                pe.wait_ge(v_ready, n + 1)
                pe.wait_ge(z_ready, n)
                for b in range(SEQS):
                    pe.wait_ge(probsT_ready[b], n + 1)
                    nc.tensor.matmul(zb[:, b * S:(b + 1) * S], v[:, i, 2 * b, :], probsT[:, b, 0:S],
                                     start=True, stop=False, skip_group_check=True)
                    last = nc.tensor.matmul(zb[:, b * S + P:(b + 1) * S], v[:, i, 2 * b + 1, :],
                                            probsT[:, b, S:CAUSAL], start=False, stop=True, skip_group_check=True)
                last.then_inc(z_done, 1)

            def output(c, k2, i, js=range(CT), first=False, last_head=False):
                n = c * H + 2 * k2 + i
                if 0 in js:
                    pe.wait_ge(wo_in[i], 16 * (c * (H // 2) + k2 + 1))
                    pe.wait_ge(z_ready, n + 1)
                    if first:
                        pe.wait_ge(out_used, c)
                for j in js:
                    last = nc.tensor.matmul(out[:, j, :], z[:, i, j * P:(j + 1) * P], wo[:, i, :],
                                            start=first and j % 2 == 0, stop=last_head, skip_group_check=True)
                if CT - 1 in js:
                    last.then_inc(wo_done, 1)

            def step(c, head, following, before=None, first=False):
                project_qk(c, *following)
                project_v(c, *following)
                if before:
                    output(c, *before, js=(0, 1), first=first)
                turn(c, *head)
                if before:
                    output(c, *before, js=(2, 3), first=first)
                values(c, *head)
                scores(c, *following)

            with pe.Fori(0, CHUNKS) as c:
                pe.wait_ge(xn_ready, c)
                pe_features(nc, sh.xn, sh.ident, (qb, kb), xT_banked)
                pe.wait_ge(xT_ready, 2 * (c + 1))
                pe.wait_ge(w_in[0], 16 * (c * (H // 2) + 1))
                project_v(c, 0, 0)
                pe.wait_ge(x_low, c + 1)
                project_qk(c, 0, 0)
                scores(c, 0, 0)
                step(c, (0, 0), (0, 1))
                step(c, (0, 1), (1, 0), before=(0, 0), first=True)
                with pe.Fori(1, H // 2 - 1) as k2:
                    step(c, (k2, 0), (k2, 1), before=(k2 - 1, 1))
                    step(c, (k2, 1), (k2 + 1, 0), before=(k2, 0))
                step(c, (H // 2 - 1, 0), (H // 2 - 1, 1), before=(H // 2 - 2, 1))
                output(c, H // 2 - 1, 0)
                turn(c, H // 2 - 1, 1)
                values(c, H // 2 - 1, 1)
                output(c, H // 2 - 1, 1, last_head=True)

        @block.scalar
        def _(act):
            act.dma_start(bias[:, :, :], d["a0_bias"]).then_inc(bias_in, 16)

            def take_q(c, k2, i):
                n = c * H + 2 * k2 + i
                act.wait_ge(q_done, n + 1)
                act.wait_ge(scores_done, 2 * n)
                nc.scalar.activation(q[:, :], qb[:, :], ACT.Copy, scale=SCALE).then_inc(q_ready, 1)

            def take_k(c, k2, i):
                act.wait_ge(k_done, c * H + 2 * k2 + i + 1)
                nc.scalar.activation(k[:, :], kb[:, :], ACT.Copy).then_inc(k_ready, 1)

            def take_v(c, k2, i):
                n = c * H + 2 * k2 + i
                act.wait_ge(v_done, n + 1)
                nc.scalar.activation(v[:, i, :, :].rearrange("p j e -> p (j e)"), vb[:, :], ACT.Copy).then_inc(v_ready, 1)

            def softmax(c, k2, i, b):
                n = c * H + 2 * k2 + i
                act.wait_ge(top_ready, 2 * n + b + 1)
                act.wait_ge(probs_ready, 2 * n)
                for half in range(2):
                    c0, c1 = QCOLS[half]
                    last = nc.scalar.activation(exps[:, b, c0:c1], biased[:, b, c0:c1], ACT.Exp,
                                                bias=neg_top[:, b, half:half + 1],
                                                accum_out=sums[:, b, half:half + 1])
                last.then_inc(exps_done, 1)

            def take_probsT(c, k2, i):
                act.wait_ge(turned, 2 * (c * H + 2 * k2 + i) + 2)
                nc.scalar.activation(probsT[:, 1, :], score[:, 1, 0:CAUSAL], ACT.Copy).then_inc(probsT_ready[1], 1)

            def high(c, k2, i):
                act.wait_ge(w_in[i], 16 * (c * (H // 2) + k2 + 1))
                nc.scalar.activation(w_h[:, i, :, :, :].rearrange("p a k m -> p (a k m)"),
                                     w[:, i, 0:2, :, :].rearrange("p a k m -> p (a k m)"), ACT.Copy).then_inc(w_high, 1)

            def step(c, head, following, weights=None):
                softmax(c, *head, 0)
                take_q(c, *following)
                softmax(c, *head, 1)
                take_k(c, *following)
                take_v(c, *following)
                if weights:
                    high(c, *weights)
                take_probsT(c, *head)

            with act.Fori(0, CHUNKS) as c:
                high(c, 0, 0)
                for kc, bank in enumerate((qb, kb)):
                    act.wait_ge(xT_banked, 2 * c + kc + 1)
                    nc.scalar.activation(sh.xT[:, kc, :], bank[:, :], ACT.Copy)
                    nc.scalar.activation(x_h[:, kc, :], bank[:, :], ACT.Copy).then_inc(xT_ready, 1)
                high(c, 0, 1)
                take_v(c, 0, 0)
                take_q(c, 0, 0)
                take_k(c, 0, 0)
                step(c, (0, 0), (0, 1), (1, 0))
                with act.Fori(1, H // 2 - 1) as k2:
                    step(c, (k2 - 1, 1), (k2, 0), (k2, 1))
                    step(c, (k2, 0), (k2, 1), (k2 + 1, 0))
                step(c, (H // 2 - 2, 1), (H // 2 - 1, 0), (H // 2 - 1, 1))
                step(c, (H // 2 - 1, 0), (H // 2 - 1, 1))
                softmax(c, H // 2 - 1, 1, 0)
                softmax(c, H // 2 - 1, 1, 1)
                take_probsT(c, H // 2 - 1, 1)

        @block.gpsimd
        def _(pool):
            def low_w(n, i):
                pool.wait_ge(w_high, n + 1)
                pool_low(nc, w[:, i, 0:2, :, :].rearrange("p a k m -> p (a k m)"),
                         w_h[:, i, :, :, :].rearrange("p a k m -> p (a k m)"),
                         w_l[:, i, :, :, :].rearrange("p a k m -> p (a k m)")).then_inc(w_low, 1)

            def low_x(c):
                pool.wait_ge(xT_ready, 2 * c + 2)
                pool_low(nc, sh.xT[:, :, :], x_h[:, :, :], x_l[:, :, :]).then_inc(x_low, 1)

            def normalise(n):
                for b in range(SEQS):
                    pool.wait_ge(inv_ready, 2 * n + b + 1)
                    pool.wait_ge(turned, 2 * n)
                    pool_carry(nc, sh, b)
                    for half in range(2):
                        c0, c1 = QCOLS[half]
                        ins = nc.gpsimd.tensor_scalar(probs[:, b, c0:c1], exps[:, b, c0:c1],
                                                      inv[:, b, half:half + 1], 1.0, ALU.mult, ALU.mult)
                    ins.then_inc(probs_ready, 1)

            def chunk(c, last=False):
                low_w(c * H + 1, 1)
                with pool.Fori(0, H // 2 - 1) as k2:
                    for i in range(2):
                        normalise(c * H + 2 * k2 + i)
                        low_w(c * H + 2 * k2 + i + 2, i)
                for i in range(2):
                    normalise(c * H + H - 2 + i)
                if not last:
                    low_w((c + 1) * H, 0)
                    low_x(c + 1)
                pool_rstd(nc, sh, pool, c, var_ready, rstd_ready)

            low_w(0, 0)
            low_x(0)
            with pool.Fori(0, CHUNKS - 1) as c:
                chunk(c)
            chunk(CHUNKS - 1, last=True)

        @block.vector
        def _(dve):
            PER_HEAD = SEQS * 4
            LINKS = H * PER_HEAD + STATS_LINKS
            dve.wait_ge(bias_in, 16)
            with dve.Fori(0, CHUNKS) as c:
                with dve.Fori(0, H // 2) as k2:
                    for i in range(2):
                        h = 2 * k2 + i
                        n = c * H + h
                        chain = Chain(dve, own, c * LINKS + h * PER_HEAD, PER_HEAD)
                        for b in range(SEQS):
                            dve.wait_ge(scores_done, 2 * n + b + 1)
                            chain.link(nc.vector.tensor_scalar(clipped[:, b, :], score[:, b, 0:CAUSAL], CLIP, -CLIP,
                                                               ALU.min, ALU.max))
                            dve.wait_ge(exps_done, 2 * n)
                            chain.link(nc.vector.tensor_tensor(biased[:, b, :], clipped[:, b, :],
                                                               bias[:, bass.ds(h, 1), :], ALU.add))
                            for half in range(2):
                                c0, c1 = QCOLS[half]
                                chain.mark(nc.vector.tensor_reduce(top[:, b, half:half + 1], biased[:, b, c0:c1],
                                                                   AX, ALU.max))
                            chain.wait()
                            nc.vector.tensor_scalar(neg_top[:, b, :], top[:, b, :], -1.0, None,
                                                    ALU.mult).then_inc(top_ready, 1)
                        for b in range(SEQS):
                            dve.wait_ge(exps_done, 2 * n + b + 1)
                            nc.vector.reciprocal(inv[:, b, :], sums[:, b, :]).then_inc(inv_ready, 1)
                        chain.done()
                        dve.wait_ge(turned, 2 * n + 1)
                        nc.vector.tensor_copy(probsT[:, 0, :], score[:, 0, 0:CAUSAL]).then_inc(probsT_ready[0], 1)
                        dve.wait_ge(z_done, n + 1)
                        nc.vector.tensor_copy(z[:, i, :], zb[:, :]).then_inc(z_ready, 1)
                chain = Chain(dve, own, c * LINKS + H * PER_HEAD, STATS_LINKS)
                dve_normalise(nc, sh, c + 1, xn_ready)
                dve.wait_ge(wo_done, (c + 1) * H)
                dve_add_residual(nc, sh, dve, c, out, out_used, kept)
                dve_stats(nc, sh, dve, c, sh.fresh, chain, var_ready, rstd_ready, kept)
                chain.done()
            dve_first_normalised(nc, sh, dve, xn_ready, kept, CHUNKS)


def ffn_block(nc, sh, tag, weights, router, sel, experts, top, n_tiles, gated):
    R = experts + 1
    T = n_tiles
    PAIRS = T // 2
    pad = max(8 - top, 4)
    assert T % 2 == 0 and 3 * R <= P
    s = lambda name: sh.sem(f"{tag}_{name}")
    rt_in, hot_in = s("rt_in"), s("hot_in")
    w_gu_in = [s(f"w_gu_in{i}") for i in range(2)]
    w_down_in = [s(f"w_down_in{i}") for i in range(2)]
    xn_ready, xT_banked, xT_ready = s("xn_ready"), s("xT_banked"), s("xT_ready")
    logits_done, shifted, exps_done, parts_ready = s("logits"), s("shifted"), s("exps"), s("parts")
    shares_banked, shares_ready = s("shares_banked"), s("shares")
    gate_done, up_done, bcast_done = s("gate_done"), s("up_done"), s("bcast_done")
    silu_done, act_done, hidden_done = s("silu_done"), s("act_done"), s("hidden_done")
    down_done, out_used = s("down_done"), s("out_used")
    own, init, var_ready, rstd_ready = s("own"), s("init"), s("var"), s("rstd")
    kept = s("kept")
    gu_high, gu_low, down_high, down_low = s("gu_high"), s("gu_low"), s("down_high"), s("down_low")
    hidden_high, hidden_low, x_low = s("hidden_high"), s("hidden_low"), s("x_low")

    with ExitStack() as ctx:
        sb = lambda name, shape, dt=F32: ctx.enter_context(nc.sbuf_tensor(f"{tag}_{name}", shape, dt))
        ps = lambda name, shape, dt=F32: ctx.enter_context(nc.psum_tensor(f"{tag}_{name}", shape, dt))
        gu = sb("gu", [P, 2, 2 * KC * P])
        down = sb("down", [P, 2, D])
        gu_h, gu_l = sb("gu_h", [P, 2, 2 * KC * P], F32R), sb("gu_l", [P, 2, 2 * KC * P], F32R)
        down_h, down_l = sb("down_h", [P, 2, D], F32R), sb("down_l", [P, 2, D], F32R)
        x_h, x_l = sb("x_h", [P, KC, N], F32R), sb("x_l", [P, KC, N], F32R)
        hidden_h, hidden_l = sb("hidden_h", [P, 2, N], F32R), sb("hidden_l", [P, 2, N], F32R)
        rt = sb("rt", [P, KC, R])
        onehot = sb("onehot", [P, T * P], BF16)
        logit = sb("logit", [P, CT, R])
        top1 = sb("top1", [P, CT])
        exps = sb("exps", [P, CT, R])
        total = sb("total", [P, CT])
        inv = sb("inv", [P, CT])
        probs = sb("probs", [P, CT, experts + pad])
        best = sb("best", [P, CT, 8])
        rest = sb("rest", [P, CT, experts + pad])
        share = sb("share", [P, CT, R])
        left = sb("left", [P, 2, CT, R])
        parts = sb("parts", [P, CT, P], BF16)
        shares = sb("shares", [P, N], BF16)
        act_g = sb("act_g", [P, 2, N])
        hidden = sb("hidden", [P, 2, N])
        gate = [ps(f"gate{i}", [P, N]) for i in range(2)]
        up = [ps(f"up{i}", [P, N]) for i in range(2)]
        bcast = [ps(f"bcast{i}", [P, N]) for i in range(2)]
        out = ps("out", [P, CT, D])
        logits = bcast[0][:, 0:CT * R].rearrange("p (j r) -> p j r", j=CT)
        turned = bcast[1][:, 0:N // 2].bitcast(BF16)

        block = ctx.enter_context(nc.Block())

        @block.sync
        def _(sp):
            sp.dma_start(rt[:, :, :], router).then_inc(rt_in, 16)

            def load_gate_up(t, i):
                sp.dma_start(gu[:, i, :], weights[bass.ds(t, 1), :, 0:2 * KC * P]
                             .rearrange("a p m -> (a p) m")).then_inc(w_gu_in[i], 16)

            def load_down(t, i):
                sp.dma_start(down[:, i, :],
                             weights[bass.ds(t, 1), :, 2 * KC * P:2 * KC * P + D]
                             .rearrange("a p m -> (a p) m")).then_inc(w_down_in[i], 16)

            stream_late(sp, T, (gu_low,), load_gate_up, down_low, load_down)

        @block.tensor
        def _(pe):
            def gate_up(c, k, i, first):
                n = c * T + 2 * k + i
                pe.wait_ge(gu_low, n + 1)
                if not first:
                    pe.wait_ge(silu_done, n - 1)
                for a_, bank, done in ((0, gate[i], gate_done), (1, up[i], up_done)):
                    if a_ and not first:
                        pe.wait_ge(act_done, n - 1)
                    for kc in range(KC):
                        cols = slice((a_ * KC + kc) * P, (a_ * KC + kc + 1) * P)
                        last = pe_three(nc, bank[:, :], (gu_h[:, i, cols], x_h[:, kc, :]), (gu_l[:, i, cols], x_l[:, kc, :]),
                                     kc == 0, kc == KC - 1)
                    last.then_inc(done, 1)

            def broadcast(c, k, i, first):
                t = 2 * k + i
                if not first:
                    pe.wait_ge(hidden_done, c * T + t - 1)
                nc.tensor.matmul(bcast[i][:, :], onehot[:, bass.ds(t * P, P)], shares[:, :],
                                 start=True, stop=True).then_inc(bcast_done, 1)

            def project(c, k, i, first=False, last_tile=False):
                n = c * T + 2 * k + i
                pe.wait_ge(down_low, n + 1)
                pe.wait_ge(hidden_low, n + 1)
                if first:
                    pe.wait_ge(out_used, c)
                for j in range(CT):
                    cols = slice(j * P, (j + 1) * P)
                    last = pe_three(nc, out[:, j, :], (hidden_h[:, i, cols], down_h[:, i, :]),
                                 (hidden_l[:, i, cols], down_l[:, i, :]),
                                 first and j % 2 == 0, last_tile, skip_group_check=True)
                last.then_inc(down_done, 1)

            with pe.Fori(0, CHUNKS) as c:
                pe.wait_ge(xn_ready, c)
                pe.wait_ge(silu_done, c * T)
                pe_features(nc, sh.xn, sh.ident, gate, xT_banked)
                pe.wait_ge(xT_ready, 2 * (c + 1))
                pe.wait_ge(hidden_done, c * T)
                pe.wait_ge(rt_in, 16)
                for j in range(CT):
                    for kc in range(KC):
                        last = nc.tensor.matmul(logits[:, j, :], sh.xT[:, kc, j * P:(j + 1) * P], rt[:, kc, :],
                                                start=kc == 0, stop=kc == KC - 1)
                last.then_inc(logits_done, 1)
                pe.wait_ge(x_low, c + 1)
                gate_up(c, 0, 0, True)
                gate_up(c, 0, 1, True)
                pe.wait_ge(parts_ready, c + 1)
                for j in range(CT):
                    last = nc.tensor.transpose(turned[:, j * P:(j + 1) * P], parts[:, j, :], sh.identb[:, :])
                last.then_inc(shares_banked, 1)
                pe.wait_ge(shares_ready, c + 1)
                pe.wait_ge(hot_in, 16)
                broadcast(c, 0, 0, True)
                broadcast(c, 0, 1, True)
                for i in range(2):
                    gate_up(c, 1, i, False)
                    broadcast(c, 1, i, False)
                    project(c, 0, i, first=i == 0)
                with pe.Fori(1, PAIRS - 1) as pair:
                    for i in range(2):
                        gate_up(c, pair + 1, i, False)
                        broadcast(c, pair + 1, i, False)
                        project(c, pair, i)
                project(c, PAIRS - 1, 0)
                project(c, PAIRS - 1, 1, last_tile=True)

        @block.scalar
        def _(act):
            act.dma_start(onehot[:, :], sel).then_inc(hot_in, 16)

            def high_gate_up(c, k, i, first=False):
                act.wait_ge(w_gu_in[i], 16 * (c * PAIRS + k + 1))
                if first:
                    act.wait_ge(up_done, c * T)
                else:
                    act.wait_ge(up_done, c * T + 2 * k + i - 1)
                nc.scalar.activation(gu_h[:, i, :], gu[:, i, :], ACT.Copy).then_inc(gu_high, 1)

            def high_down(c, k, i, first=False):
                act.wait_ge(w_down_in[i], 16 * (c * PAIRS + k + 1))
                if first:
                    act.wait_ge(down_done, c * T)
                else:
                    act.wait_ge(down_done, c * T + 2 * k + i - 1)
                nc.scalar.activation(down_h[:, i, :], down[:, i, :], ACT.Copy).then_inc(down_high, 1)

            def silu(c, k, i, first=False):
                n = c * T + 2 * k + i
                act.wait_ge(gate_done, n + 1)
                if first:
                    act.wait_ge(hidden_done, c * T)
                else:
                    act.wait_ge(hidden_done, n - 1)
                nc.scalar.activation(act_g[:, i, :], gate[i][:, :], ACT.Silu).then_inc(silu_done, 1)

            def high_hidden(c, k, i):
                act.wait_ge(hidden_done, c * T + 2 * k + i + 1)
                nc.scalar.activation(hidden_h[:, i, :], hidden[:, i, :], ACT.Copy).then_inc(hidden_high, 1)

            def step(c, k, i, following=None):
                silu(c, k, i)
                if following:
                    high_gate_up(c, *following)
                high_down(c, k, i)
                high_hidden(c, k, i)

            with act.Fori(0, CHUNKS) as c:
                high_gate_up(c, 0, 0, first=True)
                high_gate_up(c, 0, 1, first=True)
                for kc in range(KC):
                    act.wait_ge(xT_banked, 2 * c + kc + 1)
                    nc.scalar.activation(sh.xT[:, kc, :], gate[kc][:, :], ACT.Copy)
                    nc.scalar.activation(x_h[:, kc, :], gate[kc][:, :], ACT.Copy).then_inc(xT_ready, 1)
                act.wait_ge(shifted, c + 1)
                nc.scalar.activation(exps[:, :, :], logit[:, :, :], ACT.Exp).then_inc(exps_done, 1)
                silu(c, 0, 0, first=True)
                silu(c, 0, 1, first=True)
                for i in range(2):
                    high_gate_up(c, 1, i)
                for i in range(2):
                    high_down(c, 0, i, first=True)
                for i in range(2):
                    high_hidden(c, 0, i)
                with act.Fori(1, PAIRS - 1) as pair:
                    for i in range(2):
                        step(c, pair, i, following=(pair + 1, i))
                for i in range(2):
                    step(c, PAIRS - 1, i)

        @block.gpsimd
        def _(pool):
            nc.gpsimd.memset(parts[:, :, :], 0.0).then_inc(init, 1)
            nc.gpsimd.memset(probs[:, :, :], -1.0).then_inc(init, 1)
            if not gated:
                nc.gpsimd.memset(share[:, :, :], 1.0).then_inc(init, 1)
                nc.gpsimd.memset(logit[:, :, :], 0.0).then_inc(init, 1)

            def low(value, high, out_, high_done, n, done):
                pool.wait_ge(high_done, n)
                pool_low(nc, value, high, out_).then_inc(done, 1)

            def low_gate_up(n, i):
                low(gu[:, i, :], gu_h[:, i, :], gu_l[:, i, :], gu_high, n + 1, gu_low)

            def low_down(n, i):
                low(down[:, i, :], down_h[:, i, :], down_l[:, i, :], down_high, n + 1, down_low)

            def chunk(c, last=False):
                n = c * T
                low_gate_up(n + 2, 0)
                low_gate_up(n + 3, 1)
                low_down(n, 0)
                low_down(n + 1, 1)
                with pool.Fori(1, PAIRS - 1) as pair:
                    for i in range(2):
                        low_gate_up(n + 2 * pair + i + 2, i)
                        low_down(n + 2 * pair + i, i)
                low_down(n + T - 2, 0)
                low_down(n + T - 1, 1)
                if not last:
                    for i in range(2):
                        low_gate_up(n + T + i, i)
                pool_rstd(nc, sh, pool, c, var_ready, rstd_ready)

            for i in range(2):
                low_gate_up(i, i)
            with pool.Fori(0, CHUNKS - 1) as c:
                chunk(c)
            chunk(CHUNKS - 1, last=True)

        @block.vector
        def _(dve):
            LINKS = (24 if gated else 17) + STATS_LINKS
            E = experts
            dve.wait_ge(init, 2 if gated else 4)

            def wide(v, n):
                return v.rearrange("p (j a) -> p j a", a=1).broadcast_to([P, CT, n])

            def hidden_tile(c, t, i, first):
                n = c * T + t
                dve.wait_ge(silu_done, n + 1)
                dve.wait_ge(up_done, n + 1)
                nc.vector.tensor_tensor(act_g[:, i, :], act_g[:, i, :], up[i][:, :], ALU.mult).then_inc(act_done, 1)
                dve.wait_ge(bcast_done, n + 1)
                dve.wait_ge(act_done, n + 1)
                if not first:
                    dve.wait_ge(hidden_low, n - 1)
                nc.vector.tensor_tensor(hidden[:, i, :], act_g[:, i, :], bcast[i][:, :],
                                        ALU.mult).then_inc(hidden_done, 1)
                dve.wait_ge(hidden_high, n + 1)
                nc.vector.tensor_tensor(hidden_l[:, i, :], hidden[:, i, :], hidden_h[:, i, :].bitcast(F32),
                                        ALU.subtract).then_inc(hidden_low, 1)

            with dve.Fori(0, CHUNKS) as c:
                chain = Chain(dve, own, c * LINKS, LINKS)
                link = chain.link
                dve.wait_ge(xT_ready, 2 * c + 2)
                nc.vector.tensor_tensor(x_l[:, :, :], sh.xT[:, :, :], x_h[:, :, :].bitcast(F32), ALU.subtract).then_inc(x_low, 1)
                dve.wait_ge(logits_done, c + 1)
                link(nc.vector.tensor_reduce(top1[:, :], logits[:, :, 0:E], AX, ALU.max))
                if gated:
                    link(nc.vector.tensor_scalar(logit[:, :, E], logits[:, :, E], -1.0, None, ALU.mult))
                nc.vector.tensor_tensor(logit[:, :, 0:E], logits[:, :, 0:E], wide(top1[:, :], E),
                                        ALU.subtract).then_inc(shifted, 1)
                dve.wait_ge(exps_done, c + 1)
                link(nc.vector.tensor_reduce(total[:, :], exps[:, :, 0:E], AX, ALU.add))
                link(nc.vector.reciprocal(inv[:, :], total[:, :]))
                link(nc.vector.tensor_tensor(probs[:, :, 0:E], exps[:, :, 0:E], wide(inv[:, :], E), ALU.mult), carrier=sh.scratch[:, :])
                for j in range(CT):
                    chain.mark(nc.vector.max(best[:, j, :], probs[:, j, :]))
                chain.wait()
                if gated:
                    link(nc.vector.tensor_reduce(total[:, :], best[:, :, 0:top], AX, ALU.add))
                    link(nc.vector.tensor_scalar(total[:, :], total[:, :], 1e-9, None, ALU.max))
                    link(nc.vector.reciprocal(inv[:, :], total[:, :]))
                link(nc.vector.memset(best[:, :, top:8], -1.0), carrier=sh.scratch[:, :])
                for j in range(CT):
                    chain.mark(nc.vector.match_replace(rest[:, j, :], best[:, j, :], probs[:, j, :], 0.0))
                chain.wait()
                link(nc.vector.tensor_tensor(share[:, :, 0:E], probs[:, :, 0:E], rest[:, :, 0:E], ALU.subtract))
                if gated:
                    link(nc.vector.tensor_tensor(share[:, :, 0:E], share[:, :, 0:E], wide(inv[:, :], E), ALU.mult))
                    link(nc.vector.tensor_scalar(left[:, 0, :, E], exps[:, :, E], 1.0, None, ALU.add))
                    link(nc.vector.reciprocal(share[:, :, E], left[:, 0, :, E]))
                link(nc.vector.tensor_copy(parts[:, :, 0:R], share[:, :, :]))
                link(nc.vector.tensor_tensor(left[:, 0, :, :], share[:, :, :], parts[:, :, 0:R], ALU.subtract))
                link(nc.vector.tensor_copy(parts[:, :, R:2 * R], left[:, 0, :, :]))
                nc.vector.tensor_tensor(parts[:, :, 2 * R:3 * R], left[:, 0, :, :], parts[:, :, R:2 * R],
                                        ALU.subtract).then_inc(parts_ready, 1)
                dve.wait_ge(shares_banked, c + 1)
                nc.vector.tensor_copy(shares[:, :], turned).then_inc(shares_ready, 1)
                hidden_tile(c, 0, 0, True)
                hidden_tile(c, 1, 1, True)
                with dve.Fori(0, PAIRS - 1) as pair:
                    for i in range(2):
                        hidden_tile(c, 2 * pair + i + 2, i, False)
                dve_normalise(nc, sh, c + 1, xn_ready)
                dve.wait_ge(down_done, (c + 1) * T)
                dve_add_residual(nc, sh, dve, c, out, out_used, kept)
                dve_stats(nc, sh, dve, c, sh.fresh, chain, var_ready, rstd_ready, kept)
                chain.done()
            dve_first_normalised(nc, sh, dve, xn_ready, kept, CHUNKS)


def retention_block(nc, sh):
    d = sh.dram
    H, DK, TAPS, EPS, MT = 8, 32, 4, 1e-5, 3
    HT = H // KC
    s = lambda name: sh.sem(f"rt_{name}")
    w_in = [s(f"w_in{i}") for i in range(9)]
    init, xn_ready = s("init"), s("xn_ready")
    sq_done, ms_ready, r_ready, normed = s("sq_done"), s("ms_ready"), s("r_ready"), s("normed")
    xT_banked, xT_ready = s("xT_banked"), s("xT_ready")
    proj_done, raw_ready, conv_ready, silu_ready = s("proj_done"), s("raw_ready"), s("conv_ready"), s("silu_ready")
    g_done, g_ready = s("g_done"), s("g_ready")
    swap_done, cosed, rot_ready = s("swap_done"), s("cosed"), s("rot_ready")
    v_turned, v_ready = s("v_turned"), s("v_ready")
    a_done, a_ready, o_done = s("a_done"), s("a_ready"), s("o_done")
    og_ready, turned_done, turned_ready = s("og_ready"), s("turned_done"), s("turned_ready")
    wo_done, h_ready = s("wo_done"), s("h_ready")
    gate_done, act_ready, hidden_ready, down_done = s("gate_done"), s("act_ready"), s("hidden_ready"), s("down_done")
    out_used, kept, own, var_ready, rstd_ready = s("out_used"), s("kept"), s("own"), s("var"), s("rstd")

    with ExitStack() as ctx:
        sb = lambda name, shape, dt=F32: ctx.enter_context(nc.sbuf_tensor(f"rt_{name}", shape, dt))
        ps = lambda name: ctx.enter_context(nc.psum_tensor(f"rt_{name}", [P, 2, N], F32))
        wqkvg = sb("wqkvg", [P, 4, KC, D])
        wo = sb("wo", [P, KC, D])
        w_gate = sb("w_gate", [P, 2, KC, MT * P])
        w_down = sb("w_down", [P, MT, D])
        swap = sb("swap", [P, P])
        rope = sb("rope", [P, 2, S])
        decay = sb("decay", [P, H, S])
        cols = sb("cols", [P, KC, 3 * TAPS + 2])
        gnw = sb("gnw", [P, D])
        square = sb("square", [P, CT, D])
        squares, ms, rr = sb("squares", [P, CT]), sb("ms", [P, CT * H]), sb("rr", [P, CT * H])
        normal = sb("normal", [P, CT, D])
        raw = sb("raw", [P, 3, KC, SEQS, TAPS - 1 + S])
        conv = sb("conv", [P, 3, KC, SEQS, S])
        qkv = sb("qkv", [P, 3, KC, N])
        turned = sb("turned", [P, 2, KC, N])
        sines = sb("sines", [P, KC, N])
        v = sb("v", [P, CT, D])
        gate = sb("gate", [P, CT, D])
        ad = sb("ad", [P, 2, SEQS, CAUSAL])
        og = sb("og", [P, CT, D])
        featT = sb("featT", [P, KC, N])
        hh = sb("hh", [P, CT, D])
        act_g = sb("act_g", [P, MT, N])
        A, Bk, C, E = ps("A"), ps("B"), ps("C"), ps("D")
        block = ctx.enter_context(nc.Block())
        flat = lambda t: t.rearrange("p j e -> p (j e)")
        token = lambda bank: bank[:, :, :].rearrange("p a t -> p (a t)").rearrange("p (j e) -> p j e", j=CT)

        @block.sync
        def _(sp):
            for t, name, in_ in ((cols, "rt_cols", 0), (wqkvg, "rt_wqkvg", 1), (swap, "rt_swap", 2),
                                 (rope, "rt_rope", 3), (decay, "rt_decay", 4)):
                sp.dma_start(t[:], d[name]).then_inc(w_in[in_], 16)

        @block.tensor
        def _(pe):
            def turn(src, bank, done):
                pe_features(nc, src, sh.ident, (bank[:, 0, :], bank[:, 1, :]), done)

            with pe.Fori(0, CHUNKS) as c:
                pe.wait_ge(normed, 2 * c + 1)
                pe.wait_ge(hidden_ready, c * MT)
                turn(normal, A, xT_banked)
                pe.wait_ge(xT_ready, 2 * c + 1)
                pe.wait_ge(w_in[1], 16)
                pe.wait_ge(kept, c)
                for a, bank in enumerate((Bk, C, E)):
                    for m in range(KC):
                        for kc in range(KC):
                            last = nc.tensor.matmul(bank[:, m, :], wqkvg[:, a, kc, m * P:(m + 1) * P], sh.xT[:, kc, :],
                                                    start=kc == 0, stop=kc == KC - 1)
                    last.then_inc(proj_done, 1)
                for j in range(CT):
                    for kc in range(KC):
                        last = nc.tensor.matmul(token(A)[:, j, :], sh.xT[:, kc, j * P:(j + 1) * P], wqkvg[:, 3, kc, :],
                                                start=kc == 0, stop=kc == KC - 1, skip_group_check=True)
                last.then_inc(g_done, 1)
                pe.wait_ge(w_in[2], 16)
                for a, bank in enumerate((Bk, C)):
                    pe.wait_ge(silu_ready, 3 * c + a + 1)
                    for m in range(KC):
                        last = nc.tensor.matmul(bank[:, m, :], swap[:, :], qkv[:, a, m, :], start=True, stop=True)
                    last.then_inc(swap_done, 1)
                pe.wait_ge(silu_ready, 3 * c + 3)
                for m in range(KC):
                    for j in range(CT):
                        last = nc.tensor.transpose(token(E)[:, j, m * P:(m + 1) * P],
                                                   qkv[:, 2, m, j * P:(j + 1) * P], sh.ident[:, :])
                last.then_inc(v_turned, 1)
                pe.wait_ge(rot_ready, 2 * c + 2)

                def scores(h):
                    bank, p0, m = (Bk, C)[h % 2], DK * (h % HT), h // HT
                    if h >= 2:
                        pe.wait_ge(a_ready, c * H + h - 1)
                    for b in range(SEQS):
                        for kb in range(2):
                            t0 = b * S
                            last = nc.tensor.matmul(bank[:, b, kb * S:kb * S + S - kb * P],
                                                    turned[p0:p0 + DK, 1, m, t0 + kb * P:t0 + (kb + 1) * P],
                                                    turned[p0:p0 + DK, 0, m, t0 + kb * P:t0 + S],
                                                    start=True, stop=True, skip_group_check=True)
                    last.then_inc(a_done, 1)

                def values(h):
                    pe.wait_ge(a_ready, c * H + h + 1)
                    for b in range(SEQS):
                        for half in range(2):
                            for kb in range(half + 1):
                                c0 = half * P if kb == 0 else S
                                last = nc.tensor.matmul(token(E)[:, 2 * b + half, h * DK:(h + 1) * DK],
                                                        ad[:, h % 2, b, c0:c0 + P], v[:, 2 * b + kb, h * DK:(h + 1) * DK],
                                                        start=kb == 0, stop=kb == half, skip_group_check=True)
                    if h == H - 1:
                        last.then_inc(o_done, 1)

                scores(0)
                pe.wait_ge(v_ready, c + 1)
                for h in range(1, H):
                    scores(h)
                    values(h - 1)
                values(H - 1)
                pe.wait_ge(og_ready, c + 1)
                turn(og, Bk, turned_done)
                pe.wait_ge(turned_ready, 2 * c + 1)
                pe.wait_ge(w_in[6], 16)
                for j in range(CT):
                    for kc in range(KC):
                        last = nc.tensor.matmul(token(C)[:, j, :], featT[:, kc, j * P:(j + 1) * P], wo[:, kc, :],
                                                start=kc == 0, stop=kc == KC - 1, skip_group_check=True)
                last.then_inc(wo_done, 1)
                pe.wait_ge(normed, 2 * c + 2)
                turn(normal, Bk, turned_done)
                pe.wait_ge(turned_ready, 2 * c + 2)
                pe.wait_ge(g_ready, c + 1)
                pe.wait_ge(w_in[7], 16)
                pe.wait_ge(w_in[8], 16)
                for t, bank in enumerate((A, Bk, C)):
                    for a in range(2):
                        for kc in range(KC):
                            last = nc.tensor.matmul(bank[:, a, :], w_gate[:, a, kc, t * P:(t + 1) * P], featT[:, kc, :],
                                                    start=kc == 0, stop=kc == KC - 1)
                    last.then_inc(gate_done, 1)
                for t in range(MT):
                    pe.wait_ge(hidden_ready, c * MT + t + 1)
                    for j in range(CT):
                        last = nc.tensor.matmul(token(E)[:, j, :], act_g[:, t, j * P:(j + 1) * P], w_down[:, t, :],
                                                start=t == 0 and j % 2 == 0, stop=t == MT - 1, skip_group_check=True)
                last.then_inc(down_done, 1)

        @block.scalar
        def _(act):
            for t, name, in_ in ((gnw, "rt_gnw", 5), (wo, "rt_wo", 6), (w_gate, "rt_w_gate", 7), (w_down, "rt_w_down", 8)):
                act.dma_start(t[:], d[name]).then_inc(w_in[in_], 16)

            def squares_of(src, k, n):
                act.wait_ge(ms_ready, n)
                for j in range(CT):
                    last = nc.scalar.activation(square[:, j, :], src[:, j, :], ACT.Square, accum_out=squares[:, j:j + 1])
                last.then_inc(sq_done, 1)

            def silu(c, a):
                act.wait_ge(conv_ready, 3 * c + a + 1)
                nc.scalar.activation(qkv[:, a, :, :].rearrange("p m t -> p (m t)"),
                                     conv[:, a, :, :, :].rearrange("p m b t -> p (m b t)"), ACT.Silu).then_inc(silu_ready, 1)

            act.wait_ge(w_in[0], 16)
            act.wait_ge(init, 1)
            squares_of(sh.xn, 0, 0)
            with act.Fori(0, CHUNKS) as c:
                act.wait_ge(xT_banked, 2 * c + 2)
                for kc in range(KC):
                    last = nc.scalar.activation(sh.xT[:, kc, :], A[:, kc, :], ACT.Copy, scale=cols[:, kc, 12:13])
                    if kc == KC - 1:
                        last.then_inc(xT_ready, 2)
                for a, bank in enumerate((Bk, C, E)):
                    act.wait_ge(proj_done, 3 * c + a + 1)
                    act.wait_ge(conv_ready, 3 * c + a)
                    for m in range(KC):
                        last = nc.scalar.activation(raw[:, a, m, :, TAPS - 1:TAPS - 1 + S],
                                                    bank[:, m, :].rearrange("p (b t) -> p b t", b=SEQS), ACT.Copy)
                    last.then_inc(raw_ready, 1)
                silu(c, 0)
                silu(c, 1)
                act.wait_ge(g_done, c + 1)
                nc.scalar.activation(flat(gate[:, :, :]), A[:, :, :].rearrange("p a t -> p (a t)"), ACT.Silu).then_inc(g_ready, 1)
                silu(c, 2)
                act.wait_ge(v_turned, c + 1)
                nc.scalar.activation(flat(v[:, :, :]), E[:, :, :].rearrange("p a t -> p (a t)"), ACT.Copy).then_inc(v_ready, 1)
                act.wait_ge(o_done, c + 1)
                act.wait_ge(ms_ready, 3 * c + 1)
                nc.scalar.activation(flat(square[:, :, :]), E[:, :, :].rearrange("p a t -> p (a t)"), ACT.Square).then_inc(sq_done, 1)
                act.wait_ge(turned_done, 4 * c + 2)
                nc.scalar.activation(featT[:, :, :].rearrange("p k t -> p (k t)"),
                                     Bk[:, :, :].rearrange("p a t -> p (a t)"), ACT.Copy).then_inc(turned_ready, 1)
                act.wait_ge(h_ready, c + 1)
                squares_of(hh, 2, 3 * c + 2)
                act.wait_ge(turned_done, 4 * c + 4)
                for kc in range(KC):
                    last = nc.scalar.activation(featT[:, kc, :], Bk[:, kc, :], ACT.Copy, scale=cols[:, kc, 13:14])
                last.then_inc(turned_ready, 1)
                act.wait_ge(xn_ready, c + 1)
                squares_of(sh.xn, 0, 3 * c + 3)
                for t, bank in enumerate((A, Bk, C)):
                    act.wait_ge(gate_done, c * MT + t + 1)
                    nc.scalar.activation(act_g[:, t, :], bank[:, 0, :], ACT.Silu).then_inc(act_ready, 1)

        @block.gpsimd
        def _(pool):
            nc.gpsimd.memset(raw[:, :, :, :, :].rearrange("p a m b t -> p (a m b t)"), 0.0).then_inc(init, 1)
            pool.wait_ge(w_in[3], 16)

            def root(n, width):
                pool.wait_ge(ms_ready, n)
                nc.gpsimd.tensor_tensor(rr[:, 0:width], ms[:, 0:width], sh.minus_half[:, 0:width], ALU.pow).then_inc(r_ready, 1)

            root(1, CT)
            with pool.Fori(0, CHUNKS) as c:
                for a in range(2):
                    pool.wait_ge(silu_ready, 3 * c + a + 1)
                    for m in range(KC):
                        for b in range(SEQS):
                            last = nc.gpsimd.tensor_tensor(turned[:, a, m, b * S:(b + 1) * S], qkv[:, a, m, b * S:(b + 1) * S],
                                                           rope[:, 0, :], ALU.mult)
                    last.then_inc(cosed, 1)
                root(3 * c + 2, CT * H)
                root(3 * c + 3, CT)
                root(3 * c + 4, CT)
                pool_rstd(nc, sh, pool, c, var_ready, rstd_ready)

        @block.vector
        def _(dve):
            LINKS = 3 * KC * (TAPS - 1) + 8 + STATS_LINKS

            def mean_square(chain, n, width, count, wait=True):
                nc.vector.tensor_scalar(ms[:, 0:width], ms[:, 0:width] if width > CT else squares[:, :], 1.0 / count, EPS,
                                        ALU.mult, ALU.add).then_inc(ms_ready, 1)
                if wait:
                    dve.wait_ge(r_ready, n)

            def scale_rows(src):
                for j in range(CT):
                    last = nc.vector.tensor_scalar(normal[:, j, :], src[:, j, :], rr[:, j:j + 1], None, ALU.mult)
                last.then_inc(normed, 1)

            dve.wait_ge(sq_done, 1)
            mean_square(None, 1, CT, D)
            scale_rows(sh.xn)
            for in_ in w_in[:6]:
                dve.wait_ge(in_, 16)
            with dve.Fori(0, CHUNKS) as c:
                chain = Chain(dve, own, c * LINKS, LINKS)
                for a in range(3):
                    dve.wait_ge(raw_ready, 3 * c + a + 1)
                    for i in range(TAPS):
                        for m in range(KC):
                            tap = cols[:, m, a * TAPS + i:a * TAPS + i + 1]
                            shifted = raw[:, a, m, :, i:i + S]
                            if i == 0:
                                ins = nc.vector.tensor_scalar(conv[:, a, m, :, :], shifted, tap, None, ALU.mult)
                            else:
                                ins = nc.vector.scalar_tensor_tensor(out=conv[:, a, m, :, :], in0=shifted, scalar=tap,
                                                                     in1=conv[:, a, m, :, :], op0=ALU.mult, op1=ALU.add)
                            if i < TAPS - 1:
                                chain.mark(ins)
                        if i < TAPS - 1:
                            chain.wait()
                    ins.then_inc(conv_ready, 1)
                for a, bank in enumerate((Bk, C)):
                    dve.wait_ge(swap_done, 2 * c + a + 1)
                    for m in range(KC):
                        ins = nc.vector.tensor_tensor(
                            sines[:, m, :].rearrange("p (b t) -> p b t", b=SEQS),
                            bank[:, m, :].rearrange("p (b t) -> p b t", b=SEQS),
                            rope[:, 1, :].rearrange("p (a t) -> p a t", a=1).broadcast_to([P, SEQS, S]), ALU.mult)
                        chain.mark(ins)
                    chain.wait()
                    dve.wait_ge(cosed, 2 * c + a + 1)
                    nc.vector.tensor_tensor(turned[:, a, :, :].rearrange("p m t -> p (m t)"),
                                            turned[:, a, :, :].rearrange("p m t -> p (m t)"),
                                            sines[:, :, :].rearrange("p m t -> p (m t)"), ALU.add).then_inc(rot_ready, 1)
                    dve.wait_ge(rot_ready, 2 * c + a + 1)
                for h in range(H):
                    dve.wait_ge(a_done, c * H + h + 1)
                    bank = (Bk, C)[h % 2]
                    for b in range(SEQS):
                        nc.vector.tensor_tensor(ad[:, h % 2, b, 0:S], bank[:, b, 0:S], decay[:, h, :], ALU.mult)
                        last = nc.vector.tensor_tensor(ad[:, h % 2, b, S:CAUSAL], bank[:, b, S:CAUSAL],
                                                       decay[:, h, 0:P], ALU.mult)
                    last.then_inc(a_ready, 1)
                dve.wait_ge(g_ready, c + 1)
                chain.mark(nc.vector.tensor_tensor(gate[:, :, :], gate[:, :, :],
                                                   gnw[:, :].rearrange("p (a e) -> p a e", a=1).broadcast_to([P, CT, D]),
                                                   ALU.mult))
                dve.wait_ge(sq_done, 3 * c + 2)
                chain.link(nc.vector.tensor_reduce(ms[:, :], flat(square[:, :, :]).rearrange("p (g e) -> p g e", e=DK),
                                                   AX, ALU.add))
                mean_square(chain, 3 * c + 2, CT * H, DK, wait=False)
                chain.link(nc.vector.tensor_tensor(flat(og[:, :, :]), E[:, :, :].rearrange("p a t -> p (a t)"),
                                                   flat(gate[:, :, :]), ALU.mult))
                dve.wait_ge(r_ready, 3 * c + 2)
                nc.vector.tensor_tensor(
                    flat(og[:, :, :]).rearrange("p (g e) -> p g e", e=DK),
                    flat(og[:, :, :]).rearrange("p (g e) -> p g e", e=DK),
                    rr[:, :].rearrange("p (g a) -> p g a", a=1).broadcast_to([P, CT * H, DK]), ALU.mult).then_inc(og_ready, 1)
                dve.wait_ge(wo_done, c + 1)
                nc.vector.tensor_tensor(hh[:, :, :], sh.xn[:, :, :], token(C), ALU.add).then_inc(h_ready, 1)
                dve.wait_ge(sq_done, 3 * c + 3)
                dve.wait_ge(h_ready, c + 1)
                mean_square(chain, 3 * c + 3, CT, D)
                scale_rows(hh)
                dve_normalise(nc, sh, c + 1, xn_ready)
                for t, bank in enumerate((A, Bk, C)):
                    dve.wait_ge(act_ready, c * MT + t + 1)
                    nc.vector.tensor_tensor(act_g[:, t, :], act_g[:, t, :], bank[:, 1, :], ALU.mult).then_inc(hidden_ready, 1)
                dve.wait_ge(sq_done, 3 * c + 4)
                mean_square(chain, 3 * c + 4, CT, D)
                dve.wait_ge(turned_done, 4 * c + 4)
                scale_rows(sh.xn)
                dve.wait_ge(down_done, c + 1)
                chain.link(nc.vector.tensor_tensor(hh[:, :, :], hh[:, :, :], token(E), ALU.add))
                dve_add_residual(nc, sh, dve, c, hh, out_used, kept)
                dve_stats(nc, sh, dve, c, sh.fresh, chain, var_ready, rstd_ready, kept)
                chain.done()
            dve_first_normalised(nc, sh, dve, xn_ready, kept, CHUNKS)


def l1_attention_block(nc, sh):
    d = sh.dram
    H, DH, M, R = 16, 128, 64, 16
    CLAMP, EPS = 32.0, 1e-5
    RA = R + 1
    s = lambda name: sh.sem(f"a1_{name}")
    const_in = [s(f"const_in{i}") for i in range(3)]
    gn_in = s("gn_in")
    w_in = [s(f"w_in{i}") for i in range(2)]
    wo_in = [s(f"wo_in{i}") for i in range(2)]
    xn_ready, xT_banked, xT_ready = s("xn_ready"), s("xT_banked"), s("xT_ready")
    x_low, w_high, w_low = s("x_low"), s("w_high"), s("w_low")
    low_done, low_ready, init = s("low_done"), s("low_ready"), s("init")
    q_done, k_done, v_done, g_done = s("q_done"), s("k_done"), s("v_done"), s("g_done")
    qk_cosed, qk_swapped, qk_sined, qk_ready = s("qk_cosed"), s("qk_swapped"), s("qk_sined"), s("qk_ready")
    v_ready, tanh_ready, g_ready = s("v_ready"), s("tanh_ready"), s("g_ready")
    slot_done, slot_clipped, es_ready = s("slot_done"), s("slot_clipped"), s("es_ready")
    esT_done, esT_ready = s("esT_done"), s("esT_ready")
    sum_done, enz_ready = s("sum_done"), s("enz_ready")
    a_done, a_ready, ok_done, ok_read = s("a_done"), s("a_ready"), s("ok_done"), s("ok_read")
    shifted, exps_done, w_ready = s("shifted"), s("exps_done"), s("w_ready")
    wT_done, wT_ready, w2_done, w2_ready = s("wT_done"), s("wT_ready"), s("w2_done"), s("w2_ready")
    o_done, squares_done, ms_ready, rms_ready, og_ready = (
        s("o_done"), s("squares_done"), s("ms_ready"), s("rms_ready"), s("og_ready"))
    oT_done, oT_ready, wo_done = s("oT_done"), s("oT_ready"), s("wo_done")
    out_used, kept, own, var_ready, rstd_ready = s("out_used"), s("kept"), s("own"), s("var"), s("rstd")

    with ExitStack() as ctx:
        sb = lambda name, shape, dt=F32: ctx.enter_context(nc.sbuf_tensor(f"a1_{name}", shape, dt))
        ps = lambda name, shape: ctx.enter_context(nc.psum_tensor(f"a1_{name}", shape, F32))
        w = sb("w", [P, 2, 4 * D + M])
        w_h, w_l = sb("w_h", [P, 2, 2 * D], F32R), sb("w_l", [P, 2, 2 * D], F32R)
        x_h, x_l = sb("x_h", [P, KC, N], F32R), sb("x_l", [P, KC, N], F32R)
        wo = sb("wo", [P, 2, D])
        ws1 = sb("ws1", [P, KC, R])
        rope = sb("rope", [P, 2, S])
        masks = sb("masks", [P, 2, CAUSAL])
        ones = sb("ones", [P, P])
        gn = sb("gn", [P, 1])
        gn_half = sb("gn_half", [P, 1])
        low = sb("low", [RA, N])
        qk = sb("qk", [P, 2, N])
        cosed = sb("cosed", [P, 2, N])
        swapped = sb("swapped", [P, 2, N])
        v = sb("v", [P, 2, CT, DH])
        tanh = sb("tanh", [P, N])
        gate = sb("gate", [P, 2, CT, DH])
        slot_in = sb("slot_in", [P, CT, M])
        es = sb("es", [P, CT, M])
        esT = sb("esT", [M, 2, N])
        enz = sb("enz", [P, CT, M])
        a = sb("a", [P, SEQS, CAUSAL])
        ok = sb("ok", [P, CT, M])
        top = sb("top", [P, CT])
        exps = sb("exps", [P, CT, M])
        total, inv = sb("total", [P, CT]), sb("inv", [P, CT])
        slot_w = sb("slot_w", [P, CT, M])
        wT = sb("wT", [M, N])
        w2 = sb("w2", [P, SEQS, CAUSAL])
        square = sb("square", [P, CT, DH])
        squares, ms, rms = sb("squares", [P, CT]), sb("ms", [P, CT]), sb("rms", [P, CT])
        og = sb("og", [P, CT, DH])
        oT = sb("oT", [P, 2, N])
        pair = ps("pair", [P, 2, N])
        vb, gb = ps("v_bank", [P, N]), ps("g_bank", [P, N])
        ab = ps("a_bank", [P, 2, N])
        out = ps("out", [P, CT, D])
        okb = ab[:, 0, 0:CT * M].rearrange("p (j m) -> p j m", j=CT)
        slotb = ab[:, 0, CT * M:2 * CT * M].rearrange("p (j m) -> p j m", j=CT)
        sumb = gb[:, 0:CT * M].rearrange("p (j m) -> p j m", j=CT)
        wTb = esTb = ab[0:M, 1, :]
        ob = vb
        oTb = gb
        block = ctx.enter_context(nc.Block())
        HH = H // 2

        @block.sync
        def _(sp):
            def load_w(h, i):
                sp.dma_start(w[:, i, :], d["a1_w"][bass.ds(h, 1), :, 0:4 * D + M]
                             .rearrange("a p m -> (a p) m")).then_inc(w_in[i], 16)

            def load_wo(h, i):
                sp.dma_start(wo[:, i, :], d["a1_w"][bass.ds(h, 1), :, 4 * D + M:5 * D + M]
                             .rearrange("a p m -> (a p) m")).then_inc(wo_in[i], 16)

            sp.dma_start(ws1[:, :, :], d["a1_ws1"]).then_inc(const_in[0], 16)
            stream_late(sp, H, (slot_done,), load_w, wo_done, load_wo)

        @block.tensor
        def _(pe):
            part = lambda w_, i, a_, kc: w_[:, i, a_ * D + kc * P:a_ * D + (kc + 1) * P]

            def project_qk(c, k2, i):
                n = c * H + 2 * k2 + i
                pe.wait_ge(w_low, n + 1)
                for a_, done in ((0, q_done), (1, k_done)):
                    for kc in range(KC):
                        last = pe_three(nc, pair[:, a_, :], (part(w_h, i, a_, kc), x_h[:, kc, :]),
                                        (part(w_l, i, a_, kc), x_l[:, kc, :]), kc == 0, kc == KC - 1)
                    last.then_inc(done, 1)

            def project_tokens(c, k2, i, a_, bank, done, then=None):
                for j in range(CT):
                    if then and j == CT - 1:
                        pe.wait_ge(*then)
                    for kc in range(KC):
                        last = nc.tensor.matmul(bank[:, j * DH:(j + 1) * DH], sh.xT[:, kc, j * P:(j + 1) * P],
                                                part(w, i, a_, kc), start=kc == 0, stop=kc == KC - 1)
                last.then_inc(done, 1)

            def slots(c, k2, i):
                pe.wait_ge(ok_read, c * H + 2 * k2 + i)
                for j in range(CT):
                    last = nc.tensor.matmul(slotb[:, j, :], low[:, j * P:(j + 1) * P], w[0:RA, i, 4 * D:4 * D + M],
                                            start=True, stop=True, skip_group_check=True)
                last.then_inc(slot_done, 1)

            def turn_es(c, k2, i):
                for j in range(CT):
                    last = nc.tensor.transpose(esTb[:, j * P:(j + 1) * P], es[:, j, :], sh.ident[:, :])
                last.then_inc(esT_done, 1)

            def slot_sums(c, k2, i):
                n = c * H + 2 * k2 + i
                pe.wait_ge(es_ready, n + 1)
                pe.wait_ge(g_ready, n + 1)
                nc.tensor.matmul(sumb, masks[:, 1, 0:P], es[:, :, :], start=True, stop=False, skip_group_check=True)
                nc.tensor.matmul(sumb[:, 1:CT:2, :], ones[:, :], es[:, 0:CT:2, :], start=False, stop=True,
                                 skip_group_check=True).then_inc(sum_done, 1)

            def scores(c, k2, i):
                n = c * H + 2 * k2 + i
                pe.wait_ge(qk_ready, 2 * (n + 1))
                pe.wait_ge(slot_clipped, n + 1)
                pe.wait_ge(esT_ready, n + 1)
                for b in range(SEQS):
                    for kb in range(2):
                        t0 = b * S
                        last = nc.tensor.matmul(ab[:, b, kb * S:kb * S + S - kb * P],
                                                qk[:, 1, t0 + kb * P:t0 + (kb + 1) * P], qk[:, 0, t0 + kb * P:t0 + S],
                                                start=True, stop=True, skip_group_check=True)
                last.then_inc(a_done, 1)

            def key_block(t, b, half, kb):
                c0 = half * P if kb == 0 else S
                return t[:, b, c0:c0 + P]

            def ok_products(c, k2, i, then):
                pe.wait_ge(a_ready, c * H + 2 * k2 + i + 1)
                for b in range(SEQS):
                    for half in range(2):
                        for kb in range(half + 1):
                            if b == SEQS - 1 and kb:
                                for wait in then:
                                    pe.wait_ge(*wait)
                            last = nc.tensor.matmul(okb[:, 2 * b + half, :], key_block(a, b, half, kb), es[:, 2 * b + kb, :],
                                                    start=kb == 0, stop=kb == half, skip_group_check=True)
                last.then_inc(ok_done, 1)

            def turn_w(c, k2, i):
                n = c * H + 2 * k2 + i
                for j in range(CT):
                    last = nc.tensor.transpose(wTb[:, j * P:(j + 1) * P], slot_w[:, j, :], sh.ident[:, :])
                last.then_inc(wT_done, 1)

            def w2_products(c, k2, i, swapped_by):
                n = c * H + 2 * k2 + i
                pe.wait_ge(wT_ready, n + 1)
                pe.wait_ge(esT_ready, n + 1)
                pe.wait_ge(qk_swapped, swapped_by)
                for b in range(SEQS):
                    for kb in range(2):
                        t0 = b * S
                        last = nc.tensor.matmul(pair[:, b, kb * S:kb * S + S - kb * P],
                                                esT[:, i, t0 + kb * P:t0 + (kb + 1) * P], wT[:, t0 + kb * P:t0 + S],
                                                start=True, stop=True, skip_group_check=True)
                last.then_inc(w2_done, 1)

            def o_products(c, k2, i, v_taken):
                n = c * H + 2 * k2 + i
                pe.wait_ge(w2_ready, n + 1)
                pe.wait_ge(v_ready, v_taken)
                for b in range(SEQS):
                    for half in range(2):
                        j = 2 * b + half
                        for kb in range(half + 1):
                            last = nc.tensor.matmul(ob[:, j * DH:(j + 1) * DH], key_block(w2, b, half, kb),
                                                    v[:, i, 2 * b + kb, :], start=kb == 0, stop=kb == half,
                                                    skip_group_check=True)
                last.then_inc(o_done, 1)

            def turn_o(c, k2, i):
                for j in range(CT):
                    last = nc.tensor.transpose(oTb[:, j * P:(j + 1) * P], og[:, j, :], sh.ident[:, :])
                last.then_inc(oT_done, 1)

            def output(c, k2, i, first=False, last_head=False):
                n = c * H + 2 * k2 + i
                pe.wait_ge(wo_in[i], 16 * (c * HH + k2 + 1))
                pe.wait_ge(oT_ready, n + 1)
                if first:
                    pe.wait_ge(out_used, c)
                for j in range(CT):
                    last = nc.tensor.matmul(out[:, j, :], oT[:, i, j * P:(j + 1) * P], wo[:, i, :],
                                            start=first and j % 2 == 0, stop=last_head, skip_group_check=True)
                last.then_inc(wo_done, 1)

            def head(c, k2, i, following=None, before=None, first=False):
                n = c * H + 2 * k2 + i
                scores(c, k2, i)
                if following:
                    project_qk(c, *following)
                ok_products(c, k2, i, [(og_ready, n), (enz_ready, n + 1)] if before else [(enz_ready, n + 1)])
                if before:
                    turn_o(c, *before)
                if following:
                    project_tokens(c, *following, 2, vb, v_done)
                if before:
                    output(c, *before, first=first)
                if following:
                    project_tokens(c, *following, 3, gb, g_done, then=(w_ready, n + 1))
                    turn_w(c, k2, i)
                    slots(c, *following)
                else:
                    pe.wait_ge(w_ready, n + 1)
                    nc.tensor.matmul(pair[:, 0, 0:P], sh.ident[:, :], sh.ident[:, :], start=True, stop=True)
                    turn_w(c, k2, i)
                w2_products(c, k2, i, 2 * (n + 2 if following else n + 1))
                if following:
                    slot_sums(c, *following)
                    turn_es(c, *following)
                o_products(c, k2, i, n + 2 if following else n + 1)

            pe.wait_ge(init, 2)
            with pe.Fori(0, CHUNKS) as c:
                pe.wait_ge(xn_ready, c)
                pe.wait_ge(w2_ready, c * H)
                pe_features(nc, sh.xn, sh.ident, (pair[:, 0, :], pair[:, 1, :]), xT_banked)
                pe.wait_ge(xT_ready, 2 * (c + 1))
                for in_ in const_in:
                    pe.wait_ge(in_, 16)
                for kc in range(KC):
                    last = nc.tensor.matmul(vb[0:R, :], ws1[:, kc, :], sh.xT[:, kc, :], start=kc == 0, stop=kc == KC - 1)
                last.then_inc(low_done, 1)
                pe.wait_ge(x_low, c + 1)
                project_qk(c, 0, 0)
                project_tokens(c, 0, 0, 3, gb, g_done)
                pe.wait_ge(low_ready, c + 1)
                project_tokens(c, 0, 0, 2, vb, v_done)
                pe.wait_ge(w_in[0], 16)
                slots(c, 0, 0)
                slot_sums(c, 0, 0)
                turn_es(c, 0, 0)
                head(c, 0, 0, following=(0, 1))
                head(c, 0, 1, following=(1, 0), before=(0, 0), first=True)
                with pe.Fori(1, HH - 1) as k2:
                    head(c, k2, 0, following=(k2, 1), before=(k2 - 1, 1))
                    head(c, k2, 1, following=(k2 + 1, 0), before=(k2, 0))
                head(c, HH - 1, 0, following=(HH - 1, 1), before=(HH - 2, 1))
                head(c, HH - 1, 1, before=(HH - 1, 0))
                pe.wait_ge(og_ready, (c + 1) * H)
                nc.tensor.matmul(pair[:, 0, 0:P], sh.ident[:, :], sh.ident[:, :], start=True, stop=True)
                turn_o(c, HH - 1, 1)
                output(c, HH - 1, 1, last_head=True)

        @block.scalar
        def _(act):
            act.dma_start(rope[:, :, :], d["a1_rope"]).then_inc(const_in[1], 16)
            act.dma_start(masks[:, :, :], d["a1_masks"]).then_inc(const_in[2], 16)

            def take_qk(c, k2, i):
                n = c * H + 2 * k2 + i
                act.wait_ge(qk_ready, 2 * n)
                for a_ in range(2):
                    act.wait_ge(qk_cosed, 2 * n + a_ + 1)
                    nc.scalar.activation(swapped[0:64, a_, :], pair[64:P, a_, :], ACT.Copy)
                    nc.scalar.activation(swapped[64:P, a_, :], pair[0:64, a_, :], ACT.Copy).then_inc(qk_swapped, 1)

            def take_v(c, k2, i):
                n = c * H + 2 * k2 + i
                act.wait_ge(v_done, n + 1)
                nc.scalar.activation(v[:, i, :, :].rearrange("p j e -> p (j e)"), vb[:, :], ACT.Copy).then_inc(v_ready, 1)

            def tanh_g(c, k2, i):
                n = c * H + 2 * k2 + i
                act.wait_ge(g_done, n + 1)
                act.wait_ge(g_ready, n)
                nc.scalar.activation(tanh[:, :], gb[:, :], ACT.Tanh, scale=0.5).then_inc(tanh_ready, 1)

            def exp_slots(c, k2, i):
                n = c * H + 2 * k2 + i
                act.wait_ge(slot_clipped, n + 1)
                act.wait_ge(ok_done, n)
                nc.scalar.activation(es[:, :, :], slot_in[:, :, :], ACT.Exp).then_inc(es_ready, 1)
                act.wait_ge(esT_done, n + 1)
                nc.scalar.activation(esT[:, i, :], esTb, ACT.Copy).then_inc(esT_ready, 1)

            def high(c, k2, i):
                act.wait_ge(w_in[i], 16 * (c * HH + k2 + 1))
                nc.scalar.activation(w_h[:, i, :], w[:, i, 0:2 * D], ACT.Copy).then_inc(w_high, 1)

            def softmax(c, k2, i):
                n = c * H + 2 * k2 + i
                act.wait_ge(shifted, n + 1)
                nc.scalar.activation(exps[:, :, :], ok[:, :, :], ACT.Exp).then_inc(exps_done, 1)

            def take_wT(c, k2, i):
                n = c * H + 2 * k2 + i
                act.wait_ge(wT_done, n + 1)
                nc.scalar.activation(wT[:, :], wTb, ACT.Copy).then_inc(wT_ready, 1)

            def square_o(c, k2, i):
                n = c * H + 2 * k2 + i
                act.wait_ge(o_done, n + 1)
                act.wait_ge(ms_ready, n)
                for j in range(CT):
                    last = nc.scalar.activation(square[:, j, :], ob[:, j * DH:(j + 1) * DH], ACT.Square,
                                                accum_out=squares[:, j:j + 1])
                last.then_inc(squares_done, 1)

            def take_oT(c, k2, i):
                act.wait_ge(oT_done, c * H + 2 * k2 + i + 1)
                nc.scalar.activation(oT[:, i, :], oTb[:, :], ACT.Copy, scale=gn_half[:, 0:1]).then_inc(oT_ready, 1)

            def head(c, k2, i, following=None, before=None, weights=None):
                if before:
                    square_o(c, *before)
                    take_oT(c, *before)
                if following:
                    take_qk(c, *following)
                softmax(c, k2, i)
                if following:
                    take_v(c, *following)
                if weights:
                    high(c, *weights)
                if following:
                    tanh_g(c, *following)
                take_wT(c, k2, i)
                if following:
                    exp_slots(c, *following)

            act.wait_ge(init, 3)
            with act.Fori(0, CHUNKS) as c:
                high(c, 0, 0)
                for kc in range(KC):
                    act.wait_ge(xT_banked, 2 * c + kc + 1)
                    nc.scalar.activation(sh.xT[:, kc, :], pair[:, kc, :], ACT.Copy)
                    nc.scalar.activation(x_h[:, kc, :], pair[:, kc, :], ACT.Copy).then_inc(xT_ready, 1)
                high(c, 0, 1)
                act.wait_ge(low_done, c + 1)
                nc.scalar.activation(low[0:R, :], vb[0:R, :], ACT.Copy).then_inc(low_ready, 1)
                take_qk(c, 0, 0)
                tanh_g(c, 0, 0)
                take_v(c, 0, 0)
                exp_slots(c, 0, 0)
                head(c, 0, 0, following=(0, 1), weights=(1, 0))
                head(c, 0, 1, following=(1, 0), before=(0, 0), weights=(1, 1))
                with act.Fori(1, HH - 1) as k2:
                    head(c, k2, 0, following=(k2, 1), before=(k2 - 1, 1), weights=(k2 + 1, 0))
                    head(c, k2, 1, following=(k2 + 1, 0), before=(k2, 0), weights=(k2 + 1, 1))
                head(c, HH - 1, 0, following=(HH - 1, 1), before=(HH - 2, 1))
                head(c, HH - 1, 1, before=(HH - 1, 0))
                square_o(c, HH - 1, 1)
                take_oT(c, HH - 1, 1)

        @block.gpsimd
        def _(pool):
            pool.dma_start(gn[:, :], d["a1_gn"]).then_inc(gn_in, 16)
            nc.gpsimd.memset(low[:, :], 1.0).then_inc(init, 1)
            nc.gpsimd.memset(ones[:, :], 1.0).then_inc(init, 1)
            pool.wait_ge(gn_in, 16)
            nc.gpsimd.tensor_scalar(gn_half[:, :], gn[:, :], 0.5, 1.0, ALU.mult, ALU.mult).then_inc(init, 1)
            pool.wait_ge(const_in[1], 16)

            def rotate(c, n):
                for a_ in range(2):
                    pool.wait_ge(qk_swapped, 2 * n + a_ + 1)
                    for b in range(SEQS):
                        last = nc.gpsimd.tensor_tensor(swapped[:, a_, b * S:(b + 1) * S], swapped[:, a_, b * S:(b + 1) * S],
                                                       rope[:, 1, :], ALU.mult)
                    last.then_inc(qk_sined, 1)

            def rms_step(c, n):
                pool.wait_ge(ms_ready, n + 1)
                nc.gpsimd.tensor_tensor(rms[:, :], ms[:, :], sh.minus_half[:, 0:CT], ALU.pow).then_inc(rms_ready, 1)

            def low_w(n, i):
                pool.wait_ge(w_high, n + 1)
                pool_low(nc, w[:, i, 0:2 * D], w_h[:, i, :], w_l[:, i, :]).then_inc(w_low, 1)

            def low_x(c):
                pool.wait_ge(xT_ready, 2 * c + 2)
                pool_low(nc, sh.xT[:, :, :], x_h[:, :, :], x_l[:, :, :]).then_inc(x_low, 1)

            def chunk(c, last=False):
                low_w(c * H + 1, 1)
                rotate(c, c * H)
                rotate(c, c * H + 1)
                with pool.Fori(0, HH - 1) as k2:
                    for i in range(2):
                        n = c * H + 2 * k2 + i
                        low_w(n + 2, i)
                        rms_step(c, n)
                        rotate(c, n + 2)
                rms_step(c, c * H + H - 2)
                rms_step(c, c * H + H - 1)
                if not last:
                    low_w((c + 1) * H, 0)
                    low_x(c + 1)
                pool_rstd(nc, sh, pool, c, var_ready, rstd_ready)

            low_w(0, 0)
            low_x(0)
            with pool.Fori(0, CHUNKS - 1) as c:
                chunk(c)
            chunk(CHUNKS - 1, last=True)

        @block.vector
        def _(dve):
            def both(v_):
                return v_.rearrange("p (a t) -> p a t", a=1).broadcast_to([P, SEQS, v_.shape[-1]])

            def wide(v_, n_):
                return v_.rearrange("p (j a) -> p j a", a=1).broadcast_to([P, CT, n_])

            def cos_qk(c, n):
                for a_, done in ((0, q_done), (1, k_done)):
                    dve.wait_ge(done, n + 1)
                    nc.vector.tensor_tensor(cosed[:, a_, :].rearrange("p (b t) -> p b t", b=SEQS),
                                            pair[:, a_, :].rearrange("p (b t) -> p b t", b=SEQS),
                                            both(rope[:, 0, :]), ALU.mult).then_inc(qk_cosed, 1)

            def sum_qk(c, n):
                for a_ in range(2):
                    dve.wait_ge(qk_cosed, 2 * n + a_ + 1)
                    dve.wait_ge(qk_sined, 2 * n + a_ + 1)
                    nc.vector.tensor_tensor(qk[:, a_, :], cosed[:, a_, :], swapped[:, a_, :], ALU.add).then_inc(qk_ready, 1)

            def take_g(c, n, i):
                dve.wait_ge(tanh_ready, n + 1)
                nc.vector.scalar_tensor_tensor(out=gate[:, i, :, :].rearrange("p j e -> p (j e)"), in0=tanh[:, :], scalar=1.0,
                                               in1=gb[:, :], op0=ALU.add, op1=ALU.mult).then_inc(g_ready, 1)

            def take_slots(c, n):
                dve.wait_ge(slot_done, n + 1)
                dve.wait_ge(es_ready, n)
                nc.vector.tensor_scalar(slot_in[:, :, :], slotb, CLAMP, -CLAMP, ALU.min, ALU.max).then_inc(slot_clipped, 1)

            def take_sums(c, n):
                dve.wait_ge(sum_done, n + 1)
                nc.vector.reciprocal(enz[:, :, :], sumb).then_inc(enz_ready, 1)

            def masked(c, n, bank, dst, mask, done, ready):
                dve.wait_ge(done, n + 1)
                nc.vector.tensor_tensor(dst[:, :, :], bank[:, :, 0:CAUSAL], both(masks[:, mask, :]), ALU.mult).then_inc(ready, 1)

            HEAD_LINKS = 4

            def slot_softmax(c, n, chain):
                dve.wait_ge(ok_done, n + 1)
                dve.wait_ge(enz_ready, n + 1)
                nc.vector.tensor_tensor(ok[:, :, :], okb, enz[:, :, :], ALU.mult).then_inc(ok_read, 1)
                dve.wait_ge(ok_read, n + 1)
                chain.link(nc.vector.tensor_reduce(top[:, :], ok[:, :, :], AX, ALU.max))
                nc.vector.tensor_tensor(ok[:, :, :], ok[:, :, :], wide(top[:, :], M), ALU.subtract).then_inc(shifted, 1)
                dve.wait_ge(exps_done, n + 1)
                chain.link(nc.vector.tensor_reduce(total[:, :], exps[:, :, :], AX, ALU.add))
                chain.link(nc.vector.reciprocal(inv[:, :], total[:, :]))
                chain.link(nc.vector.tensor_tensor(exps[:, :, :], exps[:, :, :], enz[:, :, :], ALU.mult))
                nc.vector.tensor_tensor(slot_w[:, :, :], exps[:, :, :], wide(inv[:, :], M), ALU.mult).then_inc(w_ready, 1)

            def mean_square(c, n):
                dve.wait_ge(squares_done, n + 1)
                nc.vector.tensor_scalar(ms[:, :], squares[:, :], 1.0 / DH, EPS, ALU.mult, ALU.add).then_inc(ms_ready, 1)

            def gate_o(c, n, i):
                dve.wait_ge(rms_ready, n + 1)
                dve.wait_ge(oT_done, n)
                for j in range(CT):
                    last = nc.vector.scalar_tensor_tensor(out=og[:, j, :], in0=ob[:, j * DH:(j + 1) * DH],
                                                          scalar=rms[:, j:j + 1], in1=gate[:, i, j, :],
                                                          op0=ALU.mult, op1=ALU.mult)
                last.then_inc(og_ready, 1)

            def head(c, h, i, following=True, before=True):
                n = c * H + h
                chain = Chain(dve, own, c * LINKS + h * HEAD_LINKS, HEAD_LINKS)
                masked(c, n, ab, a, 0, a_done, a_ready)
                if before:
                    mean_square(c, n - 1)
                    gate_o(c, n - 1, 1 - i)
                if following:
                    cos_qk(c, n + 1)
                slot_softmax(c, n, chain)
                if following:
                    sum_qk(c, n + 1)
                    if before:
                        dve.wait_ge(og_ready, n)
                    take_g(c, n + 1, 1 - i)
                    take_slots(c, n + 1)
                masked(c, n, pair, w2, 1, w2_done, w2_ready)
                if following:
                    take_sums(c, n + 1)
                chain.done()

            LINKS = H * HEAD_LINKS + STATS_LINKS
            for in_ in const_in:
                dve.wait_ge(in_, 16)
            with dve.Fori(0, CHUNKS) as c:
                cos_qk(c, c * H)
                sum_qk(c, c * H)
                take_g(c, c * H, 0)
                take_slots(c, c * H)
                take_sums(c, c * H)
                head(c, 0, 0, before=False)
                head(c, 1, 1)
                with dve.Fori(1, HH - 1) as k2:
                    head(c, 2 * k2, 0)
                    head(c, 2 * k2 + 1, 1)
                head(c, H - 2, 0)
                head(c, H - 1, 1, following=False)
                mean_square(c, c * H + H - 1)
                gate_o(c, c * H + H - 1, 1)
                chain = Chain(dve, own, c * LINKS + H * HEAD_LINKS, STATS_LINKS)
                dve_normalise(nc, sh, c + 1, xn_ready)
                dve.wait_ge(wo_done, (c + 1) * H)
                dve_add_residual(nc, sh, dve, c, out, out_used, kept)
                dve_stats(nc, sh, dve, c, sh.fresh, chain, var_ready, rstd_ready, kept)
                chain.done()
            dve_first_normalised(nc, sh, dve, xn_ready, kept, CHUNKS)


def ssm_block(nc, sh):
    d = sh.dram
    NS, G, RN = 128, 4, 32
    SLOTS = 4
    EPS, FAR, LEAST = 1e-6, 1e25, 1e-22
    s = lambda name: sh.sem(f"ss_{name}")
    w_in = [s(f"w_in{i}") for i in range(7)]
    a_ready, bias_ready = s("a_ready"), s("bias_ready")
    xn_ready, sq_done, ms_ready, r_ready, normed = s("xn_ready"), s("sq_done"), s("ms_ready"), s("r_ready"), s("normed")
    turned, xT_ready, hsT_ready = s("turned"), s("xT_ready"), s("hsT_ready")
    select_done, mask_ready, xg_ready = s("select_done"), s("mask_ready"), s("xg_ready")
    proj_done, delta_ready, dt_done = s("proj_done"), s("delta_ready"), s("dt_done")
    dt_neg, dt_exp, dt_ln, dt_ready, u_ready = s("dt_neg"), s("dt_exp"), s("dt_ln"), s("dt_ready"), s("u_ready")
    split_ready = s("split_ready")
    packed_in = [s(f"packed_in{i}") for i in range(6)]
    rows_done, c_ready, decay_ready = s("rows_done"), s("c_ready"), s("decay_ready")
    dbu_ready, state_ready, hc_ready, added = s("dbu_ready"), s("state_ready"), s("hc_ready"), s("added")
    y_ready, proj_out, out_used, kept = s("y_ready"), s("proj_out"), s("out_used"), s("kept")
    own, var_ready, rstd_ready = s("own"), s("var"), s("rstd")

    with ExitStack() as ctx:
        sb = lambda name, shape, dt=F32: ctx.enter_context(nc.sbuf_tensor(f"ss_{name}", shape, dt))
        ps = lambda name, banks: ctx.enter_context(nc.psum_tensor(f"ss_{name}", [P, banks, N], F32))
        w_sel = sb("w_sel", [P, KC, D])
        w_xp = sb("w_xp", [P, KC, 3 * P])
        w_dt = sb("w_dt", [P, D])
        w_out = sb("w_out", [P, KC, D])
        onehot = sb("onehot", [3 * RN, RN, P], BF16)
        cols = sb("cols", [P, KC, 5])
        a_log = sb("a_log", [P, KC, NS])
        a_neg = sb("a_neg", [P, KC, NS])
        gated_bias = sb("gated_bias", [P, KC])
        square = sb("square", [P, CT, D])
        squares, ms, rr = sb("squares", [P, CT]), sb("ms", [P, CT]), sb("rr", [P, CT])
        normal = sb("normal", [P, CT, D])
        hsT = sb("hsT", [P, KC, N])
        mask = sb("mask", [P, KC, N])
        xg = sb("xg", [P, KC, N])
        delta = sb("delta", [P, N])
        z, e, w1, low = sb("z", [P, KC, N]), sb("e", [P, KC, N]), sb("w1", [P, KC, N]), sb("low", [P, KC, N])
        dt = sb("dt", [P, KC, N])
        u = sb("u", [P, KC, N])
        part = sb("part", [P, 2, 3, N], BF16)
        rest = sb("rest", [P, 2, N])
        packed = sb("packed", [3 * RN, 2, G, N], BF16)
        dbu = sb("dbu", [P, SLOTS, KC, N])
        decay = sb("decay", [P, 2, KC, N])
        crow = sb("crow", [P, 2, N])
        state = sb("state", [P, 2, KC, N])
        hc = sb("hc", [P, 2, KC, N])
        yT = sb("yT", [P, KC, N])
        rows = ps("rows", 4)
        spare = ps("spare", 2)
        y = ps("y", 2)
        out = spare[:, :, :].rearrange("p a t -> p (a t)").rearrange("p (j e) -> p j e", j=CT)
        flat = lambda t: t.rearrange("p k t -> p (k t)")
        block = ctx.enter_context(nc.Block())

        @block.sync
        def _(sp):
            for n_, (t, name) in enumerate(((cols, "ss_cols"), (a_log, "ss_a_log"), (w_sel, "ss_w_sel"), (w_xp, "ss_w_xp"))):
                sp.dma_start(t[:], d[name]).then_inc(w_in[n_], 16)
            with sp.Fori(0, CHUNKS) as c:
                for bc in range(2):
                    sp.wait_ge(split_ready, 2 * c + bc + 1)
                    for p in range(3):
                        for g in range(G):
                            sp.dma_start(packed[RN * p:RN * (p + 1), bc, g, :],
                                         part[RN * g:RN * (g + 1), bc, p, :]).then_inc(packed_in[3 * bc + p], 16)

        @block.tensor
        def _(pe):
            pe.sem_inc(added, 2)
            with pe.Fori(0, CHUNKS) as c:
                pe.wait_ge(normed, c + 1)
                pe_features(nc, normal, sh.ident, (rows[:, 0, :], rows[:, 1, :]), turned)
                pe.wait_ge(xT_ready, c + 1)
                pe.wait_ge(w_in[2], 16)
                for m in range(KC):
                    for kc in range(KC):
                        last = nc.tensor.matmul(rows[:, 2 + m, :], w_sel[:, kc, m * P:(m + 1) * P], sh.xT[:, kc, :],
                                                start=kc == 0, stop=kc == KC - 1)
                last.then_inc(select_done, 1)
                pe.wait_ge(out_used, c)
                pe_features(nc, sh.xn, sh.ident, (spare[:, 0, :], spare[:, 1, :]), turned)

                def project(m, bank):
                    for kc in range(KC):
                        last = nc.tensor.matmul(bank, w_xp[:, kc, m * P:(m + 1) * P], xg[:, kc, :],
                                                start=kc == 0, stop=kc == KC - 1)
                    last.then_inc(proj_done, 1)

                pe.wait_ge(xg_ready, c + 1)
                pe.wait_ge(y_ready, c)
                pe.wait_ge(w_in[3], 16)
                project(0, y[:, 0, :])
                project(1, rows[:, 0, :])
                pe.wait_ge(delta_ready, c + 1)
                pe.wait_ge(w_in[5], 16)
                for m in range(KC):
                    last = nc.tensor.matmul(rows[:, 2 + m, :], w_dt[:, m * P:(m + 1) * P], delta[:, :], start=True, stop=True)
                last.then_inc(dt_done, 1)
                project(2, rows[:, 1, :])
                pe.wait_ge(w_in[4], 16)
                pe.wait_ge(u_ready, c + 1)
                for in_ in packed_in:
                    pe.wait_ge(in_, 16 * G * (c + 1))

                def spread(g, k, i, first=False):
                    if not first:
                        pe.wait_ge(c_ready, c * NS + RN * g + 2 * k + i - 1)
                        pe.wait_ge(dbu_ready, c * NS + RN * g + 2 * k + i - 1)
                    for bc in range(2):
                        last = nc.tensor.matmul(rows[:, 2 * bc + i, :], onehot[:, bass.ds(2 * k + i, 1), :],
                                                packed[:, bc, bass.ds(g, 1), :], start=True, stop=True)
                    last.then_inc(rows_done, 1)

                def add(n, i, first=False, final=False):
                    pe.wait_ge(hc_ready, c * NS + n + 3)
                    for m in range(KC):
                        last = nc.tensor.matmul(y[:, m, :], sh.ident[:, :], hc[:, i, m, :], start=first, stop=final)
                    last.then_inc(added, 1)

                spread(0, 0, 0, first=True)
                spread(0, 0, 1, first=True)
                spread(0, 1, 0)
                spread(0, 1, 1)
                add(0, 0, first=True)
                with pe.Fori(2, RN // 2) as k:
                    for i in range(2):
                        spread(0, k, i)
                        add(2 * k + i - 3, 1 - i)
                with pe.Fori(1, G) as g:
                    with pe.Fori(0, RN // 2) as k:
                        for i in range(2):
                            spread(g, k, i)
                            add(RN * g + 2 * k + i - 3, 1 - i)
                add(NS - 3, 1)
                add(NS - 2, 0)
                add(NS - 1, 1, final=True)
                pe.wait_ge(y_ready, c + 1)
                pe.wait_ge(w_in[6], 16)
                for j in range(CT):
                    for kc in range(KC):
                        last = nc.tensor.matmul(out[:, j, :], yT[:, kc, j * P:(j + 1) * P], w_out[:, kc, :],
                                                start=kc == 0, stop=kc == KC - 1, skip_group_check=True)
                last.then_inc(proj_out, 1)

        @block.scalar
        def _(act):
            for n_, (t, name) in enumerate(((onehot, "ss_onehot"), (w_dt, "ss_w_dt"), (w_out, "ss_w_out"))):
                act.dma_start(t[:], d[name]).then_inc(w_in[4 + n_], 16)

            def squares_of_xn():
                for j in range(CT):
                    last = nc.scalar.activation(square[:, j, :], sh.xn[:, j, :], ACT.Square, accum_out=squares[:, j:j + 1])
                last.then_inc(sq_done, 1)

            act.wait_ge(w_in[1], 16)
            nc.scalar.activation(flat(a_neg[:, :, :]), flat(a_log[:, :, :]), ACT.Exp).then_inc(a_ready, 1)
            act.wait_ge(a_ready, 2)
            act.wait_ge(bias_ready, 1)
            squares_of_xn()
            with act.Fori(0, CHUNKS) as c:
                act.wait_ge(turned, 4 * c + 2)
                for kc in range(KC):
                    last = nc.scalar.activation(sh.xT[:, kc, :], rows[:, kc, :], ACT.Copy, scale=cols[:, kc, 0:1])
                last.then_inc(xT_ready, 1)
                act.wait_ge(select_done, c + 1)
                for m in range(KC):
                    last = nc.scalar.activation(mask[:, m, :], rows[:, 2 + m, :], ACT.Sigmoid, scale=cols[:, m, 2:3],
                                                bias=gated_bias[:, m:m + 1])
                last.then_inc(mask_ready, 1)
                act.wait_ge(proj_done, 3 * c + 1)
                nc.scalar.activation(delta[:, :], y[:, 0, :], ACT.Copy).then_inc(delta_ready, 1)
                act.wait_ge(dt_neg, c + 1)
                nc.scalar.activation(flat(e[:, :, :]), flat(e[:, :, :]), ACT.Exp).then_inc(dt_exp, 1)
                act.wait_ge(dt_ln, 3 * c + 1)
                nc.scalar.activation(flat(low[:, :, :]), flat(w1[:, :, :]), ACT.Ln).then_inc(dt_ln, 1)
                act.wait_ge(dt_ln, 3 * c + 2)
                nc.scalar.activation(flat(mask[:, :, :]), flat(low[:, :, :]), ACT.Exp, scale=-1.0).then_inc(dt_ln, 1)
                act.wait_ge(dt_ready, c + 1)

                def row(k, i, first=False):
                    n = c * NS + 2 * k + i
                    if not first:
                        act.wait_ge(state_ready, n - 1)
                    for m in range(KC):
                        last = nc.scalar.activation(decay[:, i, m, :], dt[:, m, :], ACT.Exp,
                                                    scale=a_neg[:, m, bass.ds(2 * k + i, 1)])
                    last.then_inc(decay_ready, 1)
                    act.wait_ge(hc_ready, n + 1)
                    act.wait_ge(rows_done, n + 1)
                    nc.scalar.activation(crow[:, i, :], rows[:, 2 + i, :], ACT.Copy).then_inc(c_ready, 1)

                row(0, 0, first=True)
                row(0, 1, first=True)
                with act.Fori(1, NS // 2) as k:
                    for i in range(2):
                        row(k, i)
                act.wait_ge(xn_ready, c + 1)
                act.wait_ge(ms_ready, c + 1)
                squares_of_xn()

        @block.gpsimd
        def _(pool):
            pool.sem_inc(hc_ready, 2)

            def root(n):
                pool.wait_ge(ms_ready, n)
                nc.gpsimd.tensor_tensor(rr[:, :], ms[:, :], sh.minus_half[:, 0:CT], ALU.pow).then_inc(r_ready, 1)

            root(1)
            with pool.Fori(0, CHUNKS) as c:
                with pool.Fori(0, NS // 2) as k:
                    for i in range(2):
                        n = c * NS + 2 * k + i
                        pool.wait_ge(state_ready, n + 1)
                        pool.wait_ge(c_ready, n + 1)
                        pool.wait_ge(added, n + 1)
                        nc.gpsimd.tensor_tensor(hc[:, i, :, :], state[:, i, :, :],
                                                crow[:, i, :].rearrange("p (a t) -> p a t", a=1).broadcast_to([P, KC, N]),
                                                ALU.mult).then_inc(hc_ready, 1)
                root(c + 2)
                pool_rstd(nc, sh, pool, c, var_ready, rstd_ready)

        @block.vector
        def _(dve):
            LINKS = 6 + 2 * 3 + STATS_LINKS
            dve.wait_ge(a_ready, 1)
            nc.vector.tensor_scalar(flat(a_neg[:, :, :]), flat(a_neg[:, :, :]), LEAST, -1.0, ALU.max,
                                    ALU.mult).then_inc(a_ready, 1)
            dve.wait_ge(w_in[0], 16)
            nc.vector.tensor_tensor(gated_bias[:, :], cols[:, :, 1], cols[:, :, 2], ALU.mult).then_inc(bias_ready, 1)

            def mean_square(n):
                dve.wait_ge(sq_done, n)
                nc.vector.tensor_scalar(ms[:, :], squares[:, :], 1.0 / D, EPS, ALU.mult, ALU.add).then_inc(ms_ready, 1)

            def scale_rows(n):
                dve.wait_ge(r_ready, n)
                for j in range(CT):
                    last = nc.vector.tensor_scalar(normal[:, j, :], sh.xn[:, j, :], rr[:, j:j + 1], None, ALU.mult)
                last.then_inc(normed, 1)

            mean_square(1)
            scale_rows(1)
            with dve.Fori(0, CHUNKS) as c:
                chain = Chain(dve, own, c * LINKS, LINKS)
                link = chain.link
                dve.wait_ge(mask_ready, c + 1)
                nc.vector.tensor_tensor(flat(xg[:, :, :]), flat(mask[:, :, :]), flat(sh.xT[:, :, :]), ALU.mult).then_inc(xg_ready, 1)
                dve.wait_ge(turned, 4 * c + 4)
                nc.vector.tensor_copy(flat(hsT[:, :, :]), flat(spare[:, :, :])).then_inc(hsT_ready, 1)

                def split_1(bc):
                    dve.wait_ge(proj_done, 3 * c + 2 + bc)
                    link(nc.vector.tensor_copy(part[:, bc, 0, :], rows[:, bc, :]))
                    link(nc.vector.tensor_tensor(rest[:, bc, :], rows[:, bc, :], part[:, bc, 0, :], ALU.subtract))

                def split_2(bc):
                    link(nc.vector.tensor_copy(part[:, bc, 1, :], rest[:, bc, :]))
                    nc.vector.tensor_tensor(part[:, bc, 2, :], rest[:, bc, :], part[:, bc, 1, :],
                                            ALU.subtract).then_inc(split_ready, 1)

                split_1(0)
                split_2(0)
                dve.wait_ge(dt_done, c + 1)
                for m in range(KC):
                    chain.mark(nc.vector.tensor_scalar(z[:, m, :], rows[:, 2 + m, :], cols[:, m, 3:4], None, ALU.add))
                chain.wait()
                nc.vector.scalar_tensor_tensor(out=flat(e[:, :, :]), in0=flat(z[:, :, :]), scalar=-1.0,
                                               in1=flat(z[:, :, :]), op0=ALU.mult, op1=ALU.min).then_inc(dt_neg, 1)
                split_1(1)
                dve.wait_ge(dt_exp, c + 1)
                nc.vector.tensor_scalar(flat(w1[:, :, :]), flat(e[:, :, :]), 1.0, None, ALU.add).then_inc(dt_ln, 1)
                dve.wait_ge(dt_ln, 3 * c + 1)
                link(nc.vector.scalar_tensor_tensor(out=flat(e[:, :, :]), in0=flat(w1[:, :, :]), scalar=-1.0,
                                                    in1=flat(e[:, :, :]), op0=ALU.add, op1=ALU.subtract))
                split_2(1)
                dve.wait_ge(dt_ln, 3 * c + 3)
                link(nc.vector.tensor_tensor(flat(e[:, :, :]), flat(e[:, :, :]), flat(mask[:, :, :]), ALU.mult))
                link(nc.vector.tensor_tensor(flat(low[:, :, :]), flat(low[:, :, :]), flat(e[:, :, :]), ALU.subtract))
                link(nc.vector.scalar_tensor_tensor(out=flat(dt[:, :, :]), in0=flat(z[:, :, :]), scalar=0.0,
                                                    in1=flat(low[:, :, :]), op0=ALU.max, op1=ALU.add))
                nc.vector.tensor_tensor(flat(u[:, :, :]), flat(dt[:, :, :]), flat(xg[:, :, :]), ALU.mult).then_inc(u_ready, 1)
                dve.wait_ge(u_ready, c + 1)
                nc.vector.memset(flat(dt[:, :, :]).rearrange("p (a t) -> p a t", t=S)[:, :, 0:1], FAR).then_inc(dt_ready, 1)

                def product(m_, j, free=False):
                    if not free:
                        dve.wait_ge(state_ready, c * NS + m_ - SLOTS + 1)
                    dve.wait_ge(rows_done, c * NS + m_ + 1)
                    nc.vector.tensor_tensor(dbu[:, j, :, :], u[:, :, :],
                                            rows[:, j % 2, :].rearrange("p (a t) -> p a t", a=1).broadcast_to([P, KC, N]),
                                            ALU.mult).then_inc(dbu_ready, 1)

                def scan(m_, j):
                    n, i = c * NS + m_, j % 2
                    dve.wait_ge(decay_ready, n + 1)
                    dve.wait_ge(hc_ready, n + 1)
                    dve.wait_ge(dbu_ready, n + 1)
                    nc.vector.tensor_tensor_scan(flat(state[:, i, :, :]), flat(decay[:, i, :, :]), flat(dbu[:, j, :, :]),
                                                 0.0, ALU.mult, ALU.add).then_inc(state_ready, 1)

                product(0, 0, free=True)
                for j in range(SLOTS):
                    product(j + 1, (j + 1) % SLOTS, free=j + 1 < SLOTS)
                    scan(j, j)
                with dve.Fori(1, NS // SLOTS - 1) as k:
                    for j in range(SLOTS):
                        product(SLOTS * k + j + 1, (j + 1) % SLOTS)
                        scan(SLOTS * k + j, j)
                for j in range(SLOTS):
                    if j < SLOTS - 1:
                        product(NS - SLOTS + j + 1, j + 1)
                    scan(NS - SLOTS + j, j)
                dve_normalise(nc, sh, c + 1, xn_ready)
                mean_square(c + 2)
                dve.wait_ge(added, (c + 1) * NS + 2)
                for m in range(KC):
                    last = nc.vector.scalar_tensor_tensor(out=yT[:, m, :], in0=hsT[:, m, :], scalar=cols[:, m, 4:5],
                                                          in1=y[:, m, :], op0=ALU.mult, op1=ALU.add)
                last.then_inc(y_ready, 1)
                scale_rows(c + 2)
                dve.wait_ge(proj_out, c + 1)
                dve_add_residual(nc, sh, dve, c, out, out_used, kept)
                dve_stats(nc, sh, dve, c, sh.fresh, chain, var_ready, rstd_ready, kept)
                chain.done()
            dve_first_normalised(nc, sh, dve, xn_ready, kept, CHUNKS)


def alibi_columns(heads):
    slopes = np.array([2.0 ** (-8.0 * (h + 1) / heads) for h in range(heads)], np.float32)
    key = np.concatenate([np.arange(P), np.arange(S)])
    query = np.arange(P)[:, None] + np.concatenate([np.zeros(P), np.full(S, P)])[None, :]
    bias = slopes[None, :, None] * key.astype(np.float32)[None, None, :]
    return np.where((key[None, :] > query)[:, None, :], np.float32(-1e30), bias).astype(np.float32)


def head_rows(w, heads):
    return w.reshape(heads, P, KC, P).transpose(0, 3, 2, 1).reshape(heads, P, KC * P)


def head_out(w, heads):
    return w.reshape(D, heads, P).transpose(1, 2, 0)


def pack_rest(i):
    out = {}
    a = {k[10:]: v for k, v in i.items() if k.startswith("L0_attn_a_W")}
    out["a0_w"] = np.concatenate([head_rows(a["Wq"], 16), head_rows(a["Wk"], 16), head_rows(a["Wv"], 16),
                                  head_out(a["Wo"], 16)], 2)
    out["a0_bias"] = alibi_columns(16)
    g = {k[10:]: v for k, v in i.items() if k.startswith("L1_attn_a_")}
    slot = np.zeros((16, P, 64), np.float32)
    slot[:, 0:16] = g["Ws2"].reshape(16, 64, 16).transpose(0, 2, 1)
    slot[:, 16] = g["bs2"].reshape(16, 64)
    out["a1_w"] = np.concatenate([head_rows(g["Wq"], 16), head_rows(g["Wk"], 16), head_rows(g["Wv"], 16),
                                  head_rows(g["Wg"], 16), slot, head_out(g["Wo"], 16)], 2)
    out["a1_ws1"] = rows_in(g["Ws1"].T)
    out["a1_rope"] = rope_table(P)
    out["a1_masks"] = np.stack([causal_columns() * np.float32(P ** -0.5), causal_columns()], 1)
    r = {k[10:]: v for k, v in i.items() if k.startswith("L0_attn_b_")}
    out["rt_wqkvg"] = np.stack([rows_in(r[k]) for k in ("Wq", "Wk", "Wv", "Wg")], 1)
    out["rt_wo"] = rows_in(r["Wo"])
    halves = [np.pad(w, ((0, 0), (0, 32))) for w in (r["W_gate"][:, :352], r["W_gate"][:, 352:])]
    out["rt_w_gate"] = np.stack([rows_in(w) for w in halves], 1)
    out["rt_w_down"] = np.pad(r["W_down"], ((0, 32), (0, 0))).reshape(3, P, D).transpose(1, 0, 2)
    columns = np.concatenate([r["conv_wq"], r["conv_wk"], r["conv_wv"], r["attn_norm_w"][:, None],
                              r["mlp_norm_w"][:, None]], 1)
    out["rt_cols"] = rows_in(columns)
    out["rt_gnw"] = np.tile(r["gnorm_w"], (P, 8))
    out["rt_swap"] = np.kron(np.eye(4), np.roll(np.eye(32), 16, 1)).astype(np.float32)
    out["rt_rope"] = rope_table(32)
    out["rt_decay"] = decay_columns(8, 32)
    m = {k[10:]: v for k, v in i.items() if k.startswith("L1_attn_b_")}
    out["ss_cols"] = rows_in(np.stack([m["norm_w"], m["select_proj_b"], m["select_gate"], m["dt_proj_b"], m["D_param"]], 1))
    out["ss_a_log"] = rows_in(m["A_log"])
    out["ss_w_sel"] = rows_in(m["select_proj_w"].T)
    out["ss_w_xp"] = rows_in(m["x_proj_w"].T)
    out["ss_w_dt"] = m["dt_proj_w"].T
    out["ss_w_out"] = rows_in(m["out_proj_w"].T)
    hot = np.tile(np.eye(32, dtype=np.float32), (3, 1))
    out["ss_onehot"] = np.broadcast_to(hot[:, :, None], (96, 32, P)).astype(mybir.dt.np(BF16))
    out["a1_gn"] = g["g_norm_weight"].reshape(P, 1)
    return out


def rope_table(width):
    half = width // 2
    freq = 1.0 / 10000.0 ** (np.arange(0, width, 2) / width)
    angle = (np.arange(S)[None, :].astype(np.float32) * freq.astype(np.float32)[:, None]).astype(np.float64)
    cos, sin = np.cos(angle), np.sin(angle)
    one = np.stack([np.concatenate([cos, cos]), np.concatenate([-sin, sin])], 1)
    return np.tile(one, (P // width, 1, 1)).astype(np.float32)


def causal_columns():
    key, query = np.arange(P)[:, None], np.arange(P)[None, :]
    tri = (query >= key).astype(np.float32)
    return np.concatenate([tri, np.ones((P, P), np.float32), tri], 1)


def decay_columns(heads, width):
    gamma = 1.0 - 2.0 ** (-5.0 - np.arange(heads))
    ahead = np.arange(S)[None, :] - np.arange(P)[:, None]
    table = gamma[None, :, None] ** np.maximum(ahead, 0)[:, None, :] * width ** -0.5
    return np.where((ahead >= 0)[:, None, :], table, 0).astype(np.float32)


def pack_ffn(gates, ups, downs):
    def cat(parts, axis):
        a = np.concatenate(parts, axis)
        short = -a.shape[axis] % P
        return np.pad(a, [(0, short if ax == axis else 0) for ax in range(2)])
    g, u, d = cat(gates, 1), cat(ups, 1), cat(downs, 0)
    lay = lambda w: w.reshape(KC, P, -1, P).transpose(2, 1, 0, 3).reshape(-1, P, KC * P)
    return np.concatenate([lay(g), lay(u), d.reshape(-1, P, D)], 2)


def rows_in(w):
    return w.reshape(KC, P, -1).transpose(1, 0, 2)


def one_hot_parts(experts, width, shared):
    owner = np.concatenate([np.repeat(np.arange(experts), width), np.full(shared, experts)])
    hot = np.zeros((P, -(-owner.size // P) * P), np.float32)
    for part in range(3):
        hot[part * (experts + 1) + owner, np.arange(owner.size)] = 1
    return hot.astype(mybir.dt.np(BF16))


def pack(i):
    i = {k: np.asarray(v) for k, v in i.items()}
    f0 = {k[7:]: v for k, v in i.items() if k.startswith("L0_ffn_")}
    f1 = {k[7:]: v for k, v in i.items() if k.startswith("L1_ffn_")}
    out = {"x": i["L0_attn_a_resid_pre"]}
    out["f0_w"] = pack_ffn([*f0["w_gate"], f0["sh_gate"]], [*f0["w_up"], f0["sh_up"]],
                           [*f0["w_down"], f0["sh_down"]])
    out["f0_router"] = rows_in(np.concatenate([f0["router_w"].T, f0["sh_gate_w"]], 1))
    out["f0_hot"] = one_hot_parts(16, 176, 704)
    t = lambda ws: [w.T for w in ws]
    out["f1_w"] = pack_ffn(t([*f1["w1"], f1["sw1"]]), t([*f1["w3"], f1["sw3"]]), t([*f1["w2"], f1["sw2"]]))
    out["f1_router"] = rows_in(np.concatenate([f1["gate_w"].T, np.zeros((D, 1), np.float32)], 1))
    out["f1_hot"] = one_hot_parts(8, 176, 352)
    out.update(pack_rest(i))
    return {k: np.ascontiguousarray(v) for k, v in out.items()}


def program(nc, d, blocks):
    with ExitStack() as ctx:
        sh = Shared(nc, ctx, d)
        load_block(nc, sh)
        sh.end_block()
        for n in blocks:
            if n == 0:
                l0_attention_block(nc, sh)
            if n in (1, 3):
                ffn_block(nc, sh, f"f0{n}", d["f0_w"], d["f0_router"], d["f0_hot"], 16, 4, 28, True)
            if n == 2:
                retention_block(nc, sh)
            if n == 4:
                l1_attention_block(nc, sh)
            if n in (5, 7):
                ffn_block(nc, sh, f"f1{n}", d["f1_w"], d["f1_router"], d["f1_hot"], 8, 2, 14, False)
            if n == 6:
                ssm_block(nc, sh)
            sh.end_block()
        store_block(nc, sh)


def kernel(**inputs):
    import concourse.bacc as bacc
    from concourse.bass_utils import run_bass_kernel_spmd

    arrays = pack(inputs)
    nc = bacc.Bacc("TRN2", target_bir_lowering=False, num_devices=1)
    d = {k: nc.dram_tensor(f"in_{k}", a.shape, mybir.dt.from_np(a.dtype), kind="ExternalInput").ap() for k, a in arrays.items()}
    d["out"] = nc.dram_tensor("out", (B, S, D), F32, kind="ExternalOutput").ap()
    program(nc, d, range(8))
    r = run_bass_kernel_spmd(nc, [{f"in_{k}": a for k, a in arrays.items()}], core_ids=[0])
    return r.results[0]["out"]
```
